# Optimizing a Trainium2 kernel written in Bass

```python
import numpy as np
import jax
import jax.numpy as jnp

def _softmax(x, axis=-1):
    return jax.nn.softmax(x, axis=axis)

def _gelu(x):
    return jax.nn.gelu(x, approximate=True)

def _silu(x):
    return jax.nn.silu(x)

def _sigmoid(x):
    return jax.nn.sigmoid(x)

def _layernorm(x, axis=-1, eps=1e-05):
    m = jnp.mean(x, axis=axis, keepdims=True)
    v = jnp.var(x, axis=axis, keepdims=True)
    return (x - m) / jnp.sqrt(v + eps)

def _scatter_add(tgt, idx, src, axis=0):
    return tgt.at[idx].add(src)

def _segment_sum(src, seg, n):
    return jax.ops.segment_sum(src, seg, n)
kernel_name = 'mk_seq_postln_d1_jaxref_r4_60163b'

def setup_inputs(seed: int=0):
    np.random.seed(seed)
    _w = jnp.asarray

    def _L0_attn_setup():
        import jax, jax.numpy as jnp
        import numpy as np
        import math
        D_MODEL = 256
        D_STATE = 128
        D_CONV = 4
        EXPAND = 2
        HEADDIM = 64
        NGROUPS = 1
        N_SCALES = 3
        D_INNER = D_MODEL * EXPAND
        D_SSM = D_INNER
        NHEADS = D_SSM // HEADDIM
        CONV_DIM = D_SSM + 2 * NGROUPS * D_STATE
        D_IN_PROJ = 2 * D_INNER + 2 * NGROUPS * D_STATE + NHEADS
        BATCH = 4
        SEQLEN = 512
        EPS = 1e-05
        key = jax.random.key(seed)
        ks = jax.random.split(key, 8)
        u = jax.random.normal(ks[0], (BATCH, SEQLEN, D_MODEL), dtype=jnp.float32)
        in_proj_w = jax.random.normal(ks[1], (D_IN_PROJ, D_MODEL), dtype=jnp.float32) * 0.02
        conv_w = jax.random.normal(ks[2], (CONV_DIM, 1, D_CONV), dtype=jnp.float32) * 0.3
        conv_b = jnp.zeros((CONV_DIM,), dtype=jnp.float32)
        dt_min, dt_max, dt_init_floor = (0.001, 0.1, 0.0001)
        r = jax.random.uniform(ks[3], (NHEADS,), dtype=jnp.float32)
        dt = jnp.exp(r * (math.log(dt_max) - math.log(dt_min)) + math.log(dt_min))
        dt = jnp.clip(dt, dt_init_floor)
        dt_bias = dt + jnp.log(-jnp.expm1(-dt))
        scales = jnp.arange(1, N_SCALES + 1, dtype=jnp.float32)[:, None]
        A = jax.random.uniform(ks[4], (N_SCALES, NHEADS), dtype=jnp.float32, minval=1.0, maxval=16.0) * scales
        A_log = jnp.log(A)
        D = jnp.ones((NHEADS,), dtype=jnp.float32)
        norm_w = jnp.ones((D_SSM,), dtype=jnp.float32)
        out_proj_w = jax.random.normal(ks[5], (D_MODEL, D_INNER), dtype=jnp.float32) * 0.02
        return {'u': u, 'in_proj_w': in_proj_w, 'conv_w': conv_w, 'conv_b': conv_b, 'dt_bias': dt_bias, 'A_log': A_log, 'D': D, 'norm_w': norm_w, 'out_proj_w': out_proj_w}
    _L0_attn_in = _L0_attn_setup()

    def _L0_ffn_setup():
        import jax, jax.numpy as jnp
        import numpy as np
        from jax import lax
        D = 256
        H = 352
        E = 8
        K = 2
        ROUTER_SCALE = 1.0

        def _expert(x, w1, b1, w3, b3, w2, b2):
            h = jax.nn.silu((x @ w1 + b1) * (x @ w3 + b3))
            return h @ w2 + b2
        key = jax.random.key(seed)
        ks = jax.random.split(key, 16)
        s = 0.02
        inp = {'x': jax.random.normal(ks[0], (2, 512, D), dtype=jnp.float32), 'gate_w': jax.random.normal(ks[1], (E, D), dtype=jnp.float32) * s, 'gate_b': jax.random.normal(ks[2], (E,), dtype=jnp.float32) * s, 'w1': jax.random.normal(ks[3], (E, D, H), dtype=jnp.float32) * s, 'b1': jax.random.normal(ks[4], (E, H), dtype=jnp.float32) * s, 'w3': jax.random.normal(ks[5], (E, D, H), dtype=jnp.float32) * s, 'b3': jax.random.normal(ks[6], (E, H), dtype=jnp.float32) * s, 'w2': jax.random.normal(ks[7], (E, H, D), dtype=jnp.float32) * s, 'b2': jax.random.normal(ks[8], (E, D), dtype=jnp.float32) * s, 'sw1': jax.random.normal(ks[9], (D, H), dtype=jnp.float32) * s, 'sb1': jax.random.normal(ks[10], (H,), dtype=jnp.float32) * s, 'sw3': jax.random.normal(ks[11], (D, H), dtype=jnp.float32) * s, 'sb3': jax.random.normal(ks[12], (H,), dtype=jnp.float32) * s, 'sw2': jax.random.normal(ks[13], (H, D), dtype=jnp.float32) * s, 'sb2': jax.random.normal(ks[14], (D,), dtype=jnp.float32) * s}
        return inp
    _L0_ffn_in = _L0_ffn_setup()
    _d = {'L0_attn_u': _L0_attn_in['u'], 'L0_attn_in_proj_w': _L0_attn_in['in_proj_w'], 'L0_attn_conv_w': _L0_attn_in['conv_w'], 'L0_attn_conv_b': _L0_attn_in['conv_b'], 'L0_attn_dt_bias': _L0_attn_in['dt_bias'], 'L0_attn_A_log': _L0_attn_in['A_log'], 'L0_attn_D': _L0_attn_in['D'], 'L0_attn_norm_w': _L0_attn_in['norm_w'], 'L0_attn_out_proj_w': _L0_attn_in['out_proj_w'], 'L0_ffn_gate_w': _L0_ffn_in['gate_w'], 'L0_ffn_gate_b': _L0_ffn_in['gate_b'], 'L0_ffn_w1': _L0_ffn_in['w1'], 'L0_ffn_b1': _L0_ffn_in['b1'], 'L0_ffn_w3': _L0_ffn_in['w3'], 'L0_ffn_b3': _L0_ffn_in['b3'], 'L0_ffn_w2': _L0_ffn_in['w2'], 'L0_ffn_b2': _L0_ffn_in['b2'], 'L0_ffn_sw1': _L0_ffn_in['sw1'], 'L0_ffn_sb1': _L0_ffn_in['sb1'], 'L0_ffn_sw3': _L0_ffn_in['sw3'], 'L0_ffn_sb3': _L0_ffn_in['sb3'], 'L0_ffn_sw2': _L0_ffn_in['sw2'], 'L0_ffn_sb2': _L0_ffn_in['sb2']}
    _x0 = _d['L0_attn_u']
    _d['L0_attn_u'] = jax.random.normal(jax.random.fold_in(jax.random.key(seed), 1), (4, 1024, 256), dtype=_x0.dtype)
    del _x0
    return _d

def reference(L0_attn_u, L0_attn_in_proj_w, L0_attn_conv_w, L0_attn_conv_b, L0_attn_dt_bias, L0_attn_A_log, L0_attn_D, L0_attn_norm_w, L0_attn_out_proj_w, L0_ffn_gate_w, L0_ffn_gate_b, L0_ffn_w1, L0_ffn_b1, L0_ffn_w3, L0_ffn_b3, L0_ffn_w2, L0_ffn_b2, L0_ffn_sw1, L0_ffn_sb1, L0_ffn_sw3, L0_ffn_sb3, L0_ffn_sw2, L0_ffn_sb2):

    def _L0_attn_ref(u, in_proj_w, conv_w, conv_b, dt_bias, A_log, D, norm_w, out_proj_w):
        import jax, jax.numpy as jnp
        import numpy as np
        import math
        D_MODEL = 256
        D_STATE = 128
        D_CONV = 4
        EXPAND = 2
        HEADDIM = 64
        NGROUPS = 1
        N_SCALES = 3
        D_INNER = D_MODEL * EXPAND
        D_SSM = D_INNER
        NHEADS = D_SSM // HEADDIM
        CONV_DIM = D_SSM + 2 * NGROUPS * D_STATE
        D_IN_PROJ = 2 * D_INNER + 2 * NGROUPS * D_STATE + NHEADS
        BATCH = 4
        SEQLEN = 512
        EPS = 1e-05
        b, l, _ = u.shape
        zxbcdt = u @ in_proj_w.T
        A = -jnp.exp(A_log.astype(jnp.float32)).mean(axis=0)
        z, xBC, dt = jnp.split(zxbcdt, [D_INNER, D_INNER + CONV_DIM], axis=-1)
        conv = jax.lax.conv_general_dilated(xBC.transpose(0, 2, 1), conv_w, window_strides=(1,), padding=[(D_CONV - 1, 0)], feature_group_count=CONV_DIM, dimension_numbers=('NCH', 'OIH', 'NCH'))
        xBC = jax.nn.silu((conv + conv_b[None, :, None]).transpose(0, 2, 1))
        x, Bm, Cm = jnp.split(xBC, [D_SSM, D_SSM + NGROUPS * D_STATE], axis=-1)
        x = x.reshape(b, l, NHEADS, HEADDIM)
        Bm = Bm.reshape(b, l, NGROUPS, D_STATE)[:, :, 0]
        Cm = Cm.reshape(b, l, NGROUPS, D_STATE)[:, :, 0]
        dt = jax.nn.softplus(dt + dt_bias)
        dA = jnp.exp(dt * A)
        dB = dt[..., None] * Bm[:, :, None, :]

        def step(h, inp):
            dA_t, x_t, dB_t, C_t = inp
            h = h * dA_t[:, :, None, None] + x_t[..., None] * dB_t[:, :, None, :]
            y_t = jnp.einsum('bhpn,bn->bhp', h, C_t)
            return (h, y_t)
        h0 = jnp.zeros((b, NHEADS, HEADDIM, D_STATE), dtype=x.dtype)
        xs = (dA.transpose(1, 0, 2), x.transpose(1, 0, 2, 3), dB.transpose(1, 0, 2, 3), Cm.transpose(1, 0, 2))
        _, ys = jax.lax.scan(step, h0, xs)
        y = ys.transpose(1, 0, 2, 3)
        y = y + D[None, None, :, None] * x
        y = y.reshape(b, l, D_SSM)
        y = norm_w * y * jax.lax.rsqrt(jnp.mean(y * y, axis=-1, keepdims=True) + EPS)
        y = y * jax.nn.silu(z)
        return y @ out_proj_w.T

    def _L0_ffn_ref(x, gate_w, gate_b, w1, b1, w3, b3, w2, b2, sw1, sb1, sw3, sb3, sw2, sb2):
        import jax, jax.numpy as jnp
        import numpy as np
        from jax import lax
        D = 256
        H = 352
        E = 8
        K = 2
        ROUTER_SCALE = 1.0

        def _expert(x, w1, b1, w3, b3, w2, b2):
            h = jax.nn.silu((x @ w1 + b1) * (x @ w3 + b3))
            return h @ w2 + b2
        shape = x.shape
        xf = x.reshape(-1, D)
        T = xf.shape[0]
        scores = jax.nn.softmax(xf @ gate_w.T, axis=-1)
        biased = scores + gate_b
        _, idx = lax.top_k(biased, K)
        w = jnp.take_along_axis(scores, idx, axis=-1) * ROUTER_SCALE
        rw = jnp.zeros((T, E), dtype=xf.dtype).at[jnp.arange(T)[:, None], idx].add(w)
        h = jax.nn.silu((jnp.einsum('td,edh->teh', xf, w1) + b1) * (jnp.einsum('td,edh->teh', xf, w3) + b3))
        oe = jnp.einsum('teh,ehd->ted', h, w2) + b2
        y = jnp.einsum('te,ted->td', rw, oe)
        z = _expert(xf, sw1, sb1, sw3, sb3, sw2, sb2)
        return (y + z).reshape(shape)
    x = L0_attn_u
    x = _layernorm(x + _L0_attn_ref(x, L0_attn_in_proj_w, L0_attn_conv_w, L0_attn_conv_b, L0_attn_dt_bias, L0_attn_A_log, L0_attn_D, L0_attn_norm_w, L0_attn_out_proj_w), axis=-1)
    x = _layernorm(x + _L0_ffn_ref(x, L0_ffn_gate_w, L0_ffn_gate_b, L0_ffn_w1, L0_ffn_b1, L0_ffn_w3, L0_ffn_b3, L0_ffn_w2, L0_ffn_b2, L0_ffn_sw1, L0_ffn_sb1, L0_ffn_sw3, L0_ffn_sb3, L0_ffn_sw2, L0_ffn_sb2), axis=-1)
    return x

_drawn_inputs = setup_inputs


def setup_inputs(seed=0):
    import zlib

    import numpy as np

    out = dict(_drawn_inputs(seed))
    spreads = {'L0_attn_conv_b': (0.0, 0.1), 'L0_attn_D': (1.0, 0.6), 'L0_attn_norm_w': (1.0, 0.6)}
    factors = {'L0_attn_dt_bias': 8.0,
     'L0_attn_A_log': 8.0,
     'L0_ffn_gate_w': 8.0,
     'L0_ffn_gate_b': 8.0,
     'L0_ffn_w1': 8.0,
     'L0_ffn_b1': 8.0,
     'L0_ffn_w3': 8.0,
     'L0_ffn_b3': 8.0,
     'L0_ffn_w2': 8.0,
     'L0_ffn_b2': 8.0,
     'L0_ffn_sw1': 2.919,
     'L0_ffn_sb1': 8.0,
     'L0_ffn_sw3': 2.9,
     'L0_ffn_sb3': 8.0,
     'L0_ffn_sw2': 2.906,
     'L0_ffn_sb2': 2.921}
    for name, (base, spread) in spreads.items():
        noise = np.random.default_rng([zlib.crc32(name.encode()), seed]).standard_normal(out[name].shape)
        drawn = base * np.exp(spread * noise) if base else spread * noise
        out[name] = jnp.asarray(drawn.astype(out[name].dtype))
    for name, factor in factors.items():
        out[name] = (out[name] * factor).astype(out[name].dtype)
    return out
```

```python
from contextlib import ExitStack

import concourse.bass as bass
from concourse import mybir

F32 = mybir.dt.float32
F32R = mybir.dt.float32r
ALU = mybir.AluOpType
ACT = mybir.ActivationFunctionType
AX = mybir.AxisListType

P = 128
EPS = 1e-5
LOG_ZERO = -104.0

HEAD = 3

FULL, REST = 256, 96


def hidden_tiles():
    tiles = [[(0, P, 8, 0)], [(0, P, 8, P)], [(0, REST, 8, FULL)]]
    for e in (0, 4):
        for i in range(4):
            tiles += [[(0, P, e + i, 0)], [(0, P, e + i, P)]]
            if i < 3:
                tiles.append([(0, REST, e + i, FULL), (REST, P - REST, e + 3, FULL + 32 * i)])
    return tiles


def mixer(nc, uT, u, w_in, conv_w, conv_b, rows, norm_w, w_out, x1_dram):
    D, TOK = uT.shape
    KT = D // P
    T = 512
    CH = T // P
    SEQ = 1024
    NBLK = TOK // T
    NSEQ = TOK // SEQ
    H, HD = 8, 64
    DI = H * HD
    CT = (DI + 2 * P) // P
    TB, TC = DI // P, DI // P + 1
    OT = DI // P
    COLS = w_in.shape[1]
    DTC = COLS - H
    TAPS = 4
    assert SEQ == 2 * T and CH * H == 32

    with ExitStack() as ctx:
        def sb(name, shape, dt=F32):
            return ctx.enter_context(nc.sbuf_tensor(name, shape, dt))

        def bank(name, cols=512):
            return ctx.enter_context(nc.psum_tensor(name, [P, cols], F32))

        def sem(name):
            return ctx.enter_context(nc.semaphore(name))

        win = sb("win", [P, KT, COLS])
        win_hi = sb("win_hi", [P, KT, DTC], F32R)
        win_lo = sb("win_lo", [P, KT, DTC], F32R)
        wo = sb("wo", [P, OT, D])
        wo_hi = sb("wo_hi", [P, OT, D], F32R)
        wo_lo = sb("wo_lo", [P, OT, D], F32R)
        cw = sb("cw", [P, CT, TAPS])
        cb = sb("cb", [P, CT])
        nw = sb("nw", [P, OT])
        rowb = sb("rowb", [P, 48])
        expA = sb("expA", [P, 3, H])
        sumA = sb("sumA", [P, H])
        negA = sb("negA", [P, H])
        upto = sb("upto", [P, P])
        after = sb("after", [P, P])
        ones = sb("ones", [P, P])
        ident = sb("ident", [P, P])
        c_eps = sb("c_eps", [P, CH])
        c_inv = sb("c_inv", [P, CH])
        c_mhalf = sb("c_mhalf", [P, CH])
        ut = [sb(f"ut{i}", [P, KT, T]) for i in range(2)]
        u_hi = [sb(f"u_hi{i}", [P, KT, T], F32R) for i in range(2)]
        u_lo = [sb(f"u_lo{i}", [P, KT, T], F32R) for i in range(2)]
        pre = [sb(f"pre{i}", [P, CT, TAPS - 1 + T]) for i in range(2)]
        xbc = [sb(f"xbc{i}", [P, CT, T]) for i in range(2)]
        zs = [sb(f"zs{i}", [P, CH, DI]) for i in range(2)]
        dt = [sb(f"dt{i}", [P, CH * H]) for i in range(2)]
        la = [sb(f"la{i}", [P, CH * H]) for i in range(2)]
        dec = [sb(f"dec{i}", [P, 3, CH * H]) for i in range(2)]
        dtw = [sb(f"dtw{i}", [P, CH * H]) for i in range(2)]
        ur = [sb(f"ur{i}", [P, CH, D]) for i in range(2)]
        x1 = [sb(f"x1_{i}", [P, CH, D]) for i in range(2)]
        ss = [sb(f"ss{i}", [P, CH]) for i in range(2)]
        v_raw, v_dt, v_neg, v_e, v_w, v_d, v_m, v_l, v_q, v_p = (
            sb(n, [P, CH * H]) for n in ("v_raw", "v_dt", "v_neg", "v_e", "v_w", "v_d", "v_m", "v_l", "v_q", "v_p"))
        steps = sb("steps", [P, H, P])
        mt = sb("mt", [P, H, P])
        cbm = sb("cbm", [P, P])
        b_tok = sb("b_tok", [P, P])
        xs = sb("xs", [P, DI])
        xdt = sb("xdt", [P, DI])
        xw = sb("xw", [P, DI])
        xd = sb("xd", [P, DI])
        yb = sb("yb", [P, DI])
        gb = sb("gb", [P, DI])
        sq = sb("sq", [P, DI])
        g_hi = sb("g_hi", [P, OT, P], F32R)
        g_lo = sb("g_lo", [P, OT, P], F32R)
        state = sb("state", [P, DI])
        rms = sb("rms", [P, CH])
        stat = sb("stat", [P, CH, 6])
        mv = sb("mv", [P, CH, 2])
        rs = sb("rs", [P, CH])
        tiny = sb("tiny", [P, 1])

        ip_bank = [bank("ip_bank0"), bank("ip_bank1")]
        seg_bank = bank("seg_bank", 1024)
        out_bank = seg_bank[:, 0:D]
        cb_bank = bank("cb_bank")
        xt_bank = bank("xt_bank")
        yd_bank = bank("yd_bank")
        yo_bank = bank("yo_bank")

        s_w = sem("s_w")
        ut_in = [sem(f"ut_in{i}") for i in range(2)]
        ur_in = [sem(f"ur_in{i}") for i in range(2)]
        x1_out = sem("x1_out")
        s_const = sem("s_const")
        s_setup_a = sem("s_setup_a")
        s_setup_v = sem("s_setup_v")
        s_ready = sem("s_ready")
        ip_ps = sem("ip_ps")
        ip_ev = sem("ip_ev")
        uhi_done = sem("uhi_done")
        ulo_done = sem("ulo_done")
        taps_done = sem("taps_done")
        halo_done = sem("halo_done")
        silu_done = sem("silu_done")
        sp_chain = sem("sp_chain")
        sp_exp = sem("sp_exp")
        sp_ln = sem("sp_ln")
        dec_ready = sem("dec_ready")
        dtw_ready = sem("dtw_ready")
        cb_ps = sem("cb_ps")
        xt_ps = sem("xt_ps")
        seg_ps = sem("seg_ps")
        yo_ps = sem("yo_ps")
        ds_ps = sem("ds_ps")
        yd_ps = sem("yd_ps")
        gt_ps = sem("gt_ps")
        out_ps = sem("out_ps")
        steps_ready = sem("steps_ready")
        xs_ready = sem("xs_ready")
        xw_ready = sem("xw_ready")
        xd_ready = sem("xd_ready")
        cbm_ready = sem("cbm_ready")
        exp_done = sem("exp_done")
        mt_ready = sem("mt_ready")
        y1_done = sem("y1_done")
        t2_done = sem("t2_done")
        st_scaled = sem("st_scaled")
        st_ready = sem("st_ready")
        y_ready = sem("y_ready")
        g_ready = sem("g_ready")
        ss_ready = sem("ss_ready")
        ghi_done = sem("ghi_done")
        glo_done = sem("glo_done")
        out_ev = sem("out_ev")
        rms_chain = sem("rms_chain")
        rms_ready = sem("rms_ready")
        res_done = sem("res_done")
        stat_done = sem("stat_done")
        mv_ready = sem("mv_ready")
        rs_chain = sem("rs_chain")
        rs_ready = sem("rs_ready")
        x1_ready = sem("x1_ready")

        uT_v = uT.rearrange("(k p) (b t) -> b p k t", p=P, t=T)
        u_v = u.rearrange("(b c p) d -> b p c d", p=P, c=CH)
        x1_v = x1_dram.rearrange("b (c p) d -> b p c d", p=P)
        NW = 6

        ITEMS = [[["dt", 0], [1, 2]], [[3], [4]], [[5], ["cs"]], [["z0", "z1"], ["z2", "z3"]]]
        ORDER = [x for slot in ITEMS for half in slot for x in half]
        NI = len(ORDER)

        def after_chunk(j):
            return j + HEAD

        def after_block(n):
            return n + HEAD

        SP_OPS = 14

        def softplus(m, i=SP_OPS):
            return m * SP_OPS + i + 1

        def taps(m, tile, i=TAPS - 1):
            return (m * CT + tile) * (TAPS - 1) + i

        block = ctx.enter_context(nc.Block())

        @block.sync
        def _(sp):
            for dst, src in ((win, w_in.rearrange("(k p) c -> p k c", p=P)), (wo, w_out.rearrange("(k p) c -> p k c", p=P)),
                             (cw, conv_w), (nw, norm_w), (cb, conv_b)):
                sp.dma_start(dst[:], src).then_inc(s_w, 16)
            sp.dma_start(rowb[:], rows.partition_broadcast(P)).then_inc(s_w, 16)
            sp.dma_start(ut[0][:], uT_v[0]).then_inc(ut_in[0], 16)
            sp.dma_start(ut[1][:], uT_v[1]).then_inc(ut_in[1], 16)

            def step(s, par, last):
                n = s * 2 + par
                sp.wait_ge(x1_ready, after_block(n - 2))
                sp.dma_start(ur[par][:], u_v[n]).then_inc(ur_in[par], 16)
                if not last:
                    sp.wait_ge(ip_ps, (n + 1) * NI)
                    sp.dma_start(ut[par][:], uT_v[n + 2]).then_inc(ut_in[par], 16)
                sp.wait_ge(x1_ready, after_block(n - 1))
                sp.dma_start(x1_v[n], x1[1 - par][:]).then_inc(x1_out, 16)

            with sp.Fori(0, NSEQ - 1) as s:
                step(s, 0, False)
                step(s, 1, False)
            step(NSEQ - 1, 0, True)
            step(NSEQ - 1, 1, True)
            sp.wait_ge(x1_ready, after_block(NBLK - 1))
            sp.dma_start(x1_v[NBLK], x1[1][:]).then_inc(x1_out, 16)
            sp.wait_ge(x1_out, 16 * (NBLK + 2))

        @block.gpsimd
        def _(pool):
            for s_, start in ((steps_ready, 2), (xw_ready, 2), (xd_ready, 2), (y_ready, 2), (g_ready, 2),
                              (ulo_done, 2), (rms_ready, 1), (rs_ready, 1)):
                pool.sem_inc(s_, start)
            pool.sem_inc(x1_out, 16)
            pool.sem_inc(ur_in[1], 16)
            for t, value in ((upto, 1.0), (after, 1.0), (ident, 0.0), (ones, 1.0), (c_eps, EPS), (c_inv, 1.0 / DI),
                             (c_mhalf, -0.5), (gb, 0.0), (yb, 0.0), (ur[1], 0.0), (x1[1], 0.0), (ss[1], 0.0),
                             (state, 0.0), (pre[0], 0.0)):
                nc.gpsimd.memset(t[:], value).then_inc(s_const, 1)
            NSET = 14
            pool.wait_ge(s_const, NSET)
            nc.gpsimd.affine_select(out=upto[:], in_=upto[:], compare_op=ALU.is_ge, fill=0.0, base=0,
                                    pattern=[[1, P]], channel_multiplier=-1).then_inc(s_const, 1)
            nc.gpsimd.affine_select(out=after[:], in_=after[:], compare_op=ALU.is_ge, fill=0.0, base=-1,
                                    pattern=[[-1, P]], channel_multiplier=1).then_inc(s_const, 1)
            nc.gpsimd.affine_select(out=ident[:], in_=ident[:], compare_op=ALU.not_equal, fill=1.0, base=0,
                                    pattern=[[-1, P]], channel_multiplier=1).then_inc(s_const, 1)
            pool.wait_ge(s_const, NSET + 3)
            pool.wait_ge(s_w, 16 * NW)

            def split_lo(n, par):
                pool.wait_ge(uhi_done, after_block(n))
                nc.gpsimd.tensor_tensor(u_lo[par][:], ut[par][:], u_hi[par][:].bitcast(F32),
                                        ALU.subtract).then_inc(ulo_done, 1)

            def make_steps(c, n, par, k):
                if k == 0:
                    pool.wait_ge(sp_chain, softplus(n))
                pool.wait_ge(seg_ps, after_chunk(c - 1))
                nc.gpsimd.tensor_tensor(
                    steps[:], upto[:].unsqueeze(1).broadcast_to([P, H, P]),
                    la[par][:, k * H:(k + 1) * H].unsqueeze(2).broadcast_to([P, H, P]), ALU.mult).then_inc(steps_ready, 1)

            def heads(t):
                return t[:].rearrange("p (h d) -> p h d", h=H)

            def per_head(t):
                return t.unsqueeze(2).broadcast_to([P, H, HD])

            def step(s, par, last):
                n = s * 2 + par
                for k in range(CH):
                    c = n * CH + k
                    if k == 0:
                        pool.wait_ge(dtw_ready, after_block(n))
                    pool.wait_ge(xs_ready, after_chunk(c))
                    pool.wait_ge(yd_ps, after_chunk(c - 1))
                    nc.gpsimd.tensor_tensor(heads(xdt), heads(xs), per_head(dt[par][:, k * H:(k + 1) * H]), ALU.mult)
                    nc.gpsimd.tensor_tensor(heads(xw), heads(xs), per_head(dtw[par][:, k * H:(k + 1) * H]),
                                            ALU.mult).then_inc(xw_ready, 1)
                    nc.gpsimd.tensor_tensor(heads(xd), heads(xs), per_head(rowb[:, 32:40]), ALU.mult).then_inc(xd_ready, 1)
                    if k < CH - 1:
                        make_steps(c + 1, n, par, k + 1)
                    elif not (last and par == 1):
                        make_steps(c + 1, n + 1, 1 - par, 0)
                    if k == 1:
                        pool.wait_ge(ss_ready, after_chunk(n * CH - 1))
                        nc.gpsimd.tensor_tensor(rms[:], ss[1 - par][:], c_inv[:], ALU.mult).then_inc(rms_chain, 1)
                        pool.wait_ge(rms_chain, n * 2 + 1)
                        nc.gpsimd.tensor_tensor(rms[:], rms[:], c_eps[:], ALU.add).then_inc(rms_chain, 1)
                        pool.wait_ge(rms_chain, n * 2 + 2)
                        nc.gpsimd.tensor_tensor(rms[:], rms[:], c_mhalf[:], ALU.pow).then_inc(rms_ready, 1)
                    if k == 2:
                        norm_scale(n)
                        if not last:
                            split_lo(n + 2, par)
                    pool.wait_ge(t2_done, after_chunk(c))
                    pool.wait_ge(xd_ready, after_chunk(c))
                    nc.gpsimd.tensor_tensor(yb[:], yb[:], xd[:], ALU.add).then_inc(y_ready, 1)
                    pool.wait_ge(gt_ps, after_chunk(c - 1))
                    pool.wait_ge(y_ready, after_chunk(c))
                    nc.gpsimd.tensor_tensor(gb[:], yb[:], zs[par][:, k, :], ALU.mult).then_inc(g_ready, 1)

            def norm_scale(n):
                pool.wait_ge(mv_ready, after_block(n - 1))
                nc.gpsimd.tensor_tensor(rs[:], mv[:, :, 1], c_eps[:], ALU.add).then_inc(rs_chain, 1)
                pool.wait_ge(rs_chain, n + 1)
                nc.gpsimd.tensor_tensor(rs[:], rs[:], c_mhalf[:], ALU.pow).then_inc(rs_ready, 1)

            split_lo(0, 0)
            split_lo(1, 1)
            make_steps(0, 0, 0, 0)
            with pool.Fori(0, NSEQ - 1) as s:
                step(s, 0, False)
                step(s, 1, False)
            step(NSEQ - 1, 0, True)
            step(NSEQ - 1, 1, True)
            n = NBLK
            pool.wait_ge(ss_ready, after_chunk(n * CH - 1))
            nc.gpsimd.tensor_tensor(rms[:], ss[1][:], c_inv[:], ALU.mult).then_inc(rms_chain, 1)
            pool.wait_ge(rms_chain, n * 2 + 1)
            nc.gpsimd.tensor_tensor(rms[:], rms[:], c_eps[:], ALU.add).then_inc(rms_chain, 1)
            pool.wait_ge(rms_chain, n * 2 + 2)
            nc.gpsimd.tensor_tensor(rms[:], rms[:], c_mhalf[:], ALU.pow).then_inc(rms_ready, 1)
            norm_scale(n)

        @block.scalar
        def _(act):
            for s_, start in ((ss_ready, 1), (ghi_done, 1), (out_ev, 1), (xs_ready, 2), (exp_done, 2),
                              (uhi_done, 2), (silu_done, 2), (dec_ready, 2), (sp_exp, 2), (sp_ln, 2)):
                act.sem_inc(s_, start)
            act.wait_ge(s_w, 16 * NW)
            nc.scalar.activation(expA[:], rowb[:, 0:24].rearrange("p (a h) -> p a h", a=3), ACT.Exp).then_inc(s_setup_a, 1)
            nc.scalar.copy(win_hi[:], win[:, :, 0:DTC]).then_inc(s_setup_a, 1)
            act.wait_ge(s_setup_v, 1)
            nc.scalar.copy(wo_hi[:], wo[:]).then_inc(s_setup_a, 1)
            act.wait_ge(s_const, 17)

            def split_hi(n, par, i):
                act.wait_ge(ut_in[par], 16 * (i + 1))
                nc.scalar.copy(u_hi[par][:], ut[par][:]).then_inc(uhi_done, 1)

            def evacuate(m, par, item):
                j = ORDER.index(item)
                b = ip_bank[j % 2]
                act.wait_ge(ip_ps, m * NI + j + 1)
                if item == "dt":
                    act.wait_ge(sp_chain, softplus(m - 1))
                    nc.scalar.copy(v_raw[:], b[:, 0:CH * H]).then_inc(ip_ev, 1)
                elif item == "cs":
                    nc.scalar.activation(dec[par][:], b[:, 0:3 * CH * H].rearrange("p (a c) -> p a c", a=3),
                                         ACT.Exp).then_inc(ip_ev, 1)
                elif isinstance(item, str):
                    nc.scalar.activation(zs[par][:, int(item[1]), :], b[:], ACT.Silu).then_inc(ip_ev, 1)
                else:
                    if item == 0:
                        if not (isinstance(m, int) and m == 0):
                            act.wait_ge(yo_ps, after_chunk(m * CH - CH - 1))
                    nc.scalar.copy(pre[par][:, item, TAPS - 1:], b[:])
                    nc.scalar.activation(xbc[par][:, item, :], b[:], ACT.Identity, bias=cb[:, item:item + 1],
                                         scale=cw[:, item, TAPS - 1:TAPS]).then_inc(ip_ev, 1)

            def softplus_exp(m):
                act.wait_ge(sp_chain, softplus(m, 2))
                nc.scalar.activation(v_e[:], v_neg[:], ACT.Exp).then_inc(sp_exp, 1)

            def softplus_ln(m):
                act.wait_ge(sp_chain, softplus(m, 3))
                nc.scalar.activation(v_l[:], v_w[:], ACT.Ln).then_inc(sp_ln, 1)

            def silu(m, par):
                act.wait_ge(taps_done, taps(m, CT - 1))
                nc.scalar.activation(xbc[par][:], xbc[par][:], ACT.Silu).then_inc(silu_done, 1)

            def square(c, par, k):
                act.wait_ge(y_ready, after_chunk(c))
                act.wait_ge(ss_ready, after_chunk(c - 1))
                nc.scalar.activation(sq[:], yb[:], ACT.Square, accum_out=ss[par][:, k:k + 1]).then_inc(ss_ready, 1)

            def g_high(c):
                act.wait_ge(gt_ps, after_chunk(c))
                act.wait_ge(out_ps, after_chunk(c - 1))
                nc.scalar.copy(g_hi[:].rearrange("p a b -> p (a b)"), yo_bank[:]).then_inc(ghi_done, 1)

            def take_out(c, par, k):
                act.wait_ge(out_ps, after_chunk(c))
                nc.scalar.copy(x1[par][:, k, :], out_bank).then_inc(out_ev, 1)

            def step(s, par, last):
                n = s * 2 + par
                more = not (last and par == 1)
                for k in range(CH):
                    c = n * CH + k
                    before = (par, k - 1) if k else (1 - par, CH - 1)
                    square(c - 1, *before)
                    act.wait_ge(xt_ps, after_chunk(c))
                    act.wait_ge(xd_ready, after_chunk(c - 1))
                    nc.scalar.copy(xs[:], xt_bank[:]).then_inc(xs_ready, 1)
                    g_high(c - 1)
                    act.wait_ge(seg_ps, after_chunk(c))
                    act.wait_ge(yd_ps, after_chunk(c - 1))
                    nc.scalar.activation(mt[:].rearrange("p h i -> p (h i)"), seg_bank[:], ACT.Exp).then_inc(exp_done, 1)
                    if more and k == 1:
                        softplus_exp(n + 1)
                    for half in range(2):
                        if more:
                            for item in ITEMS[k][half]:
                                evacuate(n + 1, 1 - par, item)
                    if more and k == 1:
                        softplus_ln(n + 1)
                    if k == 2 and not last:
                        split_hi(n + 2, par, s + 1)
                    if k == 1:
                        act.wait_ge(x1_out, 16 * (n + 1))
                    take_out(c - 1, *before)
                if more:
                    silu(n + 1, 1 - par)

            split_hi(0, 0, 0)
            split_hi(1, 1, 0)
            for item in ORDER[:NI]:
                if item == "cs":
                    softplus_exp(0)
                    softplus_ln(0)
                evacuate(0, 0, item)
            silu(0, 0)
            with act.Fori(0, NSEQ - 1) as s:
                step(s, 0, False)
                step(s, 1, False)
            step(NSEQ - 1, 0, True)
            step(NSEQ - 1, 1, True)
            c = NBLK * CH
            square(c - 1, 1, CH - 1)
            g_high(c - 1)
            take_out(c - 1, 1, CH - 1)

        @block.vector
        def _(dve):
            for s_, start in ((cbm_ready, 2), (mt_ready, 2), (y1_done, 2), (t2_done, 2), (st_scaled, 2), (st_ready, 2),
                              (glo_done, 1), (dtw_ready, 2), (sp_chain, 1), (res_done, 1), (stat_done, 1), (mv_ready, 1), (x1_ready, 1)):
                dve.sem_inc(s_, start)
            dve.wait_ge(s_w, 16 * NW)
            for k in range(OT):
                ins = nc.vector.tensor_scalar(wo[:, k, :], wo[:, k, :], nw[:, k:k + 1], None, ALU.mult)
            ins.then_inc(s_setup_v, 1)
            dve.wait_ge(s_setup_a, 1)
            nc.vector.tensor_tensor(sumA[:], expA[:, 0, :], expA[:, 1, :], ALU.add).then_inc(s_setup_v, 1)
            dve.wait_ge(s_setup_v, 2)
            nc.vector.tensor_tensor(negA[:], sumA[:], expA[:, 2, :], ALU.add).then_inc(s_setup_v, 1)
            dve.wait_ge(s_setup_v, 3)
            nc.vector.tensor_scalar(negA[:], negA[:], -1.0 / 3.0, None, ALU.mult).then_inc(s_setup_v, 1)
            dve.wait_ge(s_setup_a, 2)
            nc.vector.tensor_tensor(win_lo[:], win[:, :, 0:DTC], win_hi[:].bitcast(F32), ALU.subtract).then_inc(s_setup_v, 1)
            dve.wait_ge(s_setup_a, 3)
            nc.vector.tensor_tensor(wo_lo[:], wo[:], wo_hi[:].bitcast(F32), ALU.subtract).then_inc(s_setup_v, 1)
            dve.wait_ge(s_setup_v, 6)
            dve.wait_ge(s_const, 17)

            def by_head(row):
                return row.unsqueeze(1).broadcast_to([P, CH, H])

            def by_chunk(t):
                return t[:].rearrange("p (c h) -> p c h", c=CH)

            def convolve(s, m, par, tile):
                dve.wait_ge(ip_ev, m * NI + ORDER.index(tile) + 1)
                if par == 1:
                    nc.vector.tensor_copy(pre[1][:, tile, 0:TAPS - 1], pre[0][:, tile, T:T + TAPS - 1]).then_inc(halo_done, 1)
                    dve.wait_ge(halo_done, s * CT + tile + 1)
                for tap in range(TAPS - 1):
                    if tap:
                        dve.wait_ge(taps_done, taps(m, tile, tap))
                    nc.vector.scalar_tensor_tensor(out=xbc[par][:, tile, :], in0=pre[par][:, tile, tap:tap + T],
                                                   scalar=cw[:, tile, tap:tap + 1], in1=xbc[par][:, tile, :],
                                                   op0=ALU.mult, op1=ALU.add).then_inc(taps_done, 1)

            def softplus_a(m):
                dve.wait_ge(ip_ev, m * NI + ORDER.index("dt") + 1)
                nc.vector.tensor_tensor(by_chunk(v_dt), by_chunk(v_raw), by_head(rowb[:, 24:32]), ALU.add).then_inc(sp_chain, 1)
                dve.wait_ge(sp_chain, softplus(m, 1))
                nc.vector.scalar_tensor_tensor(out=v_neg[:], in0=v_dt[:], scalar=-1.0, in1=v_dt[:], op0=ALU.mult,
                                               op1=ALU.min).then_inc(sp_chain, 1)

            def softplus_b(m):
                dve.wait_ge(sp_exp, after_block(m))
                nc.vector.tensor_scalar(v_w[:], v_e[:], 1.0, None, ALU.add).then_inc(sp_chain, 1)
                dve.wait_ge(sp_chain, softplus(m, 3))
                nc.vector.tensor_scalar(v_d[:], v_w[:], -1.0, None, ALU.add).then_inc(sp_chain, 1)
                dve.wait_ge(sp_chain, softplus(m, 4))
                nc.vector.tensor_scalar(v_m[:], v_d[:], 0.0, None, ALU.is_equal).then_inc(sp_chain, 1)
                dve.wait_ge(sp_chain, softplus(m, 5))
                nc.vector.tensor_tensor(v_d[:], v_d[:], v_m[:], ALU.add).then_inc(sp_chain, 1)
                dve.wait_ge(sp_chain, softplus(m, 6))
                nc.vector.reciprocal(v_q[:], v_d[:]).then_inc(sp_chain, 1)
                nc.vector.tensor_tensor(v_p[:], v_e[:], v_m[:], ALU.mult).then_inc(sp_chain, 1)
                dve.wait_ge(sp_chain, softplus(m, 8))
                nc.vector.tensor_tensor(v_q[:], v_e[:], v_q[:], ALU.mult).then_inc(sp_chain, 1)

            def softplus_c(m, par):
                dve.wait_ge(sp_ln, after_block(m))
                dve.wait_ge(sp_chain, softplus(m, 9))
                nc.vector.tensor_tensor(v_q[:], v_l[:], v_q[:], ALU.mult).then_inc(sp_chain, 1)
                dve.wait_ge(sp_chain, softplus(m, 10))
                nc.vector.tensor_tensor(v_q[:], v_q[:], v_p[:], ALU.add).then_inc(sp_chain, 1)
                dve.wait_ge(sp_chain, softplus(m, 11))
                nc.vector.scalar_tensor_tensor(out=dt[par][:], in0=v_dt[:], scalar=0.0, in1=v_q[:], op0=ALU.max,
                                               op1=ALU.add).then_inc(sp_chain, 1)
                dve.wait_ge(sp_chain, softplus(m, 12))
                nc.vector.tensor_tensor(by_chunk(la[par]), by_chunk(dt[par]), by_head(negA[:]), ALU.mult).then_inc(sp_chain, 1)
                dve.wait_ge(sp_chain, softplus(m, 13))
                nc.vector.tensor_scalar(la[par][:], la[par][:], LOG_ZERO, None, ALU.max).then_inc(sp_chain, 1)

            def end_weights(m, par):
                dve.wait_ge(ip_ev, m * NI + ORDER.index("cs") + 1)
                nc.vector.tensor_tensor(dtw[par][:], dt[par][:], dec[par][:, 1, :], ALU.mult).then_inc(dtw_ready, 1)

            def g_low(c):
                dve.wait_ge(ghi_done, after_chunk(c))
                nc.vector.tensor_tensor(g_lo[:].rearrange("p a b -> p (a b)"), yo_bank[:],
                                        g_hi[:].rearrange("p a b -> p (a b)").bitcast(F32), ALU.subtract).then_inc(glo_done, 1)

            def residual(s, n, par):
                q = 1 - par
                dve.wait_ge(rms_ready, after_block(n - 1))
                dve.wait_ge(out_ev, after_chunk(n * CH - 1))
                dve.wait_ge(ur_in[q], 16 * (s + 1))
                for k in range(CH):
                    ins = nc.vector.scalar_tensor_tensor(out=x1[q][:, k, :], in0=x1[q][:, k, :], scalar=rms[:, k:k + 1],
                                                         in1=ur[q][:, k, :], op0=ALU.mult, op1=ALU.add)
                ins.then_inc(res_done, 1)
                dve.wait_ge(res_done, after_block(n - 1))
                for k in range(CH):
                    ins = nc.vector.bn_stats(stat[:, k, :], x1[q][:, k, :])
                ins.then_inc(stat_done, 1)
                dve.wait_ge(stat_done, after_block(n - 1))
                nc.vector.memset(tiny[:], 0.0)
                for k in range(CH):
                    ins = nc.vector.bn_aggr(mv[:, k, :], stat[:, k, :])
                ins.then_inc(mv_ready, 1)

            def normalise(n, par):
                q = 1 - par
                dve.wait_ge(rs_ready, after_block(n - 1))
                for k in range(CH):
                    ins = nc.vector.tensor_scalar(x1[q][:, k, :], x1[q][:, k, :], mv[:, k, 0:1], rs[:, k:k + 1],
                                                  ALU.subtract, ALU.mult)
                ins.then_inc(x1_ready, 1)

            def heads(t):
                return t[:].rearrange("p (h d) -> p h d", h=H)

            def per_head(t):
                return t.unsqueeze(2).broadcast_to([P, H, HD])

            def step(s, par, last):
                n = s * 2 + par
                m = n + 1
                more = not (last and par == 1)
                for k in range(CH):
                    c = n * CH + k
                    hk = slice(k * H, (k + 1) * H)
                    dve.wait_ge(cb_ps, after_chunk(c))
                    nc.vector.tensor_tensor(cbm[:], cb_bank[:, 0:P], upto[:], ALU.mult)
                    dve.wait_ge(st_ready, after_chunk(c - 1))
                    nc.vector.tensor_copy(b_tok[:], cb_bank[:, P:2 * P]).then_inc(cbm_ready, 1)
                    g_low(c - 1)
                    dve.wait_ge(exp_done, after_chunk(c))
                    dve.wait_ge(cbm_ready, after_chunk(c))
                    nc.vector.tensor_tensor(mt[:], mt[:], cbm[:].unsqueeze(1).broadcast_to([P, H, P]), ALU.mult).then_inc(mt_ready, 1)
                    dve.wait_ge(yo_ps, after_chunk(c))
                    dve.wait_ge(g_ready, after_chunk(c - 1))
                    dve.wait_ge(ss_ready, after_chunk(c - 1))
                    if par == 0 and k == 0:
                        nc.vector.memset(yb[:], 0.0).then_inc(y1_done, 1)
                        nc.vector.memset(state[:], 0.0).then_inc(st_scaled, 1)
                    else:
                        nc.vector.tensor_tensor(heads(yb), heads(yo_bank), per_head(dec[par][:, 0, hk]), ALU.mult).then_inc(y1_done, 1)
                        nc.vector.tensor_tensor(heads(state), heads(state), per_head(dec[par][:, 2, hk]), ALU.mult).then_inc(st_scaled, 1)
                    dve.wait_ge(ds_ps, after_chunk(c))
                    dve.wait_ge(st_scaled, after_chunk(c))
                    nc.vector.tensor_tensor(state[:], xt_bank[:], state[:], ALU.add).then_inc(st_ready, 1)
                    dve.wait_ge(yd_ps, after_chunk(c))
                    dve.wait_ge(y1_done, after_chunk(c))
                    nc.vector.tensor_tensor(yb[:], yd_bank[:], yb[:], ALU.add).then_inc(t2_done, 1)
                    if more:
                        if k == 0:
                            softplus_a(m)
                        if k == 1:
                            softplus_b(m)
                        for half in range(2):
                            for item in ITEMS[k][half]:
                                if isinstance(item, int):
                                    convolve(s + par, m, 1 - par, item)
                        if k == 1:
                            softplus_c(m, 1 - par)
                        if k == 2:
                            end_weights(m, 1 - par)
                    if k == 1:
                        residual(s, n, par)
                    if k == 3:
                        normalise(n, par)

            softplus_a(0)
            softplus_b(0)
            for tile in range(CT):
                convolve(0, 0, 0, tile)
            softplus_c(0, 0)
            end_weights(0, 0)
            with dve.Fori(0, NSEQ - 1) as s:
                step(s, 0, False)
                step(s, 1, False)
            step(NSEQ - 1, 0, True)
            step(NSEQ - 1, 1, True)
            g_low(NBLK * CH - 1)
            residual(NSEQ, NBLK, 0)
            normalise(NBLK, 0)

        @block.tensor
        def _(pe):
            for s_, start in ((cb_ps, 2), (xt_ps, 2), (seg_ps, 2), (yo_ps, 2), (ds_ps, 2), (yd_ps, 2), (gt_ps, 1), (out_ps, 1)):
                pe.sem_inc(s_, start)
            pe.wait_ge(s_w, 16 * NW)
            pe.wait_ge(s_const, 17)
            pe.wait_ge(s_setup_v, 6)
            PASSES = ((0, 0), (0, 1), (1, 0))
            w_parts = (win_hi, win_lo)

            def project(m, par, item):
                j = ORDER.index(item)
                b = ip_bank[j % 2]
                u_parts = (u_hi[par], u_lo[par])
                if j == 0:
                    pe.wait_ge(ulo_done, after_block(m))
                if not (isinstance(m, int) and m == 0 and j < 2):
                    pe.wait_ge(ip_ev, m * NI + j - 1)
                if item == "dt":
                    for q in range(CH):
                        for k in range(KT):
                            ins = pe.matmul(b[:, q * H:(q + 1) * H], ut[par][:, k, q * P:(q + 1) * P],
                                            win[:, k, DTC:DTC + H], start=(k == 0), stop=(k == KT - 1))
                elif item == "cs":
                    pe.wait_ge(sp_chain, softplus(m))
                    for i, mask in enumerate((upto, after, ones)):
                        ins = pe.matmul(b[:, i * CH * H:(i + 1) * CH * H], mask[:], la[par][:], start=True, stop=True)
                else:
                    for k in range(KT):
                        for a, w in PASSES:
                            if isinstance(item, str):
                                q = int(item[1])
                                lhs, rhs = u_parts[a][:, k, q * P:(q + 1) * P], w_parts[w][:, k, 0:DI]
                            else:
                                lhs = w_parts[w][:, k, DI + item * P:DI + (item + 1) * P]
                                rhs = u_parts[a][:, k, :]
                            ins = pe.matmul(b[:], lhs, rhs, start=(k == 0 and a + w == 0), stop=(k == KT - 1 and a == 1))
                ins.then_inc(ip_ps, 1)

            def g_transposes(c):
                pe.wait_ge(g_ready, after_chunk(c))
                for q in range(OT):
                    ins = pe.transpose(yo_bank[:, q * P:(q + 1) * P], gb[:, q * P:(q + 1) * P], ident[:])
                ins.then_inc(gt_ps, 1)

            def out_project(c):
                for k in range(OT):
                    for a, w in PASSES:
                        ins = pe.matmul(out_bank, (g_hi, g_lo)[a][:, k, :], (wo_hi, wo_lo)[w][:, k, :],
                                        start=(k == 0 and a + w == 0), stop=(k == OT - 1 and a == 1))
                ins.then_inc(out_ps, 1)

            def step(s, par, last):
                n = s * 2 + par
                more = not (last and par == 1)
                for k in range(CH):
                    c = n * CH + k
                    tok = slice(k * P, (k + 1) * P)
                    if k == 0:
                        pe.wait_ge(silu_done, after_block(n))
                    pe.wait_ge(cbm_ready, after_chunk(c - 1))
                    pe.matmul(cb_bank[:, 0:P], xbc[par][:, TB, tok], xbc[par][:, TC, tok], start=True, stop=True)
                    pe.transpose(cb_bank[:, P:2 * P], xbc[par][:, TB, tok], ident[:]).then_inc(cb_ps, 1)
                    pe.wait_ge(st_ready, after_chunk(c - 1))
                    for q in range(OT):
                        ins = pe.transpose(xt_bank[:, q * P:(q + 1) * P], xbc[par][:, q, tok], ident[:])
                    ins.then_inc(xt_ps, 1)
                    pe.wait_ge(steps_ready, after_chunk(c))
                    pe.matmul(seg_bank[:, 512:1024], after[:], steps[:, 4:8, :].rearrange("p h i -> p (h i)"), start=True, stop=True)
                    pe.wait_ge(out_ev, after_chunk(c - 2))
                    pe.matmul(seg_bank[:, 0:512], after[:], steps[:, 0:4, :].rearrange("p h i -> p (h i)"),
                              start=True, stop=True).then_inc(seg_ps, 1)
                    g_transposes(c - 1)
                    if more:
                        for item in ITEMS[k][0]:
                            project(n + 1, 1 - par, item)
                    pe.wait_ge(glo_done, after_chunk(c - 1))
                    pe.matmul(yo_bank[:], xbc[par][:, TC, tok], state[:], start=True, stop=True).then_inc(yo_ps, 1)
                    pe.wait_ge(xw_ready, after_chunk(c))
                    pe.wait_ge(cbm_ready, after_chunk(c))
                    pe.matmul(xt_bank[:], b_tok[:], xw[:], start=True, stop=True).then_inc(ds_ps, 1)
                    pe.wait_ge(mt_ready, after_chunk(c))
                    for h in range(H):
                        ins = pe.matmul(yd_bank[:, h * HD:(h + 1) * HD], mt[:, h, :], xdt[:, h * HD:(h + 1) * HD],
                                        start=True, stop=True)
                    ins.then_inc(yd_ps, 1)
                    if more:
                        for item in ITEMS[k][1]:
                            project(n + 1, 1 - par, item)
                    out_project(c - 1)

            for item in ORDER:
                project(0, 0, item)
            with pe.Fori(0, NSEQ - 1) as s:
                step(s, 0, False)
                step(s, 1, False)
            step(NSEQ - 1, 0, True)
            step(NSEQ - 1, 1, True)
            c = NBLK * CH
            g_transposes(c - 1)
            pe.wait_ge(glo_done, after_chunk(c - 1))
            out_project(c - 1)


def split_weights(nc, wts, w1, w3, w2):
    w13_hi, w13_lo, w2_hi, w2_lo = wts
    KT, NT, D = w13_hi.shape[2], w2_hi.shape[1], w2_hi.shape[2]
    G = 5
    NG = NT // G
    with ExitStack() as ctx:
        st13 = [ctx.enter_context(nc.sbuf_tensor(f"st13_{i}", [P, 2, KT, G * P], F32)) for i in range(2)]
        st2 = [ctx.enter_context(nc.sbuf_tensor(f"st2_{i}", [P, G, D], F32)) for i in range(2)]
        staged = [ctx.enter_context(nc.semaphore(f"staged{i}")) for i in range(2)]
        high_done = ctx.enter_context(nc.semaphore("high_done"))
        low_done = ctx.enter_context(nc.semaphore("low_done"))
        block = ctx.enter_context(nc.Block())

        def cols(g):
            return slice(g * G * P, (g + 1) * G * P)

        @block.sync
        def _(sp):
            for g in range(NG):
                if g >= 2:
                    sp.wait_ge(low_done, 3 * (g - 1))
                for i, w in enumerate((w1, w3)):
                    sp.dma_start(st13[g % 2][:, i], w.rearrange("(k p) c -> p k c", p=P)[:, :, cols(g)]).then_inc(staged[g % 2], 16)
                sp.dma_start(st2[g % 2][:], w2[:, g * G:(g + 1) * G, :]).then_inc(staged[g % 2], 16)

        @block.scalar
        def _(act):
            for g in range(NG):
                act.wait_ge(staged[g % 2], 48 * (g // 2 + 1))
                for i in range(2):
                    nc.scalar.copy(w13_hi[:, i, :, cols(g)], st13[g % 2][:, i]).then_inc(high_done, 1)
                nc.scalar.copy(w2_hi[:, g * G:(g + 1) * G, :], st2[g % 2][:]).then_inc(high_done, 1)

        @block.vector
        def _(dve):
            for g in range(NG):
                for i in range(2):
                    dve.wait_ge(high_done, 3 * g + i + 1)
                    nc.vector.tensor_tensor(w13_lo[:, i, :, cols(g)], st13[g % 2][:, i],
                                            w13_hi[:, i, :, cols(g)].bitcast(F32), ALU.subtract).then_inc(low_done, 1)
                dve.wait_ge(high_done, 3 * g + 3)
                nc.vector.tensor_tensor(w2_lo[:, g * G:(g + 1) * G, :], st2[g % 2][:],
                                        w2_hi[:, g * G:(g + 1) * G, :].bitcast(F32), ALU.subtract).then_inc(low_done, 1)


def experts(nc, wts, x1_dram, gate, rows, b1, b3, b2, sb2, rw_dram, out):
    w13_hi, w13_lo, w2_hi, w2_lo = wts
    KT = w13_hi.shape[2]
    NT = w2_hi.shape[1]
    D = w2_hi.shape[2]
    DT = D // P
    T = 512
    CH = T // P
    NBLK = out.shape[0] // T
    E = gate.shape[1]
    TILES = hidden_tiles()
    NSH = sum(t[0][2] == 8 for t in TILES)
    NR = NT - NSH
    LAG = 2
    HB = 5
    assert NT % HB == 0 and NT == len(TILES)

    with ExitStack() as ctx:
        def sb(name, shape, dt=F32):
            return ctx.enter_context(nc.sbuf_tensor(name, shape, dt))

        def bank(name):
            return ctx.enter_context(nc.psum_tensor(name, [P, T], F32))

        def sem(name):
            return ctx.enter_context(nc.semaphore(name))

        gate_f = sb("gate_f", [P, KT, E])
        gate_hi = sb("gate_hi", [P, KT, E], F32R)
        gate_lo = sb("gate_lo", [P, KT, E], F32R)
        gate_b = sb("gate_b", [P, 48])
        b1_sb = sb("b1_sb", [P, NT])
        b3_sb = sb("b3_sb", [P, NT])
        sb2_sb = sb("sb2_sb", [P, DT])
        b2_st = sb("b2_st", [4 * E, D], F32R)
        upper = sb("upper", [4 * E, 1])
        lower = sb("lower", [4 * E, 1])
        ident = sb("ident2", [P, P])
        before = sb("before", [P, E, E])
        c_eps = sb("c_eps2", [P, CH])
        c_mhalf = sb("c_mhalf2", [P, CH])

        x_in = sb("x_in", [P, CH, D])
        x_res = sb("x_res", [P, CH, D])
        x_hi = sb("x_hi", [P, KT, T], F32R)
        x_lo = sb("x_lo", [P, KT, T], F32R)
        hb = [sb(f"hb{i}", [P, T]) for i in range(HB)]
        h_hi = [sb(f"h_hi{i}", [P, T], F32R) for i in range(2)]
        h_lo = [sb(f"h_lo{i}", [P, T], F32R) for i in range(2)]
        rwb = sb("rwb", [P, E, T])
        yT = x_in[:].rearrange("p c d -> p (c d)").rearrange("p (k t) -> p k t", t=T)
        b2_f, b2_h, b2_l = hb[0][0:4 * E, 0:D], h_hi[0][0:4 * E, 0:D], hb[1][0:4 * E, 0:D]
        r = x_res
        mx = sb("mx", [P, CH])
        sh = sb("sh", [P, CH, E])
        es = sb("es", [P, CH, E])
        sm = sb("sm", [P, CH])
        rc = sb("rc", [P, CH])
        sc = sb("sc", [P, CH, E])
        bi = sb("bi", [P, CH, E])
        above, equal = (rwb[:, 0, i * 256:(i + 1) * 256].rearrange("p (c e f) -> p c e f", c=CH, e=E) for i in range(2))
        rank = sb("rank", [P, CH, E])
        rw_hi = sb("rw_hi", [P, CH, E], F32R)
        rw = rwb[:, 1, :].rearrange("p (c i) -> p c i", c=CH)
        rw_st = sb("rw_st", [4 * E, T], F32R)
        rw_f = sb("rw_f", [4 * E + E, T])
        stat = sb("stat2", [P, CH, 6])
        mv = sb("mv2", [P, CH, 2])
        rs = sb("rs2", [P, CH])
        tiny = sb("tiny2", [P, 1])

        h_bank = [[bank(f"h{i}_{w}") for w in (1, 3)] for i in range(2)]
        y_bank = [bank(f"y_bank{d}") for d in range(DT)]
        t_bank = [bank("t_bank0"), bank("t_bank1")]

        s_w, s_const, s_set_a, s_set_v = sem("e_w"), sem("e_const"), sem("e_set_a"), sem("e_set_v")
        x_loaded = sem("x_loaded")
        xres_loaded = sem("xres_loaded")
        xt_ps = sem("e_xt_ps")
        xhi_done = sem("xhi_done")
        xlo_done = sem("xlo_done")
        rt_ps = sem("rt_ps")
        rt_chain = sem("rt_chain")
        exp_done = sem("e_exp_done")
        rwt_ps = sem("rwt_ps")
        rwt_ev = sem("rwt_ev")
        rw_out = sem("rw_out")
        rwb_in = [sem("rwb_in0"), sem("rwb_in1")]
        h1_ps, h3_ps = sem("h1_ps"), sem("h3_ps")
        t_done, g_done, silu_done = sem("t_done"), sem("g_done"), sem("e_silu_done")
        sr_done, hi_done, lo_done = sem("sr_done"), sem("hi_done"), sem("lo_done")
        w2_ps, y_ev, yt_ps = sem("w2_ps"), sem("y_ev"), sem("yt_ps")
        res_done, stat_done, mv_ready = sem("e_res_done"), sem("e_stat_done"), sem("e_mv_ready")
        rs_chain, rs_ready, fin_done, stored = sem("e_rs_chain"), sem("e_rs_ready"), sem("fin_done"), sem("stored")

        x_v = x1_dram.rearrange("b (c p) d -> b p c d", p=P)
        out_v = out.rearrange("(b c p) d -> b p c d", p=P, c=CH)
        RT_OPS = 15

        def wait(eng, s_, value):
            if not (isinstance(value, int) and value <= 0):
                eng.wait_ge(s_, value)

        def tile_no(b, s):
            return b * NT + s + 1

        def routed_no(b, s):
            return b * NR + (s - NSH) + 1

        def route(b, i):
            return b * RT_OPS + i

        def banks(s):
            return t_bank if s == NT - 1 else h_bank[s % 2]

        block = ctx.enter_context(nc.Block())

        @block.sync
        def _(sp):
            sp.dma_start(x_in[:], x_v[1]).then_inc(x_loaded, 16)
            for dst, src in ((gate_f, gate.rearrange("(k p) e -> p k e", p=P)), (gate_b, rows.partition_broadcast(P)),
                             (b1_sb, b1), (b3_sb, b3), (sb2_sb, sb2)):
                sp.dma_start(dst[:], src).then_inc(s_w, 16)
            for i in range(4):
                sp.dma_start(b2_f[i * E:(i + 1) * E, :], b2).then_inc(s_w, 16)

            def loads(b):
                sp.wait_ge(rwt_ev, b + 1)
                sp.dma_start(rw_dram, rw_f[4 * E:5 * E, :]).then_inc(rw_out, 16)
                sp.wait_ge(rw_out, (b + 1) * 16)
                for i in range(2):
                    sp.dma_start(rwb[:, i * 4:(i + 1) * 4, :].rearrange("p e t -> p (e t)"),
                                 rw_dram[i * 4:(i + 1) * 4, :].rearrange("e t -> (e t)").partition_broadcast(P)).then_inc(rwb_in[i], 16)

            def next_in(b, first):
                if first:
                    sp.wait_ge(xt_ps, b + 1)
                else:
                    sp.wait_ge(yt_ps, b)
                sp.dma_start(x_in[:], x_v[b + 2]).then_inc(x_loaded, 16)

            def residual_in(b):
                sp.dma_start(x_res[:], x_v[b + 1]).then_inc(xres_loaded, 16)

            def store(b):
                sp.wait_ge(fin_done, b + 1)
                sp.dma_start(out_v[b], r[:]).then_inc(stored, 16)

            def body(b, last):
                loads(b)
                if not last:
                    next_in(b, False)
                store(b - 1)
                sp.wait_ge(stored, b * 16)
                residual_in(b)

            loads(0)
            next_in(0, True)
            residual_in(0)
            with sp.Fori(1, NBLK - 1) as b:
                body(b, False)
            body(NBLK - 1, True)
            store(NBLK - 1)
            sp.wait_ge(stored, NBLK * 16)

        @block.gpsimd
        def _(pool):
            for t, value in ((ident, 0.0), (before, 1.0), (upper, 1.0), (lower, 1.0), (c_eps, EPS), (c_mhalf, -0.5), (rwb[:, 1], 0.0)):
                nc.gpsimd.memset(t[:], value).then_inc(s_const, 1)
            pool.wait_ge(s_const, 7)
            nc.gpsimd.affine_select(out=ident[:], in_=ident[:], compare_op=ALU.not_equal, fill=1.0, base=0,
                                    pattern=[[-1, P]], channel_multiplier=1).then_inc(s_const, 1)
            nc.gpsimd.affine_select(out=before[:], in_=before[:], compare_op=ALU.is_ge, fill=0.0, base=-1,
                                    pattern=[[1, E], [-1, E]], channel_multiplier=0).then_inc(s_const, 1)
            nc.gpsimd.affine_select(out=upper[:], in_=upper[:], compare_op=ALU.is_ge, fill=0.0, base=-2 * E,
                                    pattern=[[1, 1]], channel_multiplier=1).then_inc(s_const, 1)
            nc.gpsimd.affine_select(out=lower[:], in_=lower[:], compare_op=ALU.is_ge, fill=0.0, base=2 * E - 1,
                                    pattern=[[1, 1]], channel_multiplier=-1).then_inc(s_const, 1)

            def norm_scale(b):
                pool.wait_ge(mv_ready, b + 1)
                nc.gpsimd.tensor_tensor(rs[:], mv[:, :, 1], c_eps[:], ALU.add).then_inc(rs_chain, 1)
                pool.wait_ge(rs_chain, b + 1)
                nc.gpsimd.tensor_tensor(rs[:], rs[:], c_mhalf[:], ALU.pow).then_inc(rs_ready, 1)

            with pool.Fori(1, NBLK) as b:
                norm_scale(b - 1)
            norm_scale(NBLK - 1)

        @block.scalar
        def _(act):
            act.wait_ge(s_w, 16 * 9)
            nc.scalar.copy(gate_hi[:], gate_f[:]).then_inc(s_set_a, 1)
            nc.scalar.copy(b2_h, b2_f).then_inc(s_set_a, 1)

            def high(b, s):
                if s >= NSH:
                    act.wait_ge(sr_done, routed_no(b, s))
                else:
                    act.wait_ge(silu_done, tile_no(b, s))
                wait(act, w2_ps, tile_no(b, s) - 2 if s else tile_no(b, -1))
                nc.scalar.copy(h_hi[s % 2][:], hb[s % HB][:]).then_inc(hi_done, 1)

            def x_high(b):
                act.wait_ge(xt_ps, b + 1)
                for k in range(KT):
                    nc.scalar.copy(x_hi[:, k, :], h_bank[0][k][:]).then_inc(xhi_done, 1)

            def take_y(b):
                act.wait_ge(w2_ps, tile_no(b, NT - 1))
                for d in range(DT):
                    ins = nc.scalar.activation(yT[:, d, :], y_bank[d][:], ACT.Identity, bias=sb2_sb[:, d:d + 1])
                ins.then_inc(y_ev, 1)

            def body(b, first):
                x_high(b)
                if not first:
                    high(b - 1, NT - 1)
                    take_y(b - 1)
                act.wait_ge(rt_chain, route(b, 2))
                nc.scalar.activation(es[:], sh[:], ACT.Exp).then_inc(exp_done, 1)
                for s in range(NT):
                    act.wait_ge(h1_ps, tile_no(b, s))
                    wait(act, lo_done, tile_no(b, s) - HB)
                    nc.scalar.activation(hb[s % HB][:], banks(s)[0][:], ACT.Identity, bias=b1_sb[:, s:s + 1]).then_inc(t_done, 1)
                    if s:
                        high(b, s - 1)
                    act.wait_ge(g_done, tile_no(b, s))
                    nc.scalar.activation(hb[s % HB][:], hb[s % HB][:], ACT.Silu).then_inc(silu_done, 1)
                    if s == 2:
                        act.wait_ge(rwt_ps, b + 1)
                        nc.scalar.copy(rw_st[:], t_bank[1][0:4 * E, :])
                        nc.scalar.copy(rw_f[4 * E:5 * E, :], t_bank[1][4 * E:5 * E, :]).then_inc(rwt_ev, 1)

            body(0, True)
            with act.Fori(1, NBLK) as b:
                body(b, False)
            high(NBLK - 1, NT - 1)
            take_y(NBLK - 1)

        @block.vector
        def _(dve):
            dve.wait_ge(s_set_a, 1)
            nc.vector.tensor_tensor(gate_lo[:], gate_f[:], gate_hi[:].bitcast(F32), ALU.subtract).then_inc(s_set_v, 1)
            dve.wait_ge(s_set_a, 2)
            nc.vector.tensor_tensor(b2_l, b2_f, b2_h.bitcast(F32), ALU.subtract).then_inc(s_set_v, 1)
            dve.wait_ge(s_const, 11)
            dve.wait_ge(s_set_v, 2)
            nc.vector.tensor_scalar(b2_l, b2_l, upper[:, 0:1], None, ALU.mult).then_inc(s_set_v, 1)
            dve.wait_ge(s_set_v, 3)
            nc.vector.scalar_tensor_tensor(out=b2_st[:], in0=b2_h.bitcast(F32), scalar=lower[:, 0:1], in1=b2_l,
                                           op0=ALU.mult, op1=ALU.add).then_inc(s_set_v, 1)
            dve.wait_ge(s_set_v, 4)

            def gated(b, s):
                dve.wait_ge(h3_ps, tile_no(b, s))
                dve.wait_ge(t_done, tile_no(b, s))
                nc.vector.scalar_tensor_tensor(out=hb[s % HB][:], in0=banks(s)[1][:], scalar=b3_sb[:, s:s + 1],
                                               in1=hb[s % HB][:], op0=ALU.add, op1=ALU.mult).then_inc(g_done, 1)

            def low(b, s):
                dve.wait_ge(hi_done, tile_no(b, s))
                nc.vector.tensor_tensor(h_lo[s % 2][:], hb[s % HB][:], h_hi[s % 2][:].bitcast(F32), ALU.subtract).then_inc(lo_done, 1)

            def weigh(b, s):
                dve.wait_ge(silu_done, tile_no(b, s))
                if s == NSH:
                    dve.wait_ge(rwb_in[0], (b + 1) * 16)
                if s == NSH + NR // 2:
                    dve.wait_ge(rwb_in[1], (b + 1) * 16)
                for row, n, e, _ in TILES[s]:
                    ins = nc.vector.tensor_tensor(hb[s % HB][row:row + n, :], hb[s % HB][row:row + n, :],
                                                  rwb[row:row + n, e, :], ALU.mult)
                ins.then_inc(sr_done, 1)

            def x_low(b):
                for k in range(KT):
                    dve.wait_ge(xhi_done, b * KT + k + 1)
                    nc.vector.tensor_tensor(x_lo[:, k, :], h_bank[0][k][:], x_hi[:, k, :].bitcast(F32), ALU.subtract).then_inc(xlo_done, 1)

            logits = t_bank[0][:, 0:CH * E].rearrange("p (c e) -> p c e", c=CH)

            def over_e(t):
                return t[:].unsqueeze(2).broadcast_to([P, CH, E])

            def route_a(b):
                dve.wait_ge(rt_ps, b + 1)
                nc.vector.tensor_reduce(mx[:], logits, AX.X, ALU.max).then_inc(rt_chain, 1)
                dve.wait_ge(rt_chain, route(b, 1))
                nc.vector.tensor_tensor(sh[:], logits, over_e(mx), ALU.subtract).then_inc(rt_chain, 1)

            def route_b(b):
                dve.wait_ge(exp_done, b + 1)
                nc.vector.tensor_reduce(sm[:], es[:], AX.X, ALU.add).then_inc(rt_chain, 1)
                dve.wait_ge(rt_chain, route(b, 3))
                nc.vector.reciprocal(rc[:], sm[:]).then_inc(rt_chain, 1)
                dve.wait_ge(rt_chain, route(b, 4))
                nc.vector.tensor_tensor(sc[:], es[:], over_e(rc), ALU.mult).then_inc(rt_chain, 1)
                dve.wait_ge(rt_chain, route(b, 5))
                nc.vector.tensor_tensor(bi[:], sc[:], gate_b[:, 40:48].unsqueeze(1).broadcast_to([P, CH, E]), ALU.add).then_inc(rt_chain, 1)
                dve.wait_ge(rt_chain, route(b, 6))

            def route_c(b):
                mine = bi[:].unsqueeze(3).broadcast_to([P, CH, E, E])
                other = bi[:].unsqueeze(2).broadcast_to([P, CH, E, E])
                nc.vector.tensor_tensor(above, other, mine, ALU.is_gt).then_inc(rt_chain, 1)
                nc.vector.tensor_tensor(equal, other, mine, ALU.is_equal).then_inc(rt_chain, 1)
                dve.wait_ge(rt_chain, route(b, 8))
                nc.vector.tensor_tensor(equal, equal, before[:].unsqueeze(1).broadcast_to([P, CH, E, E]), ALU.mult).then_inc(rt_chain, 1)
                dve.wait_ge(rt_chain, route(b, 9))
                nc.vector.tensor_tensor(above, above, equal, ALU.add).then_inc(rt_chain, 1)
                dve.wait_ge(rt_chain, route(b, 10))
                nc.vector.tensor_reduce(rank[:], above, AX.X, ALU.add).then_inc(rt_chain, 1)
                dve.wait_ge(rt_chain, route(b, 11))
                nc.vector.scalar_tensor_tensor(out=rw[:, :, 4 * E:5 * E], in0=rank[:], scalar=2.0, in1=sc[:],
                                               op0=ALU.is_lt, op1=ALU.mult).then_inc(rt_chain, 1)
                dve.wait_ge(rt_chain, route(b, 12))
                nc.vector.tensor_copy(rw_hi[:], rw[:, :, 4 * E:5 * E]).then_inc(rt_chain, 1)
                dve.wait_ge(rt_chain, route(b, 13))
                pairs = rw[:, :, 0:4 * E].rearrange("p c (i e) -> p c i e", e=2 * E)
                high_part = rw_hi[:].bitcast(F32).unsqueeze(2).broadcast_to([P, CH, 2, E])
                nc.vector.tensor_copy(pairs[:, :, :, 0:E], high_part).then_inc(rt_chain, 1)
                nc.vector.tensor_tensor(pairs[:, :, :, E:2 * E], rw[:, :, 4 * E:5 * E].unsqueeze(2).broadcast_to([P, CH, 2, E]),
                                        high_part, ALU.subtract).then_inc(rt_chain, 1)

            def residual(b):
                dve.wait_ge(yt_ps, b + 1)
                dve.wait_ge(xres_loaded, (b + 1) * 16)
                for i in range(2):
                    ins = nc.vector.tensor_tensor(r[:, 2 * i:2 * i + 2, :].rearrange("p c d -> p (c d)"), t_bank[i][:],
                                                  x_res[:, 2 * i:2 * i + 2, :].rearrange("p c d -> p (c d)"), ALU.add)
                ins.then_inc(res_done, 1)
                dve.wait_ge(res_done, b + 1)
                for k in range(CH):
                    ins = nc.vector.bn_stats(stat[:, k, :], r[:, k, :])
                ins.then_inc(stat_done, 1)
                dve.wait_ge(stat_done, b + 1)
                nc.vector.memset(tiny[:], 0.0)
                for k in range(CH):
                    ins = nc.vector.bn_aggr(mv[:, k, :], stat[:, k, :])
                ins.then_inc(mv_ready, 1)

            def normalise(b):
                dve.wait_ge(rs_ready, b + 1)
                for k in range(CH):
                    ins = nc.vector.tensor_scalar(r[:, k, :], r[:, k, :], mv[:, k, 0:1], rs[:, k:k + 1], ALU.subtract, ALU.mult)
                ins.then_inc(fin_done, 1)

            def body(b, first):
                x_low(b)
                if not first:
                    low(b - 1, NT - 1)
                route_a(b)
                for s in range(NT):
                    gated(b, s)
                    if s:
                        low(b, s - 1)
                    if s >= NSH:
                        weigh(b, s)
                    if s == 0:
                        route_b(b)
                    if s == 1:
                        route_c(b)
                    if not first and s == 5:
                        residual(b - 1)
                    if not first and s == 8:
                        normalise(b - 1)

            body(0, True)
            with dve.Fori(1, NBLK) as b:
                body(b, False)
            low(NBLK - 1, NT - 1)
            residual(NBLK - 1)
            normalise(NBLK - 1)

        @block.tensor
        def _(pe):
            PASSES = ((0, 0), (0, 1), (1, 0))
            pe.wait_ge(s_const, 11)
            pe.wait_ge(s_set_v, 4)
            x_parts, h_parts = (x_hi, x_lo), (h_hi, h_lo)
            w13_parts, w2_parts, gate_parts = (w13_hi, w13_lo), (w2_hi, w2_lo), (gate_hi, gate_lo)

            def x_transposes(b):
                pe.wait_ge(x_loaded, (b + 1) * 16)
                wait(pe, g_done, tile_no(b, 0) - 3)
                for k in range(KT):
                    for c in range(CH):
                        ins = pe.transpose(h_bank[0][k][:, c * P:(c + 1) * P], x_in[:, c, k * P:(k + 1) * P], ident[:])
                ins.then_inc(xt_ps, 1)

            def router(b):
                pe.wait_ge(xlo_done, (b + 1) * KT)
                wait(pe, g_done, tile_no(b, -1))
                for c in range(CH):
                    for k in range(KT):
                        for a, w in PASSES:
                            ins = pe.matmul(t_bank[0][:, c * E:(c + 1) * E], x_parts[a][:, k, c * P:(c + 1) * P],
                                            gate_parts[w][:, k, :], start=(k == 0 and a + w == 0), stop=(k == KT - 1 and a == 1))
                ins.then_inc(rt_ps, 1)

            def hidden(b, s):
                if s == NT - 1:
                    pe.wait_ge(rwt_ev, b + 1)
                    wait(pe, res_done, b)
                elif s == 1:
                    wait(pe, g_done, tile_no(b, -2))
                elif s:
                    pe.wait_ge(g_done, tile_no(b, s - 2))
                for i, done in enumerate((h1_ps, h3_ps)):
                    for k in range(KT):
                        for a, w in PASSES:
                            ins = pe.matmul(banks(s)[i][:], w13_parts[w][:, i, k, s * P:(s + 1) * P], x_parts[a][:, k, :],
                                            start=(k == 0 and a + w == 0), stop=(k == KT - 1 and a == 1))
                    ins.then_inc(done, 1)

            def down(b, s):
                pe.wait_ge(lo_done, tile_no(b, s))
                if s == 0:
                    wait(pe, y_ev, b)
                for d in range(DT):
                    for a, w in PASSES:
                        ins = pe.matmul(y_bank[d][:], w2_parts[w][:, s, d * P:(d + 1) * P], h_parts[a][s % 2][:],
                                        start=(s == 0 and a + w == 0), stop=(s == NT - 1 and a == 1))
                ins.then_inc(w2_ps, 1)

            def rw_transposes(b):
                pe.wait_ge(rt_chain, route(b, RT_OPS))
                for c in range(CH):
                    ins = pe.transpose(t_bank[1][:, c * P:(c + 1) * P], rw[:, c, :], ident[:])
                ins.then_inc(rwt_ps, 1)

            def bias_down(b):
                for d in range(DT):
                    pe.matmul(y_bank[d][:], b2_st[:, d * P:(d + 1) * P], rw_st[:], start=False, stop=False)

            def y_transposes(b):
                pe.wait_ge(y_ev, b + 1)
                for c in range(CH):
                    for d in range(DT):
                        ins = pe.transpose(t_bank[c // 2][:, (c % 2) * D + d * P:(c % 2) * D + (d + 1) * P],
                                           yT[:, d, c * P:(c + 1) * P], ident[:])
                ins.then_inc(yt_ps, 1)

            def body(b, first):
                x_transposes(b)
                if not first:
                    down(b - 1, NT - 2)
                router(b)
                if not first:
                    down(b - 1, NT - 1)
                for s in range(NT):
                    hidden(b, s)
                    if s >= LAG:
                        down(b, s - LAG)
                    if s == 1:
                        rw_transposes(b)
                    if s == 4:
                        pe.wait_ge(rwt_ev, b + 1)
                        bias_down(b)
                        if not first:
                            y_transposes(b - 1)

            body(0, True)
            with pe.Fori(1, NBLK) as b:
                body(b, False)
            down(NBLK - 1, NT - 2)
            down(NBLK - 1, NT - 1)
            y_transposes(NBLK - 1)


def build(nc, a, out):
    tok, d = out.shape
    nt = len(hidden_tiles())
    x1_dram = nc.dram_tensor("x1_dram", (tok // 512 + 1, 512, d), F32, kind="Internal").ap()
    rw_dram = nc.dram_tensor("rw_dram", (8, 512), F32, kind="Internal").ap()
    mixer(nc, a["uT"], a["u"], a["w_in"], a["conv_w"], a["conv_b"], a["rows"], a["norm_w"], a["w_out"], x1_dram)
    with ExitStack() as ctx:
        wts = [ctx.enter_context(nc.sbuf_tensor(n, s, F32R)) for n, s in (
            ("w13_hi", [P, 2, d // P, nt * P]), ("w13_lo", [P, 2, d // P, nt * P]), ("w2_hi", [P, nt, d]), ("w2_lo", [P, nt, d]))]
        split_weights(nc, wts, a["f_w1"], a["f_w3"], a["f_w2"])
        experts(nc, wts, x1_dram, a["f_gate"], a["rows"], a["f_b1"], a["f_b3"], a["f_b2"], a["f_sb2"], rw_dram, out)


def _layout(inputs):
    import numpy as np
    g = {k.split("_", 2)[2] if k.startswith("L0_attn") else "f_" + k.split("_", 2)[2]: np.asarray(v) for k, v in inputs.items()}
    u = g["u"].reshape(-1, g["u"].shape[-1])
    D = u.shape[1]
    tiles = hidden_tiles()
    a = {
        "uT": u.T, "u": u, "w_in": g["in_proj_w"].T,
        "conv_w": g["conv_w"][:, 0, :].reshape(-1, P, 4).transpose(1, 0, 2), "conv_b": g["conv_b"].reshape(-1, P).T,
        "rows": np.concatenate([g["A_log"].ravel(), g["dt_bias"], g["D"], g["f_gate_b"]]),
        "norm_w": g["norm_w"].reshape(-1, P).T, "w_out": g["out_proj_w"].T,
    }

    def cols(per_expert, shared):
        both = np.concatenate([per_expert, shared[None]])
        out = np.zeros((both.shape[1], len(tiles) * P), both.dtype)
        for t, parts in enumerate(tiles):
            for row, n, e, col in parts:
                out[:, t * P + row:t * P + row + n] = both[e][:, col:col + n]
        return out

    for i in "13":
        a["f_w" + i] = cols(g["f_w" + i], g["f_sw" + i])
        a["f_b" + i] = cols(g["f_b" + i][:, None, :], g["f_sb" + i][None]).reshape(len(tiles), P).T
    a["f_w2"] = cols(g["f_w2"].transpose(0, 2, 1), g["f_sw2"].T).T.reshape(len(tiles), P, D).transpose(1, 0, 2)
    a["f_gate"] = g["f_gate_w"].T
    a["f_b2"] = g["f_b2"]
    a["f_sb2"] = g["f_sb2"].reshape(-1, P).T
    return {k: np.ascontiguousarray(v) for k, v in a.items()}


def kernel(**inputs):
    import concourse.bacc as bacc
    from concourse.bass_utils import run_bass_kernel_spmd

    shape = inputs["L0_attn_u"].shape
    arrays = _layout(inputs)
    nc = bacc.Bacc("TRN2", target_bir_lowering=False, num_devices=1)
    a = {k: nc.dram_tensor("in_" + k, v.shape, mybir.dt.from_np(v.dtype), kind="ExternalInput").ap() for k, v in arrays.items()}
    tok, d = arrays["u"].shape
    out = nc.dram_tensor("out", (tok, d), F32, kind="ExternalOutput").ap()
    build(nc, a, out)
    r = run_bass_kernel_spmd(nc, [{"in_" + k: v for k, v in arrays.items()}], core_ids=[0])
    return r.results[0]["out"].reshape(shape)
```

```python
from contextlib import ExitStack

import concourse.bass as bass
from concourse import mybir

F32 = mybir.dt.float32
F32R = mybir.dt.float32r
I32 = mybir.dt.int32
ALU = mybir.AluOpType
ACT = mybir.ActivationFunctionType
AX = mybir.AxisListType

P = 128
PASSES = ((0, 0), (0, 1), (1, 0))
EPS = 1e-5
LOG_ZERO = -104.0

HEAD = 3

TILE = 256
TOP = 2


def routed_tiles(tok, experts):
    return (tok * TOP + experts * (TILE - 1)) // TILE


def mixer(nc, uT, u, w_in, conv_w, conv_b, rows, norm_w, w_out, x1_dram):
    D, TOK = uT.shape
    KT = D // P
    T = 512
    CH = T // P
    SEQ = 1024
    NBLK = TOK // T
    NSEQ = TOK // SEQ
    H, HD = 8, 64
    DI = H * HD
    CT = (DI + 2 * P) // P
    TB, TC = DI // P, DI // P + 1
    OT = DI // P
    COLS = w_in.shape[1]
    DTC = COLS - H
    TAPS = 4
    assert SEQ == 2 * T and CH * H == 32

    with ExitStack() as ctx:
        def sb(name, shape, dt=F32):
            return ctx.enter_context(nc.sbuf_tensor(name, shape, dt))

        def bank(name, cols=512):
            return ctx.enter_context(nc.psum_tensor(name, [P, cols], F32))

        def sem(name):
            return ctx.enter_context(nc.semaphore(name))

        win = sb("win", [P, KT, COLS])
        win_hi = sb("win_hi", [P, KT, DTC], F32R)
        win_lo = sb("win_lo", [P, KT, DTC], F32R)
        wo = sb("wo", [P, OT, D])
        wo_hi = sb("wo_hi", [P, OT, D], F32R)
        wo_lo = sb("wo_lo", [P, OT, D], F32R)
        cw = sb("cw", [P, CT, TAPS])
        cb = sb("cb", [P, CT])
        nw = sb("nw", [P, OT])
        rowb = sb("rowb", [P, 48])
        expA = sb("expA", [P, 3, H])
        sumA = sb("sumA", [P, H])
        negA = sb("negA", [P, H])
        upto = sb("upto", [P, P])
        after = sb("after", [P, P])
        ones = sb("ones", [P, P])
        ident = sb("ident", [P, P])
        c_eps = sb("c_eps", [P, CH])
        c_inv = sb("c_inv", [P, CH])
        c_mhalf = sb("c_mhalf", [P, CH])
        ut = [sb(f"ut{i}", [P, KT, T]) for i in range(2)]
        u_hi = [sb(f"u_hi{i}", [P, KT, T], F32R) for i in range(2)]
        u_lo = [sb(f"u_lo{i}", [P, KT, T], F32R) for i in range(2)]
        pre = [sb(f"pre{i}", [P, CT, TAPS - 1 + T]) for i in range(2)]
        xbc = [sb(f"xbc{i}", [P, CT, T]) for i in range(2)]
        zs = [sb(f"zs{i}", [P, CH, DI]) for i in range(2)]
        dt = [sb(f"dt{i}", [P, CH * H]) for i in range(2)]
        la = [sb(f"la{i}", [P, CH * H]) for i in range(2)]
        dec = [sb(f"dec{i}", [P, 3, CH * H]) for i in range(2)]
        dtw = [sb(f"dtw{i}", [P, CH * H]) for i in range(2)]
        ur = [sb(f"ur{i}", [P, CH, D]) for i in range(2)]
        x1 = [sb(f"x1_{i}", [P, CH, D]) for i in range(2)]
        ss = [sb(f"ss{i}", [P, CH]) for i in range(2)]
        v_raw, v_dt, v_neg, v_e, v_w, v_d, v_m, v_l, v_q, v_p = (
            sb(n, [P, CH * H]) for n in ("v_raw", "v_dt", "v_neg", "v_e", "v_w", "v_d", "v_m", "v_l", "v_q", "v_p"))
        steps = sb("steps", [P, H, P])
        mt = sb("mt", [P, H, P])
        cbm = sb("cbm", [P, P])
        b_tok = sb("b_tok", [P, P])
        xs = sb("xs", [P, DI])
        xdt = sb("xdt", [P, DI])
        xw = sb("xw", [P, DI])
        xd = sb("xd", [P, DI])
        yb = sb("yb", [P, DI])
        gb = sb("gb", [P, DI])
        sq = sb("sq", [P, DI])
        g_hi = sb("g_hi", [P, OT, P], F32R)
        g_lo = sb("g_lo", [P, OT, P], F32R)
        state = sb("state", [P, DI])
        rms = sb("rms", [P, CH])
        stat = sb("stat", [P, CH, 6])
        mv = sb("mv", [P, CH, 2])
        rs = sb("rs", [P, CH])
        tiny = sb("tiny", [P, 1])

        ip_bank = [bank("ip_bank0"), bank("ip_bank1")]
        seg_bank = bank("seg_bank", 1024)
        out_bank = seg_bank[:, 0:D]
        cb_bank = bank("cb_bank")
        xt_bank = bank("xt_bank")
        yd_bank = bank("yd_bank")
        yo_bank = bank("yo_bank")

        s_w = sem("s_w")
        ut_in = [sem(f"ut_in{i}") for i in range(2)]
        ur_in = [sem(f"ur_in{i}") for i in range(2)]
        x1_out = sem("x1_out")
        s_const = sem("s_const")
        s_setup_a = sem("s_setup_a")
        s_setup_v = sem("s_setup_v")
        s_ready = sem("s_ready")
        ip_ps = sem("ip_ps")
        ip_ev = sem("ip_ev")
        uhi_done = sem("uhi_done")
        ulo_done = sem("ulo_done")
        taps_done = sem("taps_done")
        halo_done = sem("halo_done")
        silu_done = sem("silu_done")
        sp_chain = sem("sp_chain")
        sp_exp = sem("sp_exp")
        sp_ln = sem("sp_ln")
        dec_ready = sem("dec_ready")
        dtw_ready = sem("dtw_ready")
        cb_ps = sem("cb_ps")
        xt_ps = sem("xt_ps")
        seg_ps = sem("seg_ps")
        yo_ps = sem("yo_ps")
        ds_ps = sem("ds_ps")
        yd_ps = sem("yd_ps")
        gt_ps = sem("gt_ps")
        out_ps = sem("out_ps")
        steps_ready = sem("steps_ready")
        xs_ready = sem("xs_ready")
        xw_ready = sem("xw_ready")
        xd_ready = sem("xd_ready")
        cbm_ready = sem("cbm_ready")
        exp_done = sem("exp_done")
        mt_ready = sem("mt_ready")
        y1_done = sem("y1_done")
        t2_done = sem("t2_done")
        st_scaled = sem("st_scaled")
        st_ready = sem("st_ready")
        y_ready = sem("y_ready")
        g_ready = sem("g_ready")
        ss_ready = sem("ss_ready")
        ghi_done = sem("ghi_done")
        glo_done = sem("glo_done")
        out_ev = sem("out_ev")
        rms_chain = sem("rms_chain")
        rms_ready = sem("rms_ready")
        res_done = sem("res_done")
        stat_done = sem("stat_done")
        mv_ready = sem("mv_ready")
        rs_chain = sem("rs_chain")
        rs_ready = sem("rs_ready")
        x1_ready = sem("x1_ready")

        uT_v = uT.rearrange("(k p) (b t) -> b p k t", p=P, t=T)
        u_v = u.rearrange("(b c p) d -> b p c d", p=P, c=CH)
        x1_v = x1_dram.rearrange("b (c p) d -> b p c d", p=P)
        NW = 6

        ITEMS = [[["dt", 0], [1, 2]], [[3], [4]], [[5], ["cs"]], [["z0", "z1"], ["z2", "z3"]]]
        ORDER = [x for slot in ITEMS for half in slot for x in half]
        NI = len(ORDER)

        def after_chunk(j):
            return j + HEAD

        def after_block(n):
            return n + HEAD

        SP_OPS = 14

        def softplus(m, i=SP_OPS):
            return m * SP_OPS + i + 1

        def taps(m, tile, i=TAPS - 1):
            return (m * CT + tile) * (TAPS - 1) + i

        block = ctx.enter_context(nc.Block())

        @block.sync
        def _(sp):
            for dst, src in ((win, w_in.rearrange("(k p) c -> p k c", p=P)), (wo, w_out.rearrange("(k p) c -> p k c", p=P)),
                             (cw, conv_w), (nw, norm_w), (cb, conv_b)):
                sp.dma_start(dst[:], src).then_inc(s_w, 16)
            sp.dma_start(rowb[:], rows.partition_broadcast(P)).then_inc(s_w, 16)
            sp.dma_start(ut[0][:], uT_v[0]).then_inc(ut_in[0], 16)
            sp.dma_start(ut[1][:], uT_v[1]).then_inc(ut_in[1], 16)

            def step(s, par, last):
                n = s * 2 + par
                sp.wait_ge(x1_ready, after_block(n - 2))
                sp.dma_start(ur[par][:], u_v[n]).then_inc(ur_in[par], 16)
                if not last:
                    sp.wait_ge(ip_ps, (n + 1) * NI)
                    sp.dma_start(ut[par][:], uT_v[n + 2]).then_inc(ut_in[par], 16)
                sp.wait_ge(x1_ready, after_block(n - 1))
                sp.dma_start(x1_v[n], x1[1 - par][:]).then_inc(x1_out, 16)

            with sp.Fori(0, NSEQ - 1) as s:
                step(s, 0, False)
                step(s, 1, False)
            step(NSEQ - 1, 0, True)
            step(NSEQ - 1, 1, True)
            sp.wait_ge(x1_ready, after_block(NBLK - 1))
            sp.dma_start(x1_v[NBLK], x1[1][:]).then_inc(x1_out, 16)
            sp.wait_ge(x1_out, 16 * (NBLK + 2))

        @block.gpsimd
        def _(pool):
            for s_, start in ((steps_ready, 2), (xw_ready, 2), (xd_ready, 2), (y_ready, 2), (g_ready, 2),
                              (ulo_done, 2), (rms_ready, 1), (rs_ready, 1)):
                pool.sem_inc(s_, start)
            pool.sem_inc(x1_out, 16)
            pool.sem_inc(ur_in[1], 16)
            for t, value in ((upto, 1.0), (after, 1.0), (ident, 0.0), (ones, 1.0), (c_eps, EPS), (c_inv, 1.0 / DI),
                             (c_mhalf, -0.5), (gb, 0.0), (yb, 0.0), (ur[1], 0.0), (x1[1], 0.0), (ss[1], 0.0),
                             (state, 0.0), (pre[0], 0.0)):
                nc.gpsimd.memset(t[:], value).then_inc(s_const, 1)
            NSET = 14
            pool.wait_ge(s_const, NSET)
            nc.gpsimd.affine_select(out=upto[:], in_=upto[:], compare_op=ALU.is_ge, fill=0.0, base=0,
                                    pattern=[[1, P]], channel_multiplier=-1).then_inc(s_const, 1)
            nc.gpsimd.affine_select(out=after[:], in_=after[:], compare_op=ALU.is_ge, fill=0.0, base=-1,
                                    pattern=[[-1, P]], channel_multiplier=1).then_inc(s_const, 1)
            nc.gpsimd.affine_select(out=ident[:], in_=ident[:], compare_op=ALU.not_equal, fill=1.0, base=0,
                                    pattern=[[-1, P]], channel_multiplier=1).then_inc(s_const, 1)
            pool.wait_ge(s_const, NSET + 3)
            pool.wait_ge(s_w, 16 * NW)

            def split_lo(n, par):
                pool.wait_ge(uhi_done, after_block(n))
                nc.gpsimd.tensor_tensor(u_lo[par][:], ut[par][:], u_hi[par][:].bitcast(F32),
                                        ALU.subtract).then_inc(ulo_done, 1)

            def make_steps(c, n, par, k):
                if k == 0:
                    pool.wait_ge(sp_chain, softplus(n))
                pool.wait_ge(seg_ps, after_chunk(c - 1))
                nc.gpsimd.tensor_tensor(
                    steps[:], upto[:].unsqueeze(1).broadcast_to([P, H, P]),
                    la[par][:, k * H:(k + 1) * H].unsqueeze(2).broadcast_to([P, H, P]), ALU.mult).then_inc(steps_ready, 1)

            def heads(t):
                return t[:].rearrange("p (h d) -> p h d", h=H)

            def per_head(t):
                return t.unsqueeze(2).broadcast_to([P, H, HD])

            def step(s, par, last):
                n = s * 2 + par
                for k in range(CH):
                    c = n * CH + k
                    if k == 0:
                        pool.wait_ge(dtw_ready, after_block(n))
                    pool.wait_ge(xs_ready, after_chunk(c))
                    pool.wait_ge(yd_ps, after_chunk(c - 1))
                    nc.gpsimd.tensor_tensor(heads(xdt), heads(xs), per_head(dt[par][:, k * H:(k + 1) * H]), ALU.mult)
                    nc.gpsimd.tensor_tensor(heads(xw), heads(xs), per_head(dtw[par][:, k * H:(k + 1) * H]),
                                            ALU.mult).then_inc(xw_ready, 1)
                    nc.gpsimd.tensor_tensor(heads(xd), heads(xs), per_head(rowb[:, 32:40]), ALU.mult).then_inc(xd_ready, 1)
                    if k < CH - 1:
                        make_steps(c + 1, n, par, k + 1)
                    elif not (last and par == 1):
                        make_steps(c + 1, n + 1, 1 - par, 0)
                    if k == 1:
                        pool.wait_ge(ss_ready, after_chunk(n * CH - 1))
                        nc.gpsimd.tensor_tensor(rms[:], ss[1 - par][:], c_inv[:], ALU.mult).then_inc(rms_chain, 1)
                        pool.wait_ge(rms_chain, n * 2 + 1)
                        nc.gpsimd.tensor_tensor(rms[:], rms[:], c_eps[:], ALU.add).then_inc(rms_chain, 1)
                        pool.wait_ge(rms_chain, n * 2 + 2)
                        nc.gpsimd.tensor_tensor(rms[:], rms[:], c_mhalf[:], ALU.pow).then_inc(rms_ready, 1)
                    if k == 2:
                        norm_scale(n)
                        if not last:
                            split_lo(n + 2, par)
                    pool.wait_ge(t2_done, after_chunk(c))
                    pool.wait_ge(xd_ready, after_chunk(c))
                    nc.gpsimd.tensor_tensor(yb[:], yb[:], xd[:], ALU.add).then_inc(y_ready, 1)
                    pool.wait_ge(gt_ps, after_chunk(c - 1))
                    pool.wait_ge(y_ready, after_chunk(c))
                    nc.gpsimd.tensor_tensor(gb[:], yb[:], zs[par][:, k, :], ALU.mult).then_inc(g_ready, 1)

            def norm_scale(n):
                pool.wait_ge(mv_ready, after_block(n - 1))
                nc.gpsimd.tensor_tensor(rs[:], mv[:, :, 1], c_eps[:], ALU.add).then_inc(rs_chain, 1)
                pool.wait_ge(rs_chain, n + 1)
                nc.gpsimd.tensor_tensor(rs[:], rs[:], c_mhalf[:], ALU.pow).then_inc(rs_ready, 1)

            split_lo(0, 0)
            split_lo(1, 1)
            make_steps(0, 0, 0, 0)
            with pool.Fori(0, NSEQ - 1) as s:
                step(s, 0, False)
                step(s, 1, False)
            step(NSEQ - 1, 0, True)
            step(NSEQ - 1, 1, True)
            n = NBLK
            pool.wait_ge(ss_ready, after_chunk(n * CH - 1))
            nc.gpsimd.tensor_tensor(rms[:], ss[1][:], c_inv[:], ALU.mult).then_inc(rms_chain, 1)
            pool.wait_ge(rms_chain, n * 2 + 1)
            nc.gpsimd.tensor_tensor(rms[:], rms[:], c_eps[:], ALU.add).then_inc(rms_chain, 1)
            pool.wait_ge(rms_chain, n * 2 + 2)
            nc.gpsimd.tensor_tensor(rms[:], rms[:], c_mhalf[:], ALU.pow).then_inc(rms_ready, 1)
            norm_scale(n)

        @block.scalar
        def _(act):
            for s_, start in ((ss_ready, 1), (ghi_done, 1), (out_ev, 1), (xs_ready, 2), (exp_done, 2),
                              (uhi_done, 2), (silu_done, 2), (dec_ready, 2), (sp_exp, 2), (sp_ln, 2)):
                act.sem_inc(s_, start)
            act.wait_ge(s_w, 16 * NW)
            nc.scalar.activation(expA[:], rowb[:, 0:24].rearrange("p (a h) -> p a h", a=3), ACT.Exp).then_inc(s_setup_a, 1)
            nc.scalar.copy(win_hi[:], win[:, :, 0:DTC]).then_inc(s_setup_a, 1)
            act.wait_ge(s_setup_v, 1)
            nc.scalar.copy(wo_hi[:], wo[:]).then_inc(s_setup_a, 1)
            act.wait_ge(s_const, 17)

            def split_hi(n, par, i):
                act.wait_ge(ut_in[par], 16 * (i + 1))
                nc.scalar.copy(u_hi[par][:], ut[par][:]).then_inc(uhi_done, 1)

            def evacuate(m, par, item):
                j = ORDER.index(item)
                b = ip_bank[j % 2]
                act.wait_ge(ip_ps, m * NI + j + 1)
                if item == "dt":
                    act.wait_ge(sp_chain, softplus(m - 1))
                    nc.scalar.copy(v_raw[:], b[:, 0:CH * H]).then_inc(ip_ev, 1)
                elif item == "cs":
                    nc.scalar.activation(dec[par][:], b[:, 0:3 * CH * H].rearrange("p (a c) -> p a c", a=3),
                                         ACT.Exp).then_inc(ip_ev, 1)
                elif isinstance(item, str):
                    nc.scalar.activation(zs[par][:, int(item[1]), :], b[:], ACT.Silu).then_inc(ip_ev, 1)
                else:
                    if item == 0:
                        if not (isinstance(m, int) and m == 0):
                            act.wait_ge(yo_ps, after_chunk(m * CH - CH - 1))
                    nc.scalar.copy(pre[par][:, item, TAPS - 1:], b[:])
                    nc.scalar.activation(xbc[par][:, item, :], b[:], ACT.Identity, bias=cb[:, item:item + 1],
                                         scale=cw[:, item, TAPS - 1:TAPS]).then_inc(ip_ev, 1)

            def softplus_exp(m):
                act.wait_ge(sp_chain, softplus(m, 2))
                nc.scalar.activation(v_e[:], v_neg[:], ACT.Exp).then_inc(sp_exp, 1)

            def softplus_ln(m):
                act.wait_ge(sp_chain, softplus(m, 3))
                nc.scalar.activation(v_l[:], v_w[:], ACT.Ln).then_inc(sp_ln, 1)

            def silu(m, par):
                act.wait_ge(taps_done, taps(m, CT - 1))
                nc.scalar.activation(xbc[par][:], xbc[par][:], ACT.Silu).then_inc(silu_done, 1)

            def square(c, par, k):
                act.wait_ge(y_ready, after_chunk(c))
                act.wait_ge(ss_ready, after_chunk(c - 1))
                nc.scalar.activation(sq[:], yb[:], ACT.Square, accum_out=ss[par][:, k:k + 1]).then_inc(ss_ready, 1)

            def g_high(c):
                act.wait_ge(gt_ps, after_chunk(c))
                act.wait_ge(out_ps, after_chunk(c - 1))
                nc.scalar.copy(g_hi[:].rearrange("p a b -> p (a b)"), yo_bank[:]).then_inc(ghi_done, 1)

            def take_out(c, par, k):
                act.wait_ge(out_ps, after_chunk(c))
                nc.scalar.copy(x1[par][:, k, :], out_bank).then_inc(out_ev, 1)

            def step(s, par, last):
                n = s * 2 + par
                more = not (last and par == 1)
                for k in range(CH):
                    c = n * CH + k
                    before = (par, k - 1) if k else (1 - par, CH - 1)
                    square(c - 1, *before)
                    act.wait_ge(xt_ps, after_chunk(c))
                    act.wait_ge(xd_ready, after_chunk(c - 1))
                    nc.scalar.copy(xs[:], xt_bank[:]).then_inc(xs_ready, 1)
                    g_high(c - 1)
                    act.wait_ge(seg_ps, after_chunk(c))
                    act.wait_ge(yd_ps, after_chunk(c - 1))
                    nc.scalar.activation(mt[:].rearrange("p h i -> p (h i)"), seg_bank[:], ACT.Exp).then_inc(exp_done, 1)
                    if more and k == 1:
                        softplus_exp(n + 1)
                    for half in range(2):
                        if more:
                            for item in ITEMS[k][half]:
                                evacuate(n + 1, 1 - par, item)
                    if more and k == 1:
                        softplus_ln(n + 1)
                    if k == 2 and not last:
                        split_hi(n + 2, par, s + 1)
                    if k == 1:
                        act.wait_ge(x1_out, 16 * (n + 1))
                    take_out(c - 1, *before)
                if more:
                    silu(n + 1, 1 - par)

            split_hi(0, 0, 0)
            split_hi(1, 1, 0)
            for item in ORDER[:NI]:
                if item == "cs":
                    softplus_exp(0)
                    softplus_ln(0)
                evacuate(0, 0, item)
            silu(0, 0)
            with act.Fori(0, NSEQ - 1) as s:
                step(s, 0, False)
                step(s, 1, False)
            step(NSEQ - 1, 0, True)
            step(NSEQ - 1, 1, True)
            c = NBLK * CH
            square(c - 1, 1, CH - 1)
            g_high(c - 1)
            take_out(c - 1, 1, CH - 1)

        @block.vector
        def _(dve):
            for s_, start in ((cbm_ready, 2), (mt_ready, 2), (y1_done, 2), (t2_done, 2), (st_scaled, 2), (st_ready, 2),
                              (glo_done, 1), (dtw_ready, 2), (sp_chain, 1), (res_done, 1), (stat_done, 1), (mv_ready, 1), (x1_ready, 1)):
                dve.sem_inc(s_, start)
            dve.wait_ge(s_w, 16 * NW)
            for k in range(OT):
                ins = nc.vector.tensor_scalar(wo[:, k, :], wo[:, k, :], nw[:, k:k + 1], None, ALU.mult)
            ins.then_inc(s_setup_v, 1)
            dve.wait_ge(s_setup_a, 1)
            nc.vector.tensor_tensor(sumA[:], expA[:, 0, :], expA[:, 1, :], ALU.add).then_inc(s_setup_v, 1)
            dve.wait_ge(s_setup_v, 2)
            nc.vector.tensor_tensor(negA[:], sumA[:], expA[:, 2, :], ALU.add).then_inc(s_setup_v, 1)
            dve.wait_ge(s_setup_v, 3)
            nc.vector.tensor_scalar(negA[:], negA[:], -1.0 / 3.0, None, ALU.mult).then_inc(s_setup_v, 1)
            dve.wait_ge(s_setup_a, 2)
            nc.vector.tensor_tensor(win_lo[:], win[:, :, 0:DTC], win_hi[:].bitcast(F32), ALU.subtract).then_inc(s_setup_v, 1)
            dve.wait_ge(s_setup_a, 3)
            nc.vector.tensor_tensor(wo_lo[:], wo[:], wo_hi[:].bitcast(F32), ALU.subtract).then_inc(s_setup_v, 1)
            dve.wait_ge(s_setup_v, 6)
            dve.wait_ge(s_const, 17)

            def by_head(row):
                return row.unsqueeze(1).broadcast_to([P, CH, H])

            def by_chunk(t):
                return t[:].rearrange("p (c h) -> p c h", c=CH)

            def convolve(s, m, par, tile):
                dve.wait_ge(ip_ev, m * NI + ORDER.index(tile) + 1)
                if par == 1:
                    nc.vector.tensor_copy(pre[1][:, tile, 0:TAPS - 1], pre[0][:, tile, T:T + TAPS - 1]).then_inc(halo_done, 1)
                    dve.wait_ge(halo_done, s * CT + tile + 1)
                for tap in range(TAPS - 1):
                    if tap:
                        dve.wait_ge(taps_done, taps(m, tile, tap))
                    nc.vector.scalar_tensor_tensor(out=xbc[par][:, tile, :], in0=pre[par][:, tile, tap:tap + T],
                                                   scalar=cw[:, tile, tap:tap + 1], in1=xbc[par][:, tile, :],
                                                   op0=ALU.mult, op1=ALU.add).then_inc(taps_done, 1)

            def softplus_a(m):
                dve.wait_ge(ip_ev, m * NI + ORDER.index("dt") + 1)
                nc.vector.tensor_tensor(by_chunk(v_dt), by_chunk(v_raw), by_head(rowb[:, 24:32]), ALU.add).then_inc(sp_chain, 1)
                dve.wait_ge(sp_chain, softplus(m, 1))
                nc.vector.scalar_tensor_tensor(out=v_neg[:], in0=v_dt[:], scalar=-1.0, in1=v_dt[:], op0=ALU.mult,
                                               op1=ALU.min).then_inc(sp_chain, 1)

            def softplus_b(m):
                dve.wait_ge(sp_exp, after_block(m))
                nc.vector.tensor_scalar(v_w[:], v_e[:], 1.0, None, ALU.add).then_inc(sp_chain, 1)
                dve.wait_ge(sp_chain, softplus(m, 3))
                nc.vector.tensor_scalar(v_d[:], v_w[:], -1.0, None, ALU.add).then_inc(sp_chain, 1)
                dve.wait_ge(sp_chain, softplus(m, 4))
                nc.vector.tensor_scalar(v_m[:], v_d[:], 0.0, None, ALU.is_equal).then_inc(sp_chain, 1)
                dve.wait_ge(sp_chain, softplus(m, 5))
                nc.vector.tensor_tensor(v_d[:], v_d[:], v_m[:], ALU.add).then_inc(sp_chain, 1)
                dve.wait_ge(sp_chain, softplus(m, 6))
                nc.vector.reciprocal(v_q[:], v_d[:]).then_inc(sp_chain, 1)
                nc.vector.tensor_tensor(v_p[:], v_e[:], v_m[:], ALU.mult).then_inc(sp_chain, 1)
                dve.wait_ge(sp_chain, softplus(m, 8))
                nc.vector.tensor_tensor(v_q[:], v_e[:], v_q[:], ALU.mult).then_inc(sp_chain, 1)

            def softplus_c(m, par):
                dve.wait_ge(sp_ln, after_block(m))
                dve.wait_ge(sp_chain, softplus(m, 9))
                nc.vector.tensor_tensor(v_q[:], v_l[:], v_q[:], ALU.mult).then_inc(sp_chain, 1)
                dve.wait_ge(sp_chain, softplus(m, 10))
                nc.vector.tensor_tensor(v_q[:], v_q[:], v_p[:], ALU.add).then_inc(sp_chain, 1)
                dve.wait_ge(sp_chain, softplus(m, 11))
                nc.vector.scalar_tensor_tensor(out=dt[par][:], in0=v_dt[:], scalar=0.0, in1=v_q[:], op0=ALU.max,
                                               op1=ALU.add).then_inc(sp_chain, 1)
                dve.wait_ge(sp_chain, softplus(m, 12))
                nc.vector.tensor_tensor(by_chunk(la[par]), by_chunk(dt[par]), by_head(negA[:]), ALU.mult).then_inc(sp_chain, 1)
                dve.wait_ge(sp_chain, softplus(m, 13))
                nc.vector.tensor_scalar(la[par][:], la[par][:], LOG_ZERO, None, ALU.max).then_inc(sp_chain, 1)

            def end_weights(m, par):
                dve.wait_ge(ip_ev, m * NI + ORDER.index("cs") + 1)
                nc.vector.tensor_tensor(dtw[par][:], dt[par][:], dec[par][:, 1, :], ALU.mult).then_inc(dtw_ready, 1)

            def g_low(c):
                dve.wait_ge(ghi_done, after_chunk(c))
                nc.vector.tensor_tensor(g_lo[:].rearrange("p a b -> p (a b)"), yo_bank[:],
                                        g_hi[:].rearrange("p a b -> p (a b)").bitcast(F32), ALU.subtract).then_inc(glo_done, 1)

            def residual(s, n, par):
                q = 1 - par
                dve.wait_ge(rms_ready, after_block(n - 1))
                dve.wait_ge(out_ev, after_chunk(n * CH - 1))
                dve.wait_ge(ur_in[q], 16 * (s + 1))
                for k in range(CH):
                    ins = nc.vector.scalar_tensor_tensor(out=x1[q][:, k, :], in0=x1[q][:, k, :], scalar=rms[:, k:k + 1],
                                                         in1=ur[q][:, k, :], op0=ALU.mult, op1=ALU.add)
                ins.then_inc(res_done, 1)
                dve.wait_ge(res_done, after_block(n - 1))
                for k in range(CH):
                    ins = nc.vector.bn_stats(stat[:, k, :], x1[q][:, k, :])
                ins.then_inc(stat_done, 1)
                dve.wait_ge(stat_done, after_block(n - 1))
                nc.vector.memset(tiny[:], 0.0)
                for k in range(CH):
                    ins = nc.vector.bn_aggr(mv[:, k, :], stat[:, k, :])
                ins.then_inc(mv_ready, 1)

            def normalise(n, par):
                q = 1 - par
                dve.wait_ge(rs_ready, after_block(n - 1))
                for k in range(CH):
                    ins = nc.vector.tensor_scalar(x1[q][:, k, :], x1[q][:, k, :], mv[:, k, 0:1], rs[:, k:k + 1],
                                                  ALU.subtract, ALU.mult)
                ins.then_inc(x1_ready, 1)

            def heads(t):
                return t[:].rearrange("p (h d) -> p h d", h=H)

            def per_head(t):
                return t.unsqueeze(2).broadcast_to([P, H, HD])

            def step(s, par, last):
                n = s * 2 + par
                m = n + 1
                more = not (last and par == 1)
                for k in range(CH):
                    c = n * CH + k
                    hk = slice(k * H, (k + 1) * H)
                    dve.wait_ge(cb_ps, after_chunk(c))
                    nc.vector.tensor_tensor(cbm[:], cb_bank[:, 0:P], upto[:], ALU.mult)
                    dve.wait_ge(st_ready, after_chunk(c - 1))
                    nc.vector.tensor_copy(b_tok[:], cb_bank[:, P:2 * P]).then_inc(cbm_ready, 1)
                    g_low(c - 1)
                    dve.wait_ge(exp_done, after_chunk(c))
                    dve.wait_ge(cbm_ready, after_chunk(c))
                    nc.vector.tensor_tensor(mt[:], mt[:], cbm[:].unsqueeze(1).broadcast_to([P, H, P]), ALU.mult).then_inc(mt_ready, 1)
                    dve.wait_ge(yo_ps, after_chunk(c))
                    dve.wait_ge(g_ready, after_chunk(c - 1))
                    dve.wait_ge(ss_ready, after_chunk(c - 1))
                    if par == 0 and k == 0:
                        nc.vector.memset(yb[:], 0.0).then_inc(y1_done, 1)
                        nc.vector.memset(state[:], 0.0).then_inc(st_scaled, 1)
                    else:
                        nc.vector.tensor_tensor(heads(yb), heads(yo_bank), per_head(dec[par][:, 0, hk]), ALU.mult).then_inc(y1_done, 1)
                        nc.vector.tensor_tensor(heads(state), heads(state), per_head(dec[par][:, 2, hk]), ALU.mult).then_inc(st_scaled, 1)
                    dve.wait_ge(ds_ps, after_chunk(c))
                    dve.wait_ge(st_scaled, after_chunk(c))
                    nc.vector.tensor_tensor(state[:], xt_bank[:], state[:], ALU.add).then_inc(st_ready, 1)
                    dve.wait_ge(yd_ps, after_chunk(c))
                    dve.wait_ge(y1_done, after_chunk(c))
                    nc.vector.tensor_tensor(yb[:], yd_bank[:], yb[:], ALU.add).then_inc(t2_done, 1)
                    if more:
                        if k == 0:
                            softplus_a(m)
                        if k == 1:
                            softplus_b(m)
                        for half in range(2):
                            for item in ITEMS[k][half]:
                                if isinstance(item, int):
                                    convolve(s + par, m, 1 - par, item)
                        if k == 1:
                            softplus_c(m, 1 - par)
                        if k == 2:
                            end_weights(m, 1 - par)
                    if k == 1:
                        residual(s, n, par)
                    if k == 3:
                        normalise(n, par)

            softplus_a(0)
            softplus_b(0)
            for tile in range(CT):
                convolve(0, 0, 0, tile)
            softplus_c(0, 0)
            end_weights(0, 0)
            with dve.Fori(0, NSEQ - 1) as s:
                step(s, 0, False)
                step(s, 1, False)
            step(NSEQ - 1, 0, True)
            step(NSEQ - 1, 1, True)
            g_low(NBLK * CH - 1)
            residual(NSEQ, NBLK, 0)
            normalise(NBLK, 0)

        @block.tensor
        def _(pe):
            for s_, start in ((cb_ps, 2), (xt_ps, 2), (seg_ps, 2), (yo_ps, 2), (ds_ps, 2), (yd_ps, 2), (gt_ps, 1), (out_ps, 1)):
                pe.sem_inc(s_, start)
            pe.wait_ge(s_w, 16 * NW)
            pe.wait_ge(s_const, 17)
            pe.wait_ge(s_setup_v, 6)
            PASSES = ((0, 0), (0, 1), (1, 0))
            w_parts = (win_hi, win_lo)

            def project(m, par, item):
                j = ORDER.index(item)
                b = ip_bank[j % 2]
                u_parts = (u_hi[par], u_lo[par])
                if j == 0:
                    pe.wait_ge(ulo_done, after_block(m))
                if not (isinstance(m, int) and m == 0 and j < 2):
                    pe.wait_ge(ip_ev, m * NI + j - 1)
                if item == "dt":
                    for q in range(CH):
                        for k in range(KT):
                            ins = pe.matmul(b[:, q * H:(q + 1) * H], ut[par][:, k, q * P:(q + 1) * P],
                                            win[:, k, DTC:DTC + H], start=(k == 0), stop=(k == KT - 1))
                elif item == "cs":
                    pe.wait_ge(sp_chain, softplus(m))
                    for i, mask in enumerate((upto, after, ones)):
                        ins = pe.matmul(b[:, i * CH * H:(i + 1) * CH * H], mask[:], la[par][:], start=True, stop=True)
                else:
                    for k in range(KT):
                        for a, w in PASSES:
                            if isinstance(item, str):
                                q = int(item[1])
                                lhs, rhs = u_parts[a][:, k, q * P:(q + 1) * P], w_parts[w][:, k, 0:DI]
                            else:
                                lhs = w_parts[w][:, k, DI + item * P:DI + (item + 1) * P]
                                rhs = u_parts[a][:, k, :]
                            ins = pe.matmul(b[:], lhs, rhs, start=(k == 0 and a + w == 0), stop=(k == KT - 1 and a == 1))
                ins.then_inc(ip_ps, 1)

            def g_transposes(c):
                pe.wait_ge(g_ready, after_chunk(c))
                for q in range(OT):
                    ins = pe.transpose(yo_bank[:, q * P:(q + 1) * P], gb[:, q * P:(q + 1) * P], ident[:])
                ins.then_inc(gt_ps, 1)

            def out_project(c):
                for k in range(OT):
                    for a, w in PASSES:
                        ins = pe.matmul(out_bank, (g_hi, g_lo)[a][:, k, :], (wo_hi, wo_lo)[w][:, k, :],
                                        start=(k == 0 and a + w == 0), stop=(k == OT - 1 and a == 1))
                ins.then_inc(out_ps, 1)

            def step(s, par, last):
                n = s * 2 + par
                more = not (last and par == 1)
                for k in range(CH):
                    c = n * CH + k
                    tok = slice(k * P, (k + 1) * P)
                    if k == 0:
                        pe.wait_ge(silu_done, after_block(n))
                    pe.wait_ge(cbm_ready, after_chunk(c - 1))
                    pe.matmul(cb_bank[:, 0:P], xbc[par][:, TB, tok], xbc[par][:, TC, tok], start=True, stop=True)
                    pe.transpose(cb_bank[:, P:2 * P], xbc[par][:, TB, tok], ident[:]).then_inc(cb_ps, 1)
                    pe.wait_ge(st_ready, after_chunk(c - 1))
                    for q in range(OT):
                        ins = pe.transpose(xt_bank[:, q * P:(q + 1) * P], xbc[par][:, q, tok], ident[:])
                    ins.then_inc(xt_ps, 1)
                    pe.wait_ge(steps_ready, after_chunk(c))
                    pe.matmul(seg_bank[:, 512:1024], after[:], steps[:, 4:8, :].rearrange("p h i -> p (h i)"), start=True, stop=True)
                    pe.wait_ge(out_ev, after_chunk(c - 2))
                    pe.matmul(seg_bank[:, 0:512], after[:], steps[:, 0:4, :].rearrange("p h i -> p (h i)"),
                              start=True, stop=True).then_inc(seg_ps, 1)
                    g_transposes(c - 1)
                    if more:
                        for item in ITEMS[k][0]:
                            project(n + 1, 1 - par, item)
                    pe.wait_ge(glo_done, after_chunk(c - 1))
                    pe.matmul(yo_bank[:], xbc[par][:, TC, tok], state[:], start=True, stop=True).then_inc(yo_ps, 1)
                    pe.wait_ge(xw_ready, after_chunk(c))
                    pe.wait_ge(cbm_ready, after_chunk(c))
                    pe.matmul(xt_bank[:], b_tok[:], xw[:], start=True, stop=True).then_inc(ds_ps, 1)
                    pe.wait_ge(mt_ready, after_chunk(c))
                    for h in range(H):
                        ins = pe.matmul(yd_bank[:, h * HD:(h + 1) * HD], mt[:, h, :], xdt[:, h * HD:(h + 1) * HD],
                                        start=True, stop=True)
                    ins.then_inc(yd_ps, 1)
                    if more:
                        for item in ITEMS[k][1]:
                            project(n + 1, 1 - par, item)
                    out_project(c - 1)

            for item in ORDER:
                project(0, 0, item)
            with pe.Fori(0, NSEQ - 1) as s:
                step(s, 0, False)
                step(s, 1, False)
            step(NSEQ - 1, 0, True)
            step(NSEQ - 1, 1, True)
            c = NBLK * CH
            g_transposes(c - 1)
            pe.wait_ge(glo_done, after_chunk(c - 1))
            out_project(c - 1)


def route(nc, x1_dram, xg, gate, rows, picks):
    slot_a, slot_b, w_a, w_b, eid, eid_f = picks
    D, E = gate.shape
    KT = D // P
    TOK = (x1_dram.shape[0] - 1) * 512
    T = 512
    CH = T // P
    NBLK = TOK // T
    NC = TOK // P
    NS = TOK // TILE
    NR = routed_tiles(TOK, E)
    MAXT = TOK // TILE
    BIG = float(1 << 14)
    assert TOP == 2 and NR * TILE < BIG

    with ExitStack() as ctx:
        def sb(name, shape, dt=F32):
            return ctx.enter_context(nc.sbuf_tensor(name, shape, dt))

        def sem(name):
            return ctx.enter_context(nc.semaphore(name))

        xk = [sb(f"xk{i}", [P, CH, D + 2]) for i in range(2)]
        x_hi = [sb(f"r_x_hi{i}", [P, KT, T], F32R) for i in range(2)]
        x_lo = [sb(f"r_x_lo{i}", [P, KT, T], F32R) for i in range(2)]
        gate_f = sb("gate_f", [P, KT, E])
        gate_hi = sb("gate_hi", [P, KT, E], F32R)
        gate_lo = sb("gate_lo", [P, KT, E], F32R)
        gate_b = sb("gate_b", [P, 48])
        spare = sb("spare", [P, 2, D + 2])
        ident = sb("r_ident", [P, P])
        lower = sb("r_lower", [P, P])
        ones = sb("r_ones", [P, P])
        before = sb("before", [P, E, E])
        fills = sb("fills", [P, MAXT])
        tile_ids = sb("tile_ids", [P, NR])
        mx, sm, rc, mn, sb_f, wt = (sb("r_" + n, [P, NC]) for n in ("mx", "sm", "rc", "mn", "sb", "wt"))
        sh, es, sc, bi, rank, sel, cum0, cum1, slot, m, in_a, in_b, prod = (
            sb("r_" + n, [P, NC, E]) for n in ("sh", "es", "sc", "bi", "rank", "sel", "cum0", "cum1", "slot", "m", "in_a", "in_b", "prod"))
        above = sb("above", [P, NC, E, E])
        equal = sb("equal", [P, NC, E, E])
        full = sb("full", [P, E, MAXT])
        ntiles, base, ends = (sb("r_" + n, [P, E]) for n in ("ntiles", "base", "ends"))
        base_p = sb("base_p", [P, E, E])
        last = sb("last", [P, NR])
        past = sb("past", [P, NR, E])

        xt_bank = [[ctx.enter_context(nc.psum_tensor(f"r_xt{i}{k}", [P, T], F32)) for k in range(KT)] for i in range(2)]
        lg_bank = ctx.enter_context(nc.psum_tensor("lg_bank", [P, NC, E], F32))
        cnt_bank = ctx.enter_context(nc.psum_tensor("cnt_bank", [P, 2, NC, E], F32))

        s_w, s_const, s_set_a, s_set_v = sem("r_w"), sem("r_const"), sem("r_set_a"), sem("r_set_v")
        x_in = [sem("r_x_in0"), sem("r_x_in1")]
        xt_ps, hi_done, lo_done, rt_ps, xg_out = sem("r_xt_ps"), sem("r_hi"), sem("r_lo"), sem("r_ps"), sem("xg_out")
        xg_done, ids_set = [sem("xg_done0"), sem("xg_done1")], sem("ids_set")
        passed = sem("r_passed")
        chain, exp_done, cnt_ps = sem("r_chain"), sem("r_exp"), sem("cnt_ps")
        NCONST = 15

        x_v = x1_dram.rearrange("b (c p) d -> b p c d", p=P)
        xg_v = xg[0:TOK, :].rearrange("(b c p) d -> b p c d", p=P, c=CH)
        block = ctx.enter_context(nc.Block())

        @block.sync
        def _(sp):
            for dst, src in ((gate_f, gate.rearrange("(k p) e -> p k e", p=P)), (gate_b, rows.partition_broadcast(P))):
                sp.dma_start(dst[:], src).then_inc(s_w, 16)

            def load(b, par):
                sp.dma_start(xk[par][:, :, 0:D], x_v[b + 1]).then_inc(x_in[par], 16)

            load(0, 0)
            load(1, 1)
            sp.wait_ge(s_const, NCONST)
            empty = xg[TOK:, :].rearrange("(t h p) d -> h p t d", p=P, h=2)
            for h in range(2):
                sp.dma_start(empty[h], spare[:, h, :].unsqueeze(1).broadcast_to([P, NR, D + 2])).then_inc(xg_out, 16)

            def copy_out(b, par, s):
                sp.wait_ge(x_in[par], (s + 1) * 16)
                sp.sem_inc(passed, 1)
                sp.wait_ge(ids_set, b + 1)
                sp.dma_start(xg_v[b], xk[par][:]).then_inc(xg_done[par], 16)

            with sp.Fori(0, NBLK // 2 - 1) as s:
                for par in range(2):
                    b = s * 2 + par
                    copy_out(b, par, s)
                    sp.wait_ge(xt_ps, b + 1)
                    sp.sem_inc(passed, 1)
                    sp.wait_ge(xg_done[par], (s + 1) * 16)
                    load(b + 2, par)
            for b in (NBLK - 2, NBLK - 1):
                copy_out(b, b % 2, NBLK // 2 - 1)
            for par in range(2):
                sp.wait_ge(xg_done[par], NBLK // 2 * 16)
            sp.wait_ge(xg_out, 16 * 2)

        @block.gpsimd
        def _(pool):
            for t, value in ((ident[:], 0.0), (lower[:], 1.0), (ones[:], 1.0), (before[:], 1.0), (spare[:], 0.0),
                             (xk[0][:, :, D + 1], 1.0), (xk[1][:, :, D + 1], 1.0), (eid[:, 0:NS], E), (eid_f[:, 0:NS], float(E))):
                nc.gpsimd.memset(t, value).then_inc(s_const, 1)
            nc.gpsimd.iota(fills[:], [[TILE, MAXT]], 0, 0, allow_small_or_imprecise_dtypes=True).then_inc(s_const, 1)
            nc.gpsimd.iota(tile_ids[:], [[1, NR]], 0, 0, allow_small_or_imprecise_dtypes=True).then_inc(s_const, 1)
            pool.wait_ge(s_const, 11)
            nc.gpsimd.affine_select(out=ident[:], in_=ident[:], compare_op=ALU.not_equal, fill=1.0, base=0,
                                    pattern=[[-1, P]], channel_multiplier=1).then_inc(s_const, 1)
            nc.gpsimd.affine_select(out=lower[:], in_=lower[:], compare_op=ALU.is_ge, fill=0.0, base=-1,
                                    pattern=[[1, P]], channel_multiplier=-1).then_inc(s_const, 1)
            nc.gpsimd.affine_select(out=before[:], in_=before[:], compare_op=ALU.is_ge, fill=0.0, base=-1,
                                    pattern=[[1, E], [-1, E]], channel_multiplier=0).then_inc(s_const, 1)
            nc.gpsimd.iota(spare[:, :, D:D + 1].bitcast(I32), [[P, 2], [1, 1]], 0, 1).then_inc(s_const, 1)
            for b in range(NBLK):
                if b >= 2:
                    pool.wait_ge(xg_done[b % 2], b // 2 * 16)
                nc.gpsimd.iota(xk[b % 2][:, :, D:D + 1].bitcast(I32), [[P, CH], [1, 1]], T * (b + 1), 1).then_inc(ids_set, 1)

        @block.scalar
        def _(act):
            act.wait_ge(s_w, 32)
            nc.scalar.copy(gate_hi[:], gate_f[:]).then_inc(s_set_a, 1)
            act.sem_inc(hi_done, 2)

            def high(b, par):
                act.wait_ge(xt_ps, b + 1)
                act.wait_ge(rt_ps, b + 1)
                for k in range(KT):
                    ins = nc.scalar.copy(x_hi[par][:, k, :], xt_bank[par][k][:])
                ins.then_inc(hi_done, 1)

            with act.Fori(0, NBLK // 2) as s:
                high(s * 2, 0)
                high(s * 2 + 1, 1)
            act.wait_ge(chain, 2)
            nc.scalar.activation(es[:], sh[:], ACT.Exp).then_inc(exp_done, 1)

        @block.vector
        def _(dve):
            dve.wait_ge(s_set_a, 1)
            nc.vector.tensor_tensor(gate_lo[:], gate_f[:], gate_hi[:].bitcast(F32), ALU.subtract).then_inc(s_set_v, 1)
            dve.sem_inc(lo_done, 2)

            def low(b, par):
                dve.wait_ge(hi_done, b + 3)
                for k in range(KT):
                    ins = nc.vector.tensor_tensor(x_lo[par][:, k, :], xt_bank[par][k][:], x_hi[par][:, k, :].bitcast(F32), ALU.subtract)
                ins.then_inc(lo_done, 1)

            with dve.Fori(0, NBLK // 2) as s:
                low(s * 2, 0)
                low(s * 2 + 1, 1)

            def over_e(t):
                return t[:].unsqueeze(2).broadcast_to([P, NC, E])

            dve.wait_ge(rt_ps, NBLK + 2)
            dve.wait_ge(s_const, NCONST)
            nc.vector.tensor_reduce(mx[:], lg_bank[:], AX.X, ALU.max).then_inc(chain, 1)
            dve.wait_ge(chain, 1)
            nc.vector.tensor_tensor(sh[:], lg_bank[:], over_e(mx), ALU.subtract).then_inc(chain, 1)
            dve.wait_ge(exp_done, 1)
            nc.vector.tensor_reduce(sm[:], es[:], AX.X, ALU.add).then_inc(chain, 1)
            dve.wait_ge(chain, 3)
            nc.vector.reciprocal(rc[:], sm[:]).then_inc(chain, 1)
            dve.wait_ge(chain, 4)
            nc.vector.tensor_tensor(sc[:], es[:], over_e(rc), ALU.mult).then_inc(chain, 1)
            dve.wait_ge(chain, 5)
            nc.vector.tensor_tensor(bi[:], sc[:], gate_b[:, 40:48].unsqueeze(1).broadcast_to([P, NC, E]), ALU.add).then_inc(chain, 1)
            dve.wait_ge(chain, 6)
            mine = bi[:].unsqueeze(3).broadcast_to([P, NC, E, E])
            other = bi[:].unsqueeze(2).broadcast_to([P, NC, E, E])
            nc.vector.tensor_tensor(above[:], other, mine, ALU.is_gt).then_inc(chain, 1)
            nc.vector.tensor_tensor(equal[:], other, mine, ALU.is_equal).then_inc(chain, 1)
            dve.wait_ge(chain, 8)
            nc.vector.tensor_tensor(equal[:], equal[:], before[:].unsqueeze(1).broadcast_to([P, NC, E, E]), ALU.mult).then_inc(chain, 1)
            dve.wait_ge(chain, 9)
            nc.vector.tensor_tensor(above[:], above[:], equal[:], ALU.add).then_inc(chain, 1)
            dve.wait_ge(chain, 10)
            nc.vector.tensor_reduce(rank[:], above[:], AX.X, ALU.add).then_inc(chain, 1)
            dve.wait_ge(chain, 11)
            nc.vector.tensor_scalar(sel[:], rank[:], float(TOP), None, ALU.is_lt).then_inc(chain, 1)
            dve.wait_ge(cnt_ps, 1)
            pos, total = cnt_bank[:, 0], cnt_bank[:, 1]
            nc.vector.tensor_copy(cum0[:], total).then_inc(chain, 1)
            dve.wait_ge(chain, 13)
            cums, step = (cum0, cum1), 1
            for i in range(5):
                a, b = cums[i % 2], cums[1 - i % 2]
                nc.vector.tensor_copy(b[:, 0:step], a[:, 0:step])
                nc.vector.tensor_tensor(b[:, step:], a[:, step:], a[:, 0:NC - step], ALU.add).then_inc(chain, 1)
                dve.wait_ge(chain, 14 + i)
                step *= 2
            cum, free = cums[1], cums[0]
            assert step == NC
            nc.vector.tensor_tensor(full[:], cum[:, NC - 1].unsqueeze(2).broadcast_to([P, E, MAXT]),
                                    fills[:].unsqueeze(1).broadcast_to([P, E, MAXT]), ALU.is_gt).then_inc(chain, 1)
            nc.vector.tensor_tensor(free[:], cum[:], total, ALU.subtract).then_inc(chain, 1)
            dve.wait_ge(chain, 20)
            nc.vector.tensor_reduce(ntiles[:], full[:], AX.X, ALU.add).then_inc(chain, 1)
            nc.vector.tensor_tensor(prod[:], free[:], pos, ALU.add).then_inc(chain, 1)
            dve.wait_ge(chain, 22)
            nc.vector.tensor_tensor(base_p[:], ntiles[:].unsqueeze(1).broadcast_to([P, E, E]), before[:], ALU.mult).then_inc(chain, 1)
            dve.wait_ge(chain, 23)
            nc.vector.tensor_reduce(base[:], base_p[:], AX.X, ALU.add).then_inc(chain, 1)
            dve.wait_ge(chain, 24)
            nc.vector.scalar_tensor_tensor(out=slot[:], in0=base[:].unsqueeze(1).broadcast_to([P, NC, E]), scalar=float(TILE),
                                           in1=prod[:], op0=ALU.mult, op1=ALU.add).then_inc(chain, 1)
            nc.vector.tensor_tensor(ends[:], base[:], ntiles[:], ALU.add).then_inc(chain, 1)
            dve.wait_ge(chain, 26)
            nc.vector.tensor_tensor(past[:], tile_ids[:].unsqueeze(2).broadcast_to([P, NR, E]),
                                    ends[:].unsqueeze(1).broadcast_to([P, NR, E]), ALU.is_ge).then_inc(chain, 1)
            nc.vector.scalar_tensor_tensor(out=m[:], in0=slot[:], scalar=BIG, in1=sel[:], op0=ALU.subtract, op1=ALU.mult).then_inc(chain, 1)
            dve.wait_ge(chain, 28)
            nc.vector.tensor_reduce(last[:], past[:], AX.X, ALU.add).then_inc(chain, 1)
            nc.vector.tensor_reduce(mn[:], m[:], AX.X, ALU.min).then_inc(chain, 1)
            dve.wait_ge(chain, 30)
            nc.vector.tensor_scalar(eid[:, NS:NS + NR], last[:], float(E - 1), None, ALU.min)
            nc.vector.tensor_scalar(eid_f[:, NS:NS + NR], last[:], float(E - 1), None, ALU.min).then_inc(chain, 1)
            nc.vector.tensor_scalar(slot_a[:], mn[:], BIG + TOK, None, ALU.add).then_inc(chain, 1)
            nc.vector.tensor_tensor(in_a[:], m[:], over_e(mn), ALU.is_equal).then_inc(chain, 1)
            dve.wait_ge(chain, 33)
            nc.vector.tensor_tensor(in_b[:], sel[:], in_a[:], ALU.subtract).then_inc(chain, 1)
            nc.vector.tensor_tensor(prod[:], sc[:], in_a[:], ALU.mult).then_inc(chain, 1)
            dve.wait_ge(chain, 35)
            nc.vector.tensor_reduce(w_a[:], prod[:], AX.X, ALU.add).then_inc(chain, 1)
            nc.vector.tensor_tensor(slot[:], slot[:], in_b[:], ALU.mult).then_inc(chain, 1)
            dve.wait_ge(chain, 37)
            nc.vector.tensor_tensor(prod[:], sc[:], in_b[:], ALU.mult).then_inc(chain, 1)
            nc.vector.tensor_reduce(sb_f[:], slot[:], AX.X, ALU.add).then_inc(chain, 1)
            dve.wait_ge(chain, 39)
            nc.vector.tensor_reduce(w_b[:], prod[:], AX.X, ALU.add).then_inc(chain, 1)
            nc.vector.tensor_scalar(slot_b[:], sb_f[:], float(TOK), None, ALU.add).then_inc(chain, 1)

        @block.tensor
        def _(pe):
            pe.sem_inc(rt_ps, 2)
            pe.wait_ge(s_const, NCONST)
            pe.wait_ge(s_set_v, 1)
            x_parts, gate_parts = (x_hi, x_lo), (gate_hi, gate_lo)

            def transposes(b, par, s):
                pe.wait_ge(x_in[par], (s + 1) * 16)
                pe.wait_ge(lo_done, b + 1)
                for k in range(KT):
                    for c in range(CH):
                        ins = pe.transpose(xt_bank[par][k][:, c * P:(c + 1) * P],
                                           xk[par][:, c, k * P:(k + 1) * P], ident[:])
                ins.then_inc(xt_ps, 1)

            def logits(b, par):
                pe.wait_ge(lo_done, b + 3)
                for c in range(CH):
                    for k in range(KT):
                        for a, w in PASSES:
                            ins = pe.matmul(lg_bank[:, bass.ds(b * CH + c, 1), :].rearrange("p o e -> p (o e)"),
                                            x_parts[a][par][:, k, c * P:(c + 1) * P], gate_parts[w][:, k, :],
                                            start=(k == 0 and a + w == 0), stop=(k == KT - 1 and a == 1))
                ins.then_inc(rt_ps, 1)

            transposes(0, 0, 0)
            with pe.Fori(0, NBLK // 2 - 1) as s:
                transposes(s * 2 + 1, 1, s)
                logits(s * 2, 0)
                transposes(s * 2 + 2, 0, s + 1)
                logits(s * 2 + 1, 1)
            transposes(NBLK - 1, 1, NBLK // 2 - 1)
            logits(NBLK - 2, 0)
            logits(NBLK - 1, 1)
            pe.wait_ge(chain, 12)
            flat = sel[:].rearrange("p c e -> p (c e)")
            for i, mask in enumerate((lower, ones)):
                ins = pe.matmul(cnt_bank[:, i].rearrange("p c e -> p (c e)"), mask[:], flat, start=True, stop=True)
            ins.then_inc(cnt_ps, 1)


def split_weights(nc, wts, w1, w3, w2):
    w13_hi, w13_lo, w2_hi, w2_lo = wts
    NE = w13_hi.shape[3]
    HD = w13_hi.shape[4]
    HT = w2_hi.shape[1] // NE
    with ExitStack() as ctx:
        loaded = [ctx.enter_context(nc.semaphore(f"w_loaded{i}")) for i in range(NE)]
        high_done = ctx.enter_context(nc.semaphore("high_done"))
        low_done = ctx.enter_context(nc.semaphore("low_done"))
        block = ctx.enter_context(nc.Block())
        order = [NE - 1] + list(range(NE - 1))

        def rows2(t, e):
            return t[:, e * HT:(e + 1) * HT, :]

        @block.sync
        def _(sp):
            for e in order:
                for i, w in enumerate((w1, w3)):
                    sp.dma_start(w13_lo[:, i, :, e, :].bitcast(F32),
                                 w.rearrange("(k p) (e c) -> p k e c", p=P, c=HD)[:, :, e, :]).then_inc(loaded[e], 16)
                sp.dma_start(rows2(w2_lo, e).bitcast(F32), rows2(w2, e)).then_inc(loaded[e], 16)

        @block.scalar
        def _(act):
            for e in order:
                act.wait_ge(loaded[e], 48)
                for i in range(2):
                    nc.scalar.copy(w13_hi[:, i, :, e, :], w13_lo[:, i, :, e, :].bitcast(F32)).then_inc(high_done, 1)
                nc.scalar.copy(rows2(w2_hi, e), rows2(w2_lo, e).bitcast(F32)).then_inc(high_done, 1)

        @block.vector
        def _(dve):
            for n, e in enumerate(order):
                for i in range(2):
                    dve.wait_ge(high_done, 3 * n + i + 1)
                    nc.vector.tensor_tensor(w13_lo[:, i, :, e, :], w13_lo[:, i, :, e, :].bitcast(F32),
                                            w13_hi[:, i, :, e, :].bitcast(F32), ALU.subtract).then_inc(low_done, 1)
                dve.wait_ge(high_done, 3 * n + 3)
                nc.vector.tensor_tensor(rows2(w2_lo, e), rows2(w2_lo, e).bitcast(F32),
                                        rows2(w2_hi, e).bitcast(F32), ALU.subtract).then_inc(low_done, 1)


def experts(nc, wts, picks, xg, acc, biases):
    w13_hi, w13_lo, w2_hi, w2_lo = wts
    slot_a, slot_b, w_a, w_b, eid, eid_f = picks
    KT = w13_hi.shape[2]
    NE = w13_hi.shape[3]
    HD = w13_hi.shape[4]
    HT = w2_hi.shape[1] // NE
    D = w2_hi.shape[2]
    TOK = acc.shape[0] - 512
    NT = xg.shape[0] // TILE
    NS = TOK // TILE
    HV = TILE // P
    U = 4
    SG = 8
    NSTEP = NS // U
    HEAD = 4
    LO = 64
    assert TOK // P == SG * NSTEP and NT % U == U - 1

    with ExitStack() as ctx:
        def sb(name, shape, dt=F32):
            return ctx.enter_context(nc.sbuf_tensor(name, shape, dt))

        def bank(name, cols=512):
            return ctx.enter_context(nc.psum_tensor(name, [P, cols], F32))

        def sem(name):
            return ctx.enter_context(nc.semaphore(name))

        ident = sb("ident2", [P, P])
        xin = [sb(f"xin{i}", [P, HV, D + 2]) for i in range(2)]
        x_hi = [sb(f"x_hi{i}", [P, KT, TILE], F32R) for i in range(2)]
        x_lo = [sb(f"x_lo{i}", [P, KT, TILE], F32R) for i in range(2)]
        dest = [sb(f"dest{i}", [P, HV], I32) for i in range(U)]
        wgt = [sb(f"wgt{i}", [P, HV]) for i in range(U)]
        pick = [sb(f"pick{i}", [P, P], F32R) for i in range(U)]
        row_no = sb("row_no", [P, 1])
        is_hi = sb("is_hi", [P, 1])
        is_lo = sb("is_lo", [P, 1])
        bias = sb("bias", [P, 2 * HD + D], F32R)
        g = [sb(f"g{i}", [P, HV, HT * P]) for i in range(2)]
        h_hi = sb("h_hi", [P, HT, TILE], F32R)
        h_lo = sb("h_lo", [P, HT, TILE], F32R)
        y_sb = [sb(f"y_sb{i}", [P, HV, D]) for i in range(2)]
        xrow = sb("xrow", [P, SG, D + 2])
        idx_a = sb("idx_a", [P, SG], I32)
        idx_b = sb("idx_b", [P, SG], I32)
        NB = 2 * HD + D
        bias_f = xrow[:].rearrange("p c d -> p (c d)")[:, 0:NB]

        xt_bank = bank("e_xt")
        h_bank = [[bank(f"h_bank{h}_{n}") for n in (1, 3)] for h in range(HV)]
        ht_bank = bank("ht_bank", 1024)
        y_bank = bank("y_bank")

        s_const, s_bias, s_split, s_fix = sem("e_const"), sem("e_bias"), sem("e_split"), sem("e_fix")
        x_in = [sem("e_x_in0"), sem("e_x_in1")]
        xt_ps, xhi_done, xlo_done = sem("e_xt_ps"), sem("xhi_done"), sem("xlo_done")
        h1_ps, h1_out = sem("h1_ps"), sem("h1_out")
        h_ps, g_done, silu_done, ht_ps = sem("h_ps"), sem("g_done"), sem("e_silu"), sem("ht_ps")
        hi_done, lo_done, y_ps, y_ready = sem("e_hi"), sem("e_lo"), sem("y_ps"), sem("e_y_ready")
        added, row_in, set_done, scattered = sem("added"), sem("row_in"), sem("set_done"), sem("scattered")
        gone = sem("gone")
        passed = sem("e_passed")
        NCONST = 10

        def after(t):
            return t + 1 + HEAD

        def part(t, h):
            return (t + HEAD) * HV + h + 1

        def loads(s, j):
            return (s * (U // 2) + j // 2 + 1) * 16

        def pipeline(eng, prepare, hidden, close, turn):
            prepare(0, 0)
            prepare(0, 1)
            hidden(0, 0)
            turn(0, 0)
            with eng.Fori(0, NT // U) as s:
                for j in range(1, U + 1):
                    prepare(s, j + 1)
                    hidden(s, j)
                    close(s, j - 1)
                    turn(s, j)
            s = NT // U
            prepare(s, 2)
            hidden(s, 1)
            close(s, 0)
            turn(s, 1)
            hidden(s, 2)
            close(s, 1)
            turn(s, 2)
            close(s, 2)

        xg_v = xg.rearrange("(t h p) d -> t p h d", p=P, h=HV)
        block = ctx.enter_context(nc.Block())

        @block.sync
        def _(sp):
            def x_load(t, j):
                sp.dma_start(xin[j % 2][:], xg_v[t]).then_inc(x_in[j % 2], 16)

            def next_load(t, j):
                sp.wait_ge(xlo_done, after(t))
                x_load(t + 2, j)

            sp.wait_ge(s_const, NCONST)
            for row in (0, LO):
                sp.dma_start(bias_f[row:row + NE, :], biases).then_inc(s_bias, 16)
            x_load(0, 0)
            x_load(1, 1)
            with sp.Fori(0, NSTEP - 1) as s:
                for j in range(U):
                    next_load(s * U + j, j)
            next_load(NS - 4, 0)
            next_load(NS - 3, 1)
            sp.wait_ge(scattered, 16 * 2 * SG * NSTEP)
            next_load(NS - 2, 0)
            next_load(NS - 1, 1)
            with sp.Fori(NSTEP, NT // U) as s:
                for j in range(U):
                    next_load(s * U + j, j)
            next_load(NT - 3, 0)

        @block.gpsimd
        def _(pool):
            pool.sem_inc(gone, HEAD)
            for t, value in ((ident[:], 0.0), (is_hi[:], 1.0), (is_lo[:], 1.0), (bias_f, 0.0), (g[0][:], 0.0), (g[1][:], 0.0)):
                nc.gpsimd.memset(t, value).then_inc(s_const, 1)
            nc.gpsimd.iota(row_no[:], [[1, 1]], 0, 1, allow_small_or_imprecise_dtypes=True).then_inc(s_const, 1)
            pool.wait_ge(s_const, 7)
            nc.gpsimd.affine_select(out=ident[:], in_=ident[:], compare_op=ALU.not_equal, fill=1.0, base=0,
                                    pattern=[[-1, P]], channel_multiplier=1).then_inc(s_const, 1)
            nc.gpsimd.affine_select(out=is_hi[:], in_=is_hi[:], compare_op=ALU.is_ge, fill=0.0, base=LO - 1,
                                    pattern=[[1, 1]], channel_multiplier=-1).then_inc(s_const, 1)
            nc.gpsimd.affine_select(out=is_lo[:], in_=is_lo[:], compare_op=ALU.is_ge, fill=0.0, base=-LO,
                                    pattern=[[1, 1]], channel_multiplier=1).then_inc(s_const, 1)

            def row_load(s):
                pool.dma_start(xrow[:], xg[bass.ds(s * SG * P, SG * P), :].rearrange("(c p) d -> p c d", p=P)).then_inc(row_in, 16)

            def add(t, j):
                pool.wait_ge(y_ready, after(t))
                pool.sem_inc(passed, 1)
                for h in range(HV):
                    nc.gpsimd.indirect_dma_start(acc, bass.IndirectOffsetOnAxis(dest[j][:, h:h + 1], 0), y_sb[j % 2][:, h, :], None,
                                                 compute_op=ALU.add).then_inc(added, 16)

            def settle(t):
                pool.wait_ge(added, 16 * HV * (t + 1))
                pool.sem_inc(gone, 1)

            def scatter(idx):
                for c in range(SG):
                    nc.gpsimd.indirect_dma_start(xg, bass.IndirectOffsetOnAxis(idx[:, c:c + 1], 0), xrow[:, c, :], None).then_inc(scattered, 16)

            def put(dst, src, s):
                return nc.gpsimd.tensor_copy(dst, src[:, bass.ds(s * SG, SG)])

            pool.wait_ge(s_split, 3)
            row_load(0)
            with pool.Fori(0, NSTEP) as s:
                pool.wait_ge(row_in, (s + 1) * 16)
                pool.sem_inc(passed, 1)
                put(idx_a[:], slot_a, s).then_inc(set_done, 1)
                put(idx_b[:], slot_b, s).then_inc(set_done, 1)
                put(xrow[:, :, D + 1], w_a, s).then_inc(set_done, 1)
                pool.wait_ge(set_done, 6 * s + 3)
                pool.sem_inc(passed, 1)
                scatter(idx_a)
                add(s * U, 0)
                settle(s * U)
                pool.wait_ge(scattered, 16 * SG * (2 * s + 1))
                pool.sem_inc(passed, 1)
                put(xrow[:, :, D + 1], w_b, s).then_inc(set_done, 3)
                pool.wait_ge(set_done, 6 * s + 6)
                pool.sem_inc(passed, 1)
                scatter(idx_b)
                add(s * U + 1, 1)
                settle(s * U + 1)
                pool.wait_ge(scattered, 16 * SG * (2 * s + 2))
                row_load(s + 1)
                for j in range(2, U):
                    add(s * U + j, j)
                    settle(s * U + j)
            with pool.Fori(NSTEP, NT // U) as s:
                for j in range(U):
                    add(s * U + j, j)
                    settle(s * U + j)
            for t in range(NT - U + 1, NT):
                add(t, t % U)
                settle(t)
            pool.wait_ge(row_in, 16 * (NSTEP + 1))

        @block.scalar
        def _(act):
            for s_, start in ((xhi_done, HEAD), (h1_out, HEAD * HV), (silu_done, HEAD * HV), (hi_done, HEAD), (y_ready, HEAD)):
                act.sem_inc(s_, start)
            act.wait_ge(s_bias, 32)
            nc.scalar.copy(bias[:], bias_f).then_inc(s_split, 1)

            def x_high(s, j):
                t = s * U + j
                act.wait_ge(xt_ps, after(t))
                act.wait_ge(h_ps, part(t - 2, HV - 1))
                nc.scalar.copy(x_hi[j % 2][:], xt_bank[:].rearrange("p (k t) -> p k t", k=KT)).then_inc(xhi_done, 1)

            def silu(s, j):
                t = s * U + j
                for h in range(HV):
                    act.wait_ge(h1_ps, part(t, h))
                    act.wait_ge(ht_ps, after(t - 2))
                    nc.scalar.copy(g[j % 2][:, h, 0:HD], h_bank[h][0][:, 0:HD]).then_inc(h1_out, 1)
                for h in range(HV):
                    act.wait_ge(g_done, part(t, h))
                    nc.scalar.activation(g[j % 2][:, h, 0:HD], g[j % 2][:, h, 0:HD], ACT.Silu).then_inc(silu_done, 1)

            def weigh(s, j):
                t = s * U + j
                act.wait_ge(y_ps, after(t))
                act.wait_ge(gone, after(t - 2))
                for h in range(HV):
                    ins = nc.scalar.activation(y_sb[j % 2][:, h, :], y_bank[:, h * D:(h + 1) * D], ACT.Copy, scale=wgt[j % U][:, h:h + 1])
                ins.then_inc(y_ready, 1)

            def high(s, j):
                t = s * U + j
                act.wait_ge(ht_ps, after(t))
                act.wait_ge(y_ps, after(t - 1))
                nc.scalar.copy(h_hi[:], ht_bank[:, 0:HT * TILE].rearrange("p (i t) -> p i t", i=HT)).then_inc(hi_done, 1)

            pipeline(act, x_high, silu, weigh, high)

        @block.vector
        def _(dve):
            for s_, start in ((xlo_done, HEAD), (g_done, HEAD * HV), (lo_done, HEAD)):
                dve.sem_inc(s_, start)
            dve.wait_ge(s_const, NCONST)
            dve.wait_ge(s_split, 1)
            nc.vector.tensor_tensor(bias_f, bias_f, bias[:].bitcast(F32), ALU.subtract).then_inc(s_split, 1)
            dve.wait_ge(s_split, 2)
            nc.vector.tensor_scalar(bias_f, bias_f, is_lo[:, 0:1], None, ALU.mult).then_inc(s_fix, 1)
            nc.vector.tensor_scalar(row_no[:], is_lo[:], -float(LO), row_no[:, 0:1], ALU.mult, ALU.add).then_inc(s_fix, 1)
            dve.wait_ge(s_fix, 2)
            nc.vector.scalar_tensor_tensor(out=bias[:], in0=bias[:].bitcast(F32), scalar=is_hi[:, 0:1], in1=bias_f,
                                           op0=ALU.mult, op1=ALU.add).then_inc(s_split, 1)

            def x_low(s, j):
                t = s * U + j
                dve.wait_ge(xhi_done, after(t))
                nc.vector.tensor_tensor(x_lo[j % 2][:], xt_bank[:].rearrange("p (k t) -> p k t", k=KT),
                                        x_hi[j % 2][:].bitcast(F32), ALU.subtract)
                dve.wait_ge(gone, after(t - U))
                nc.vector.tensor_copy(dest[j % U][:].unsqueeze(2), xin[j % 2][:, :, D:D + 1].bitcast(I32))
                nc.vector.tensor_copy(wgt[j % U][:].unsqueeze(2), xin[j % 2][:, :, D + 1:D + 2])
                nc.vector.tensor_scalar(pick[j % U][:], eid_f[:, bass.ds(t, 1)].broadcast_to([P, P]), row_no[:, 0:1], None,
                                        ALU.is_equal).then_inc(xlo_done, 1)

            def gated(s, j):
                t = s * U + j
                for h in range(HV):
                    dve.wait_ge(h_ps, part(t, h))
                    dve.wait_ge(h1_out, part(t, h))
                    nc.vector.tensor_tensor(g[j % 2][:, h, 0:HD], h_bank[h][1][:, 0:HD], g[j % 2][:, h, 0:HD], ALU.mult).then_inc(g_done, 1)

            def low(s, j):
                t = s * U + j
                dve.wait_ge(hi_done, after(t))
                nc.vector.tensor_tensor(h_lo[:], ht_bank[:, 0:HT * TILE].rearrange("p (i t) -> p i t", i=HT),
                                        h_hi[:].bitcast(F32), ALU.subtract).then_inc(lo_done, 1)

            pipeline(dve, x_low, gated, lambda s, j: None, low)

        @block.tensor
        def _(pe):
            for s_, start in ((xt_ps, HEAD), (h1_ps, HEAD * HV), (h_ps, HEAD * HV), (y_ps, HEAD), (ht_ps, HEAD)):
                pe.sem_inc(s_, start)
            pe.wait_ge(s_const, NCONST)
            pe.wait_ge(s_split, 3)
            x_parts, h_parts = (x_hi, x_lo), (h_hi, h_lo)
            w13_parts, w2_parts = (w13_hi, w13_lo), (w2_hi, w2_lo)

            def expert_of(t):
                return pe.value_load(eid[0:1, bass.ds(t, 1)], min_val=0, max_val=NE - 1)

            def transposes(s, j):
                t = s * U + j
                pe.wait_ge(x_in[j % 2], loads(s, j))
                pe.wait_ge(xlo_done, after(t - 1))
                for k in range(KT):
                    for h in range(HV):
                        ins = pe.transpose(xt_bank[:, k * TILE + h * P:k * TILE + (h + 1) * P], xin[j % 2][:, h, k * P:(k + 1) * P], ident[:])
                ins.then_inc(xt_ps, 1)

            def hidden(s, j):
                t = s * U + j
                e = expert_of(t)
                pe.wait_ge(xlo_done, after(t))
                for h in range(HV):
                    pe.wait_ge(g_done, part(t - 1, h))
                    pe.wait_ge(s_const, NCONST)
                    for n in range(2):
                        pe.matmul(h_bank[h][n][:, 0:HD], pick[j % U][:], bias[:, n * HD:(n + 1) * HD], start=True, stop=False)
                        for k in range(KT):
                            for a, w in PASSES:
                                ins = pe.matmul(h_bank[h][n][:, 0:HD], x_parts[a][j % 2][:, k, h * P:(h + 1) * P],
                                                w13_parts[w][:, n, k, bass.ds(e, 1), :].rearrange("p o c -> p (o c)"),
                                                start=False, stop=(k == KT - 1 and a == 1))
                        if n == 0:
                            ins.then_inc(h1_ps, 1)
                    ins.then_inc(h_ps, 1)

            def turn(s, j):
                t = s * U + j
                pe.wait_ge(lo_done, after(t - 1))
                for h in range(HV):
                    pe.wait_ge(silu_done, part(t, h))
                    for i in range(HT):
                        ins = pe.transpose(ht_bank[:, i * TILE + h * P:i * TILE + (h + 1) * P], g[j % 2][:, h, i * P:(i + 1) * P], ident[:])
                ins.then_inc(ht_ps, 1)

            def down(s, j):
                t = s * U + j
                e = expert_of(t)
                pe.wait_ge(lo_done, after(t))
                pe.wait_ge(y_ready, after(t - 1))
                pe.wait_ge(s_const, NCONST)
                for h in range(HV):
                    pe.matmul(y_bank[:, h * D:(h + 1) * D], pick[j % U][:], bias[:, 2 * HD:2 * HD + D], start=True, stop=False)
                    for i in range(HT):
                        for a, w in PASSES:
                            ins = pe.matmul(y_bank[:, h * D:(h + 1) * D], h_parts[a][:, i, h * P:(h + 1) * P],
                                            w2_parts[w][:, bass.ds(e * HT + i, 1), :].rearrange("p o d -> p (o d)"),
                                            start=False, stop=(i == HT - 1 and a == 1))
                ins.then_inc(y_ps, 1)

            pipeline(pe, transposes, hidden, down, turn)


def finish(nc, acc, out):
    D = out.shape[1]
    T = 512
    CH = T // P
    NBLK = out.shape[0] // T
    with ExitStack() as ctx:
        def sb(name, shape):
            return ctx.enter_context(nc.sbuf_tensor(name, shape, F32))

        def sem(name):
            return ctx.enter_context(nc.semaphore(name))

        r = [sb(f"r{i}", [P, CH, D]) for i in range(NBLK)]
        stat = [sb(f"f_stat{i}", [P, CH, 6]) for i in range(NBLK)]
        mv = [sb(f"f_mv{i}", [P, CH, 2]) for i in range(NBLK)]
        rs = [sb(f"f_rs{i}", [P, CH]) for i in range(NBLK)]
        nb = [sb(f"f_nb{i}", [P, CH]) for i in range(NBLK)]
        c_eps = sb("f_eps", [P, CH])
        c_mhalf = sb("f_mhalf", [P, CH])
        c_zero = sb("f_zero", [P, CH])
        loaded = [sem(f"f_in{i}") for i in range(NBLK)]
        s_const, stat_done, mv_ready, rs_chain, done_v, done_a, stored = (
            sem("f_" + n) for n in ("const", "stat", "mv", "rs", "v", "a", "out"))
        acc_v = acc[512:, :].rearrange("(b c p) d -> b p c d", p=P, c=CH)
        out_v = out.rearrange("(b c p) d -> b p c d", p=P, c=CH)
        block = ctx.enter_context(nc.Block())

        @block.sync
        def _(sp):
            for b in range(NBLK):
                sp.dma_start(r[b][:], acc_v[b]).then_inc(loaded[b], 16)
            for b in range(NBLK):
                sp.wait_ge(done_v, b + 1)
                sp.wait_ge(done_a, b + 1)
                sp.dma_start(out_v[b], r[b][:]).then_inc(stored, 16)
            sp.wait_ge(stored, NBLK * 16)

        @block.gpsimd
        def _(pool):
            nc.gpsimd.memset(c_eps[:], EPS).then_inc(s_const, 1)
            nc.gpsimd.memset(c_mhalf[:], -0.5).then_inc(s_const, 1)
            nc.gpsimd.memset(c_zero[:], 0.0).then_inc(s_const, 1)
            pool.wait_ge(s_const, 3)
            for b in range(NBLK):
                pool.wait_ge(mv_ready, b + 1)
                nc.gpsimd.tensor_tensor(rs[b][:], mv[b][:, :, 1], c_eps[:], ALU.add).then_inc(rs_chain, 1)
                pool.wait_ge(rs_chain, 4 * b + 1)
                nc.gpsimd.tensor_tensor(rs[b][:], rs[b][:], c_mhalf[:], ALU.pow).then_inc(rs_chain, 1)
                pool.wait_ge(rs_chain, 4 * b + 2)
                nc.gpsimd.tensor_tensor(nb[b][:], mv[b][:, :, 0], rs[b][:], ALU.mult).then_inc(rs_chain, 1)
                pool.wait_ge(rs_chain, 4 * b + 3)
                nc.gpsimd.tensor_tensor(nb[b][:], c_zero[:], nb[b][:], ALU.subtract).then_inc(rs_chain, 1)

        @block.vector
        def _(dve):
            def stats(b):
                dve.wait_ge(loaded[b], 16)
                for k in range(CH):
                    ins = nc.vector.bn_stats(stat[b][:, k, :], r[b][:, k, :])
                ins.then_inc(stat_done, 1)
                dve.wait_ge(stat_done, b + 1)
                for k in range(CH):
                    ins = nc.vector.bn_aggr(mv[b][:, k, :], stat[b][:, k, :])
                ins.then_inc(mv_ready, 1)

            def scale(b):
                dve.wait_ge(rs_chain, 4 * b + 4)
                for k in range(CH // 2):
                    ins = nc.vector.tensor_scalar(r[b][:, k, :], r[b][:, k, :], mv[b][:, k, 0:1], rs[b][:, k:k + 1], ALU.subtract, ALU.mult)
                ins.then_inc(done_v, 1)

            for b in range(NBLK):
                stats(b)
                if b:
                    scale(b - 1)
            scale(NBLK - 1)

        @block.scalar
        def _(act):
            for b in range(NBLK):
                act.wait_ge(rs_chain, 4 * b + 4)
                for k in range(CH // 2, CH):
                    ins = nc.scalar.activation(r[b][:, k, :], r[b][:, k, :], ACT.Identity, bias=nb[b][:, k:k + 1], scale=rs[b][:, k:k + 1])
                ins.then_inc(done_a, 1)


def build(nc, a, out):
    tok, d = out.shape
    ne = a["f_gate"].shape[1]
    nr = routed_tiles(tok, ne)
    nt = tok // TILE + nr
    hd = a["f_w1"].shape[1] // (ne + 1)
    x1_dram = nc.dram_tensor("x1_dram", (tok // 512 + 1, 512, d), F32, kind="Internal").ap()
    xg = nc.dram_tensor("xg", (nt * TILE, d + 2), F32, kind="Internal").ap()
    acc = x1_dram.rearrange("b t d -> (b t) d")
    mixer(nc, a["uT"], a["u"], a["w_in"], a["conv_w"], a["conv_b"], a["rows"], a["norm_w"], a["w_out"], x1_dram)
    with ExitStack() as ctx:
        picks = [ctx.enter_context(nc.sbuf_tensor(n, [P, k], dt)) for n, k, dt in (
            ("slot_a", tok // P, I32), ("slot_b", tok // P, I32), ("w_a", tok // P, F32), ("w_b", tok // P, F32), ("eid", nt, I32), ("eid_f", nt, F32))]
        route(nc, x1_dram, xg, a["f_gate"], a["rows"], picks)
        with ExitStack() as inner:
            wts = [inner.enter_context(nc.sbuf_tensor(n, s, F32R)) for n, s in (
                ("w13_hi", [P, 2, d // P, ne + 1, hd]), ("w13_lo", [P, 2, d // P, ne + 1, hd]),
                ("w2_hi", [P, a["f_w2"].shape[1], d]), ("w2_lo", [P, a["f_w2"].shape[1], d]))]
            split_weights(nc, wts, a["f_w1"], a["f_w3"], a["f_w2"])
            experts(nc, wts, picks, xg, acc, a["f_bias"])
    finish(nc, acc, out)


def _layout(inputs):
    import numpy as np
    g = {k.split("_", 2)[2] if k.startswith("L0_attn") else "f_" + k.split("_", 2)[2]: np.asarray(v) for k, v in inputs.items()}
    u = g["u"].reshape(-1, g["u"].shape[-1])
    D = u.shape[1]
    H = g["f_sw1"].shape[1]
    HP = (H + P - 1) // P * P
    a = {
        "uT": u.T, "u": u, "w_in": g["in_proj_w"].T,
        "conv_w": g["conv_w"][:, 0, :].reshape(-1, P, 4).transpose(1, 0, 2), "conv_b": g["conv_b"].reshape(-1, P).T,
        "rows": np.concatenate([g["A_log"].ravel(), g["dt_bias"], g["D"], g["f_gate_b"]]),
        "norm_w": g["norm_w"].reshape(-1, P).T, "w_out": g["out_proj_w"].T,
    }

    def with_shared(per_expert, shared):
        return np.concatenate([per_expert, shared[None]])

    for i in "13":
        a["f_w" + i] = with_shared(g["f_w" + i], g["f_sw" + i]).transpose(1, 0, 2).reshape(D, -1)
    w2 = with_shared(g["f_w2"], g["f_sw2"])
    w2 = np.concatenate([w2, np.zeros((len(w2), HP - H, D), w2.dtype)], 1)
    a["f_w2"] = w2.reshape(-1, P, D).transpose(1, 0, 2)
    a["f_bias"] = np.concatenate([with_shared(g["f_b" + i], g["f_sb" + i]) for i in "132"], 1)
    a["f_gate"] = g["f_gate_w"].T
    return {k: np.ascontiguousarray(v) for k, v in a.items()}


def kernel(**inputs):
    import concourse.bacc as bacc
    from concourse.bass_utils import run_bass_kernel_spmd

    shape = inputs["L0_attn_u"].shape
    arrays = _layout(inputs)
    nc = bacc.Bacc("TRN2", target_bir_lowering=False, num_devices=1)
    a = {k: nc.dram_tensor("in_" + k, v.shape, mybir.dt.from_np(v.dtype), kind="ExternalInput").ap() for k, v in arrays.items()}
    tok, d = arrays["u"].shape
    out = nc.dram_tensor("out", (tok, d), F32, kind="ExternalOutput").ap()
    build(nc, a, out)
    r = run_bass_kernel_spmd(nc, [{"in_" + k: v for k, v in arrays.items()}], core_ids=[0])
    return r.results[0]["out"].reshape(shape)
```

```python
from contextlib import ExitStack

import concourse.bass as bass
from concourse import mybir

F32 = mybir.dt.float32
F32R = mybir.dt.float32r
I32 = mybir.dt.int32
ALU = mybir.AluOpType
ACT = mybir.ActivationFunctionType
AX = mybir.AxisListType

P = 128
PASSES = ((0, 0), (0, 1), (1, 0))
EPS = 1e-5
LOG_ZERO = -104.0

HEAD = 3

TILE = 256
TOP = 2


def routed_tiles(tok, experts):
    return (tok * TOP + experts * (TILE - 1)) // TILE


def mixer(nc, uT, u, w_in, conv_w, conv_b, rows, norm_w, w_out, x1_dram, xg):
    D, TOK = uT.shape
    KT = D // P
    T = 512
    CH = T // P
    SEQ = 1024
    NBLK = TOK // T
    NSEQ = TOK // SEQ
    H, HD = 8, 64
    DI = H * HD
    CT = (DI + 2 * P) // P
    TB, TC = DI // P, DI // P + 1
    OT = DI // P
    COLS = w_in.shape[1]
    DTC = COLS - H
    TAPS = 4
    assert SEQ == 2 * T and CH * H == 32

    with ExitStack() as ctx:
        def sb(name, shape, dt=F32):
            return ctx.enter_context(nc.sbuf_tensor(name, shape, dt))

        def bank(name, cols=512):
            return ctx.enter_context(nc.psum_tensor(name, [P, cols], F32))

        def sem(name):
            return ctx.enter_context(nc.semaphore(name))

        win = sb("win", [P, KT, COLS])
        win_hi = sb("win_hi", [P, KT, DTC], F32R)
        win_lo = sb("win_lo", [P, KT, DTC], F32R)
        wo = sb("wo", [P, OT, D])
        wo_hi = sb("wo_hi", [P, OT, D], F32R)
        wo_lo = sb("wo_lo", [P, OT, D], F32R)
        cw = sb("cw", [P, CT, TAPS])
        cb = sb("cb", [P, CT])
        nw = sb("nw", [P, OT])
        rowb = sb("rowb", [P, 48])
        expA = sb("expA", [P, 3, H])
        sumA = sb("sumA", [P, H])
        negA = sb("negA", [P, H])
        upto = sb("upto", [P, P])
        after = sb("after", [P, P])
        ones = sb("ones", [P, P])
        ident = sb("ident", [P, P])
        c_eps = sb("c_eps", [P, CH])
        c_inv = sb("c_inv", [P, CH])
        c_mhalf = sb("c_mhalf", [P, CH])
        ut = [sb(f"ut{i}", [P, KT, T]) for i in range(2)]
        u_hi = [sb(f"u_hi{i}", [P, KT, T], F32R) for i in range(2)]
        u_lo = [sb(f"u_lo{i}", [P, KT, T], F32R) for i in range(2)]
        pre = [sb(f"pre{i}", [P, CT, TAPS - 1 + T]) for i in range(2)]
        xbc = [sb(f"xbc{i}", [P, CT, T]) for i in range(2)]
        zs = [sb(f"zs{i}", [P, CH, DI]) for i in range(2)]
        dt = [sb(f"dt{i}", [P, CH * H]) for i in range(2)]
        la = [sb(f"la{i}", [P, CH * H]) for i in range(2)]
        dec = [sb(f"dec{i}", [P, 3, CH * H]) for i in range(2)]
        dtw = [sb(f"dtw{i}", [P, CH * H]) for i in range(2)]
        ur = [sb(f"ur{i}", [P, CH, D]) for i in range(2)]
        x1 = [sb(f"x1_{i}", [P, CH, D]) for i in range(2)]
        ss = [sb(f"ss{i}", [P, CH]) for i in range(2)]
        v_raw, v_dt, v_neg, v_e, v_w, v_d, v_m, v_l, v_q, v_p = (
            sb(n, [P, CH * H]) for n in ("v_raw", "v_dt", "v_neg", "v_e", "v_w", "v_d", "v_m", "v_l", "v_q", "v_p"))
        steps = sb("steps", [P, H, P])
        mt = sb("mt", [P, H, P])
        cbm = sb("cbm", [P, P])
        b_tok = sb("b_tok", [P, P])
        xs = sb("xs", [P, DI])
        xdt = sb("xdt", [P, DI])
        xw = sb("xw", [P, DI])
        xd = sb("xd", [P, DI])
        yb = sb("yb", [P, DI])
        gb = sb("gb", [P, DI])
        sq = sb("sq", [P, DI])
        g_hi = sb("g_hi", [P, OT, P], F32R)
        g_lo = sb("g_lo", [P, OT, P], F32R)
        state = sb("state", [P, DI])
        rms = sb("rms", [P, CH])
        stat = sb("stat", [P, CH, 6])
        mv = sb("mv", [P, CH, 2])
        rs = sb("rs", [P, CH])
        tiny = sb("tiny", [P, 1])
        spare = sb("spare", [P, 2, D + 2])
        own = sb("own", [P, (NBLK + 1) * CH, 2])

        ip_bank = [bank("ip_bank0"), bank("ip_bank1")]
        seg_bank = bank("seg_bank", 1024)
        out_bank = seg_bank[:, 0:D]
        cb_bank = bank("cb_bank")
        xt_bank = bank("xt_bank")
        yd_bank = bank("yd_bank")
        yo_bank = bank("yo_bank")

        s_w = sem("s_w")
        ut_in = [sem(f"ut_in{i}") for i in range(2)]
        ur_in = [sem(f"ur_in{i}") for i in range(2)]
        x1_out = sem("x1_out")
        xg_set = sem("xg_set")
        s_const = sem("s_const")
        s_spare = sem("s_spare")
        s_setup_a = sem("s_setup_a")
        s_setup_v = sem("s_setup_v")
        s_ready = sem("s_ready")
        ip_ps = sem("ip_ps")
        ip_ev = sem("ip_ev")
        uhi_done = sem("uhi_done")
        ulo_done = sem("ulo_done")
        taps_done = sem("taps_done")
        halo_done = sem("halo_done")
        silu_done = sem("silu_done")
        sp_chain = sem("sp_chain")
        sp_exp = sem("sp_exp")
        sp_ln = sem("sp_ln")
        dec_ready = sem("dec_ready")
        dtw_ready = sem("dtw_ready")
        cb_ps = sem("cb_ps")
        xt_ps = sem("xt_ps")
        seg_ps = sem("seg_ps")
        yo_ps = sem("yo_ps")
        ds_ps = sem("ds_ps")
        yd_ps = sem("yd_ps")
        gt_ps = sem("gt_ps")
        out_ps = sem("out_ps")
        steps_ready = sem("steps_ready")
        xs_ready = sem("xs_ready")
        xw_ready = sem("xw_ready")
        xd_ready = sem("xd_ready")
        cbm_ready = sem("cbm_ready")
        exp_done = sem("exp_done")
        mt_ready = sem("mt_ready")
        y1_done = sem("y1_done")
        t2_done = sem("t2_done")
        st_scaled = sem("st_scaled")
        st_ready = sem("st_ready")
        y_ready = sem("y_ready")
        g_ready = sem("g_ready")
        ss_ready = sem("ss_ready")
        ghi_done = sem("ghi_done")
        glo_done = sem("glo_done")
        out_ev = sem("out_ev")
        rms_chain = sem("rms_chain")
        rms_ready = sem("rms_ready")
        res_done = sem("res_done")
        stat_done = sem("stat_done")
        mv_ready = sem("mv_ready")
        rs_chain = sem("rs_chain")
        rs_ready = sem("rs_ready")
        x1_ready = sem("x1_ready")

        uT_v = uT.rearrange("(k p) (b t) -> b p k t", p=P, t=T)
        u_v = u.rearrange("(b c p) d -> b p c d", p=P, c=CH)
        x1_v = x1_dram.rearrange("b (c p) d -> b p c d", p=P)
        own_rows = xg[0:TOK + T]
        xg_v = own_rows.rearrange("(b c p) d -> b p c d", p=P, c=CH)
        NW = 6

        ITEMS = [[["dt", 0], [1]], [[2], [3]], [[4], [5, "cs"]], [["z0", "z1"], ["z2", "z3"]]]
        ORDER = [x for slot in ITEMS for half in slot for x in half]
        NI = len(ORDER)

        def after_chunk(j):
            return j + HEAD

        def after_block(n):
            return n + HEAD

        SP_OPS = 14

        def softplus(m, i=SP_OPS):
            return m * SP_OPS + i + 1

        def taps(m, tile, i=TAPS - 1):
            return (m * CT + tile) * (TAPS - 1) + i

        block = ctx.enter_context(nc.Block())

        @block.sync
        def _(sp):
            sp.dma_start(ut[0][:], uT_v[0]).then_inc(ut_in[0], 16)
            for dst, src in ((win, w_in.rearrange("(k p) c -> p k c", p=P)), (wo, w_out.rearrange("(k p) c -> p k c", p=P)),
                             (cw, conv_w), (nw, norm_w), (cb, conv_b)):
                sp.dma_start(dst[:], src).then_inc(s_w, 16)
            sp.dma_start(rowb[:], rows.partition_broadcast(P)).then_inc(s_w, 16)
            sp.dma_start(ut[1][:], uT_v[1]).then_inc(ut_in[1], 16)
            sp.wait_ge(s_spare, 4)
            sp.dma_start(own_rows.rearrange("(c p) d -> p c d", p=P)[:, :, D:D + 2], own[:]).then_inc(xg_set, 16)
            empty = xg[TOK + T:].rearrange("(t h p) d -> h p t d", p=P, h=2)
            for h in range(2):
                sp.dma_start(empty[h], spare[:, h, :].unsqueeze(1).broadcast_to([P, empty.shape[2], D + 2])).then_inc(xg_set, 16)

            def step(s, par, last):
                n = s * 2 + par
                sp.wait_ge(x1_ready, after_block(n - 2))
                sp.dma_start(ur[par][:], u_v[n]).then_inc(ur_in[par], 16)
                if not last:
                    sp.wait_ge(ip_ps, (n + 1) * NI)
                    sp.dma_start(ut[par][:], uT_v[n + 2]).then_inc(ut_in[par], 16)
                sp.wait_ge(x1_ready, after_block(n - 1))
                sp.dma_start(x1_v[n], x1[1 - par][:]).then_inc(x1_out, 16)
                sp.dma_start(xg_v[n][:, :, 0:D], x1[1 - par][:]).then_inc(x1_out, 16)

            with sp.Fori(0, NSEQ - 1) as s:
                step(s, 0, False)
                step(s, 1, False)
            step(NSEQ - 1, 0, True)
            step(NSEQ - 1, 1, True)
            sp.wait_ge(x1_ready, after_block(NBLK - 1))
            sp.dma_start(x1_v[NBLK], x1[1][:]).then_inc(x1_out, 16)
            sp.dma_start(xg_v[NBLK][:, :, 0:D], x1[1][:]).then_inc(x1_out, 16)
            sp.wait_ge(x1_out, 32 * (NBLK + 2))
            sp.wait_ge(xg_set, 48)

        @block.gpsimd
        def _(pool):
            for s_, start in ((steps_ready, 2), (xw_ready, 2), (xd_ready, 2), (y_ready, 2), (g_ready, 2),
                              (ulo_done, 2), (rms_ready, 1), (rs_ready, 1)):
                pool.sem_inc(s_, start)
            pool.sem_inc(x1_out, 32)
            pool.sem_inc(ur_in[1], 16)
            for t, value in ((upto, 1.0), (after, 1.0), (ident, 0.0), (ones, 1.0), (c_eps, EPS), (c_inv, 1.0 / DI),
                             (c_mhalf, -0.5), (gb, 0.0), (yb, 0.0), (ur[1], 0.0), (x1[1], 0.0), (ss[1], 0.0),
                             (state, 0.0), (pre[0], 0.0)):
                nc.gpsimd.memset(t[:], value).then_inc(s_const, 1)
            NSET = 14
            pool.wait_ge(s_const, NSET)
            nc.gpsimd.affine_select(out=upto[:], in_=upto[:], compare_op=ALU.is_ge, fill=0.0, base=0,
                                    pattern=[[1, P]], channel_multiplier=-1).then_inc(s_const, 1)
            nc.gpsimd.affine_select(out=after[:], in_=after[:], compare_op=ALU.is_ge, fill=0.0, base=-1,
                                    pattern=[[-1, P]], channel_multiplier=1).then_inc(s_const, 1)
            nc.gpsimd.affine_select(out=ident[:], in_=ident[:], compare_op=ALU.not_equal, fill=1.0, base=0,
                                    pattern=[[-1, P]], channel_multiplier=1).then_inc(s_const, 1)
            nc.gpsimd.memset(spare[:], 0.0).then_inc(s_spare, 1)
            nc.gpsimd.memset(own[:, :, 1], 1.0).then_inc(s_spare, 1)
            nc.gpsimd.iota(own[:, :, 0:1].bitcast(I32), [[P, (NBLK + 1) * CH], [1, 1]], 0, 1).then_inc(s_spare, 1)
            pool.wait_ge(s_spare, 3)
            nc.gpsimd.iota(spare[:, :, D:D + 1].bitcast(I32), [[P, 2], [1, 1]], 0, 1).then_inc(s_spare, 1)
            pool.wait_ge(s_const, NSET + 3)

            def split_lo(n, par):
                pool.wait_ge(uhi_done, after_block(n))
                nc.gpsimd.tensor_tensor(u_lo[par][:], ut[par][:], u_hi[par][:].bitcast(F32),
                                        ALU.subtract).then_inc(ulo_done, 1)

            def make_steps(c, n, par, k):
                if k == 0:
                    pool.wait_ge(sp_chain, softplus(n))
                pool.wait_ge(seg_ps, after_chunk(c - 1))
                nc.gpsimd.tensor_tensor(
                    steps[:], upto[:].unsqueeze(1).broadcast_to([P, H, P]),
                    la[par][:, k * H:(k + 1) * H].unsqueeze(2).broadcast_to([P, H, P]), ALU.mult).then_inc(steps_ready, 1)

            def heads(t):
                return t[:].rearrange("p (h d) -> p h d", h=H)

            def per_head(t):
                return t.unsqueeze(2).broadcast_to([P, H, HD])

            def step(s, par, last):
                n = s * 2 + par
                for k in range(CH):
                    c = n * CH + k
                    if k == 0:
                        pool.wait_ge(dtw_ready, after_block(n))
                    pool.wait_ge(xs_ready, after_chunk(c))
                    pool.wait_ge(yd_ps, after_chunk(c - 1))
                    nc.gpsimd.tensor_tensor(heads(xdt), heads(xs), per_head(dt[par][:, k * H:(k + 1) * H]), ALU.mult)
                    nc.gpsimd.tensor_tensor(heads(xw), heads(xs), per_head(dtw[par][:, k * H:(k + 1) * H]),
                                            ALU.mult).then_inc(xw_ready, 1)
                    nc.gpsimd.tensor_tensor(heads(xd), heads(xs), per_head(rowb[:, 32:40]), ALU.mult).then_inc(xd_ready, 1)
                    if k < CH - 1:
                        make_steps(c + 1, n, par, k + 1)
                    elif not (last and par == 1):
                        make_steps(c + 1, n + 1, 1 - par, 0)
                    if k == 1:
                        pool.wait_ge(ss_ready, after_chunk(n * CH - 1))
                        nc.gpsimd.tensor_tensor(rms[:], ss[1 - par][:], c_inv[:], ALU.mult).then_inc(rms_chain, 1)
                        pool.wait_ge(rms_chain, n * 2 + 1)
                        nc.gpsimd.tensor_tensor(rms[:], rms[:], c_eps[:], ALU.add).then_inc(rms_chain, 1)
                        pool.wait_ge(rms_chain, n * 2 + 2)
                        nc.gpsimd.tensor_tensor(rms[:], rms[:], c_mhalf[:], ALU.pow).then_inc(rms_ready, 1)
                    if k == 2 and not last:
                        split_lo(n + 2, par)
                    if k == 3:
                        norm_scale(n)
                    pool.wait_ge(t2_done, after_chunk(c))
                    pool.wait_ge(xd_ready, after_chunk(c))
                    nc.gpsimd.tensor_tensor(yb[:], yb[:], xd[:], ALU.add).then_inc(y_ready, 1)
                    pool.wait_ge(gt_ps, after_chunk(c - 1))
                    pool.wait_ge(y_ready, after_chunk(c))
                    nc.gpsimd.tensor_tensor(gb[:], yb[:], zs[par][:, k, :], ALU.mult).then_inc(g_ready, 1)

            def norm_scale(n):
                pool.wait_ge(mv_ready, after_block(n - 1))
                nc.gpsimd.tensor_tensor(rs[:], mv[:, :, 1], c_eps[:], ALU.add).then_inc(rs_chain, 1)
                pool.wait_ge(rs_chain, n + 1)
                nc.gpsimd.tensor_tensor(rs[:], rs[:], c_mhalf[:], ALU.pow).then_inc(rs_ready, 1)

            split_lo(0, 0)
            split_lo(1, 1)
            make_steps(0, 0, 0, 0)
            with pool.Fori(0, NSEQ - 1) as s:
                step(s, 0, False)
                step(s, 1, False)
            step(NSEQ - 1, 0, True)
            step(NSEQ - 1, 1, True)
            n = NBLK
            pool.wait_ge(ss_ready, after_chunk(n * CH - 1))
            nc.gpsimd.tensor_tensor(rms[:], ss[1][:], c_inv[:], ALU.mult).then_inc(rms_chain, 1)
            pool.wait_ge(rms_chain, n * 2 + 1)
            nc.gpsimd.tensor_tensor(rms[:], rms[:], c_eps[:], ALU.add).then_inc(rms_chain, 1)
            pool.wait_ge(rms_chain, n * 2 + 2)
            nc.gpsimd.tensor_tensor(rms[:], rms[:], c_mhalf[:], ALU.pow).then_inc(rms_ready, 1)
            norm_scale(n)

        @block.scalar
        def _(act):
            for s_, start in ((ss_ready, 1), (ghi_done, 1), (out_ev, 1), (xs_ready, 2), (exp_done, 2),
                              (uhi_done, 2), (silu_done, 2), (dec_ready, 2), (sp_exp, 2), (sp_ln, 2)):
                act.sem_inc(s_, start)

            def split_hi(n, par, i):
                act.wait_ge(ut_in[par], 16 * (i + 1))
                nc.scalar.copy(u_hi[par][:], ut[par][:]).then_inc(uhi_done, 1)

            split_hi(0, 0, 0)
            act.wait_ge(s_w, 16 * NW)
            nc.scalar.activation(expA[:], rowb[:, 0:24].rearrange("p (a h) -> p a h", a=3), ACT.Exp).then_inc(s_setup_a, 1)
            nc.scalar.copy(win_hi[:], win[:, :, 0:DTC]).then_inc(s_setup_a, 1)
            act.wait_ge(s_setup_v, 1)
            nc.scalar.copy(wo_hi[:], wo[:]).then_inc(s_setup_a, 1)
            act.wait_ge(s_const, 17)
            split_hi(1, 1, 0)

            def evacuate(m, par, item):
                j = ORDER.index(item)
                b = ip_bank[j % 2]
                act.wait_ge(ip_ps, m * NI + j + 1)
                if item == "dt":
                    act.wait_ge(sp_chain, softplus(m - 1))
                    nc.scalar.copy(v_raw[:], b[:, 0:CH * H]).then_inc(ip_ev, 1)
                elif item == "cs":
                    nc.scalar.activation(dec[par][:], b[:, 0:3 * CH * H].rearrange("p (a c) -> p a c", a=3),
                                         ACT.Exp).then_inc(ip_ev, 1)
                elif isinstance(item, str):
                    nc.scalar.activation(zs[par][:, int(item[1]), :], b[:], ACT.Silu).then_inc(ip_ev, 1)
                else:
                    if item == 0:
                        if not (isinstance(m, int) and m == 0):
                            act.wait_ge(yo_ps, after_chunk(m * CH - CH - 1))
                    nc.scalar.copy(pre[par][:, item, TAPS - 1:], b[:])
                    nc.scalar.activation(xbc[par][:, item, :], b[:], ACT.Identity, bias=cb[:, item:item + 1],
                                         scale=cw[:, item, TAPS - 1:TAPS]).then_inc(ip_ev, 1)

            def softplus_exp(m):
                act.wait_ge(sp_chain, softplus(m, 2))
                nc.scalar.activation(v_e[:], v_neg[:], ACT.Exp).then_inc(sp_exp, 1)

            def softplus_ln(m):
                act.wait_ge(sp_chain, softplus(m, 3))
                nc.scalar.activation(v_l[:], v_w[:], ACT.Ln).then_inc(sp_ln, 1)

            def silu(m, par):
                act.wait_ge(taps_done, taps(m, CT - 1))
                nc.scalar.activation(xbc[par][:], xbc[par][:], ACT.Silu).then_inc(silu_done, 1)

            def square(c, par, k):
                act.wait_ge(y_ready, after_chunk(c))
                act.wait_ge(ss_ready, after_chunk(c - 1))
                nc.scalar.activation(sq[:], yb[:], ACT.Square, accum_out=ss[par][:, k:k + 1]).then_inc(ss_ready, 1)

            def g_high(c):
                act.wait_ge(gt_ps, after_chunk(c))
                act.wait_ge(out_ps, after_chunk(c - 1))
                nc.scalar.copy(g_hi[:].rearrange("p a b -> p (a b)"), yo_bank[:]).then_inc(ghi_done, 1)

            def take_out(c, par, k):
                act.wait_ge(out_ps, after_chunk(c))
                nc.scalar.copy(x1[par][:, k, :], out_bank).then_inc(out_ev, 1)

            def step(s, par, last):
                n = s * 2 + par
                more = not (last and par == 1)
                for k in range(CH):
                    c = n * CH + k
                    before = (par, k - 1) if k else (1 - par, CH - 1)
                    square(c - 1, *before)
                    act.wait_ge(xt_ps, after_chunk(c))
                    act.wait_ge(xd_ready, after_chunk(c - 1))
                    nc.scalar.copy(xs[:], xt_bank[:]).then_inc(xs_ready, 1)
                    g_high(c - 1)
                    act.wait_ge(seg_ps, after_chunk(c))
                    act.wait_ge(yd_ps, after_chunk(c - 1))
                    nc.scalar.activation(mt[:].rearrange("p h i -> p (h i)"), seg_bank[:], ACT.Exp).then_inc(exp_done, 1)
                    if more and k == 1:
                        softplus_exp(n + 1)
                    if more and k == CH - 1:
                        silu(n + 1, 1 - par)
                    for half in range(2):
                        if more:
                            for item in ITEMS[k][half]:
                                evacuate(n + 1, 1 - par, item)
                    if more and k == 1:
                        softplus_ln(n + 1)
                    if k == 2 and not last:
                        split_hi(n + 2, par, s + 1)
                    if k == 1:
                        act.wait_ge(x1_out, 32 * (n + 1))
                    take_out(c - 1, *before)

            for item in ORDER:
                evacuate(0, 0, item)
                if item == "dt":
                    softplus_exp(0)
                if item == 1:
                    softplus_ln(0)
            silu(0, 0)
            with act.Fori(0, NSEQ - 1) as s:
                step(s, 0, False)
                step(s, 1, False)
            step(NSEQ - 1, 0, True)
            step(NSEQ - 1, 1, True)
            c = NBLK * CH
            square(c - 1, 1, CH - 1)
            g_high(c - 1)
            take_out(c - 1, 1, CH - 1)

        @block.vector
        def _(dve):
            for s_, start in ((cbm_ready, 2), (mt_ready, 2), (y1_done, 2), (t2_done, 2), (st_scaled, 2), (st_ready, 2),
                              (glo_done, 1), (dtw_ready, 2), (sp_chain, 1), (res_done, 1), (stat_done, 1), (mv_ready, 1), (x1_ready, 1)):
                dve.sem_inc(s_, start)
            dve.wait_ge(s_w, 16 * NW)
            for k in range(OT):
                ins = nc.vector.tensor_scalar(wo[:, k, :], wo[:, k, :], nw[:, k:k + 1], None, ALU.mult)
            ins.then_inc(s_setup_v, 1)
            dve.wait_ge(s_setup_a, 1)
            nc.vector.tensor_tensor(sumA[:], expA[:, 0, :], expA[:, 1, :], ALU.add).then_inc(s_setup_v, 1)
            dve.wait_ge(s_setup_v, 2)
            nc.vector.tensor_tensor(negA[:], sumA[:], expA[:, 2, :], ALU.add).then_inc(s_setup_v, 1)
            dve.wait_ge(s_setup_v, 3)
            nc.vector.tensor_scalar(negA[:], negA[:], -1.0 / 3.0, None, ALU.mult).then_inc(s_setup_v, 1)
            dve.wait_ge(s_setup_a, 2)
            nc.vector.tensor_tensor(win_lo[:], win[:, :, 0:DTC], win_hi[:].bitcast(F32), ALU.subtract).then_inc(s_setup_v, 1)
            dve.wait_ge(s_setup_a, 3)
            nc.vector.tensor_tensor(wo_lo[:], wo[:], wo_hi[:].bitcast(F32), ALU.subtract).then_inc(s_setup_v, 1)
            dve.wait_ge(s_setup_v, 6)
            dve.wait_ge(s_const, 17)

            def by_head(row):
                return row.unsqueeze(1).broadcast_to([P, CH, H])

            def by_chunk(t):
                return t[:].rearrange("p (c h) -> p c h", c=CH)

            def convolve(s, m, par, tile):
                dve.wait_ge(ip_ev, m * NI + ORDER.index(tile) + 1)
                if par == 1:
                    nc.vector.tensor_copy(pre[1][:, tile, 0:TAPS - 1], pre[0][:, tile, T:T + TAPS - 1]).then_inc(halo_done, 1)
                    dve.wait_ge(halo_done, s * CT + tile + 1)
                for tap in range(TAPS - 1):
                    if tap:
                        dve.wait_ge(taps_done, taps(m, tile, tap))
                    nc.vector.scalar_tensor_tensor(out=xbc[par][:, tile, :], in0=pre[par][:, tile, tap:tap + T],
                                                   scalar=cw[:, tile, tap:tap + 1], in1=xbc[par][:, tile, :],
                                                   op0=ALU.mult, op1=ALU.add).then_inc(taps_done, 1)

            def softplus_a(m):
                dve.wait_ge(ip_ev, m * NI + ORDER.index("dt") + 1)
                nc.vector.tensor_tensor(by_chunk(v_dt), by_chunk(v_raw), by_head(rowb[:, 24:32]), ALU.add).then_inc(sp_chain, 1)
                dve.wait_ge(sp_chain, softplus(m, 1))
                nc.vector.scalar_tensor_tensor(out=v_neg[:], in0=v_dt[:], scalar=-1.0, in1=v_dt[:], op0=ALU.mult,
                                               op1=ALU.min).then_inc(sp_chain, 1)

            def softplus_b(m):
                dve.wait_ge(sp_exp, after_block(m))
                nc.vector.tensor_scalar(v_w[:], v_e[:], 1.0, None, ALU.add).then_inc(sp_chain, 1)
                dve.wait_ge(sp_chain, softplus(m, 3))
                nc.vector.tensor_scalar(v_d[:], v_w[:], -1.0, None, ALU.add).then_inc(sp_chain, 1)
                dve.wait_ge(sp_chain, softplus(m, 4))
                nc.vector.tensor_scalar(v_m[:], v_d[:], 0.0, None, ALU.is_equal).then_inc(sp_chain, 1)
                dve.wait_ge(sp_chain, softplus(m, 5))
                nc.vector.tensor_tensor(v_d[:], v_d[:], v_m[:], ALU.add).then_inc(sp_chain, 1)
                dve.wait_ge(sp_chain, softplus(m, 6))
                nc.vector.reciprocal(v_q[:], v_d[:]).then_inc(sp_chain, 1)
                nc.vector.tensor_tensor(v_p[:], v_e[:], v_m[:], ALU.mult).then_inc(sp_chain, 1)
                dve.wait_ge(sp_chain, softplus(m, 8))
                nc.vector.tensor_tensor(v_q[:], v_e[:], v_q[:], ALU.mult).then_inc(sp_chain, 1)

            def softplus_c(m, par):
                dve.wait_ge(sp_ln, after_block(m))
                dve.wait_ge(sp_chain, softplus(m, 9))
                nc.vector.tensor_tensor(v_q[:], v_l[:], v_q[:], ALU.mult).then_inc(sp_chain, 1)
                dve.wait_ge(sp_chain, softplus(m, 10))
                nc.vector.tensor_tensor(v_q[:], v_q[:], v_p[:], ALU.add).then_inc(sp_chain, 1)
                dve.wait_ge(sp_chain, softplus(m, 11))
                nc.vector.scalar_tensor_tensor(out=dt[par][:], in0=v_dt[:], scalar=0.0, in1=v_q[:], op0=ALU.max,
                                               op1=ALU.add).then_inc(sp_chain, 1)
                dve.wait_ge(sp_chain, softplus(m, 12))
                nc.vector.tensor_tensor(by_chunk(la[par]), by_chunk(dt[par]), by_head(negA[:]), ALU.mult).then_inc(sp_chain, 1)
                dve.wait_ge(sp_chain, softplus(m, 13))
                nc.vector.tensor_scalar(la[par][:], la[par][:], LOG_ZERO, None, ALU.max).then_inc(sp_chain, 1)

            def end_weights(m, par):
                dve.wait_ge(ip_ev, m * NI + ORDER.index("cs") + 1)
                nc.vector.tensor_tensor(dtw[par][:], dt[par][:], dec[par][:, 1, :], ALU.mult).then_inc(dtw_ready, 1)

            def g_low(c):
                dve.wait_ge(ghi_done, after_chunk(c))
                nc.vector.tensor_tensor(g_lo[:].rearrange("p a b -> p (a b)"), yo_bank[:],
                                        g_hi[:].rearrange("p a b -> p (a b)").bitcast(F32), ALU.subtract).then_inc(glo_done, 1)

            def residual(s, n, par):
                q = 1 - par
                dve.wait_ge(rms_ready, after_block(n - 1))
                dve.wait_ge(out_ev, after_chunk(n * CH - 1))
                dve.wait_ge(ur_in[q], 16 * (s + 1))
                for k in range(CH):
                    ins = nc.vector.scalar_tensor_tensor(out=x1[q][:, k, :], in0=x1[q][:, k, :], scalar=rms[:, k:k + 1],
                                                         in1=ur[q][:, k, :], op0=ALU.mult, op1=ALU.add)
                ins.then_inc(res_done, 1)
                dve.wait_ge(res_done, after_block(n - 1))
                for k in range(CH):
                    ins = nc.vector.bn_stats(stat[:, k, :], x1[q][:, k, :])
                ins.then_inc(stat_done, 1)
                dve.wait_ge(stat_done, after_block(n - 1))
                nc.vector.memset(tiny[:], 0.0)
                for k in range(CH):
                    ins = nc.vector.bn_aggr(mv[:, k, :], stat[:, k, :])
                ins.then_inc(mv_ready, 1)

            def normalise(n, par):
                q = 1 - par
                dve.wait_ge(rs_ready, after_block(n - 1))
                for k in range(CH):
                    ins = nc.vector.tensor_scalar(x1[q][:, k, :], x1[q][:, k, :], mv[:, k, 0:1], rs[:, k:k + 1],
                                                  ALU.subtract, ALU.mult)
                ins.then_inc(x1_ready, 1)

            def heads(t):
                return t[:].rearrange("p (h d) -> p h d", h=H)

            def per_head(t):
                return t.unsqueeze(2).broadcast_to([P, H, HD])

            def step(s, par, last):
                n = s * 2 + par
                m = n + 1
                more = not (last and par == 1)
                for k in range(CH):
                    c = n * CH + k
                    hk = slice(k * H, (k + 1) * H)
                    dve.wait_ge(cb_ps, after_chunk(c))
                    nc.vector.tensor_tensor(cbm[:], cb_bank[:, 0:P], upto[:], ALU.mult)
                    dve.wait_ge(st_ready, after_chunk(c - 1))
                    nc.vector.tensor_copy(b_tok[:], cb_bank[:, P:2 * P]).then_inc(cbm_ready, 1)
                    g_low(c - 1)
                    dve.wait_ge(exp_done, after_chunk(c))
                    dve.wait_ge(cbm_ready, after_chunk(c))
                    nc.vector.tensor_tensor(mt[:], mt[:], cbm[:].unsqueeze(1).broadcast_to([P, H, P]), ALU.mult).then_inc(mt_ready, 1)
                    dve.wait_ge(yo_ps, after_chunk(c))
                    dve.wait_ge(g_ready, after_chunk(c - 1))
                    dve.wait_ge(ss_ready, after_chunk(c - 1))
                    if par == 0 and k == 0:
                        nc.vector.memset(yb[:], 0.0).then_inc(y1_done, 1)
                        nc.vector.memset(state[:], 0.0).then_inc(st_scaled, 1)
                    else:
                        nc.vector.tensor_tensor(heads(yb), heads(yo_bank), per_head(dec[par][:, 0, hk]), ALU.mult).then_inc(y1_done, 1)
                        nc.vector.tensor_tensor(heads(state), heads(state), per_head(dec[par][:, 2, hk]), ALU.mult).then_inc(st_scaled, 1)
                    dve.wait_ge(ds_ps, after_chunk(c))
                    dve.wait_ge(st_scaled, after_chunk(c))
                    nc.vector.tensor_tensor(state[:], xt_bank[:], state[:], ALU.add).then_inc(st_ready, 1)
                    dve.wait_ge(yd_ps, after_chunk(c))
                    dve.wait_ge(y1_done, after_chunk(c))
                    nc.vector.tensor_tensor(yb[:], yd_bank[:], yb[:], ALU.add).then_inc(t2_done, 1)
                    if more:
                        if k == 0:
                            softplus_a(m)
                        if k == 1:
                            softplus_b(m)
                        for half in range(2):
                            for item in ITEMS[k][half]:
                                if isinstance(item, int):
                                    convolve(s + par, m, 1 - par, item)
                        if k == 1:
                            softplus_c(m, 1 - par)
                        if k == 2:
                            end_weights(m, 1 - par)
                    if k == 2:
                        residual(s, n, par)
                    if k == 3:
                        normalise(n, par)

            softplus_a(0)
            softplus_b(0)
            convolve(0, 0, 0, 0)
            convolve(0, 0, 0, 1)
            softplus_c(0, 0)
            for tile in range(2, CT):
                convolve(0, 0, 0, tile)
            end_weights(0, 0)
            with dve.Fori(0, NSEQ - 1) as s:
                step(s, 0, False)
                step(s, 1, False)
            step(NSEQ - 1, 0, True)
            step(NSEQ - 1, 1, True)
            g_low(NBLK * CH - 1)
            residual(NSEQ, NBLK, 0)
            normalise(NBLK, 0)

        @block.tensor
        def _(pe):
            for s_, start in ((cb_ps, 2), (xt_ps, 2), (seg_ps, 2), (yo_ps, 2), (ds_ps, 2), (yd_ps, 2), (gt_ps, 1), (out_ps, 1)):
                pe.sem_inc(s_, start)
            pe.wait_ge(s_w, 16 * NW)
            pe.wait_ge(s_const, 17)
            pe.wait_ge(s_setup_v, 6)
            w_parts = (win_hi, win_lo)

            def project(m, par, item):
                j = ORDER.index(item)
                b = ip_bank[j % 2]
                u_parts = (u_hi[par], u_lo[par])
                if j == 0:
                    pe.wait_ge(ulo_done, after_block(m))
                if not (isinstance(m, int) and m == 0 and j < 2):
                    pe.wait_ge(ip_ev, m * NI + j - 1)
                if item == "dt":
                    for q in range(CH):
                        for k in range(KT):
                            ins = pe.matmul(b[:, q * H:(q + 1) * H], ut[par][:, k, q * P:(q + 1) * P],
                                            win[:, k, DTC:DTC + H], start=(k == 0), stop=(k == KT - 1))
                elif item == "cs":
                    pe.wait_ge(sp_chain, softplus(m))
                    for i, mask in enumerate((upto, after, ones)):
                        ins = pe.matmul(b[:, i * CH * H:(i + 1) * CH * H], mask[:], la[par][:], start=True, stop=True)
                else:
                    for k in range(KT):
                        for a, w in PASSES:
                            if isinstance(item, str):
                                q = int(item[1])
                                lhs, rhs = u_parts[a][:, k, q * P:(q + 1) * P], w_parts[w][:, k, 0:DI]
                            else:
                                lhs = w_parts[w][:, k, DI + item * P:DI + (item + 1) * P]
                                rhs = u_parts[a][:, k, :]
                            ins = pe.matmul(b[:], lhs, rhs, start=(k == 0 and a + w == 0), stop=(k == KT - 1 and a == 1))
                ins.then_inc(ip_ps, 1)

            def g_transposes(c):
                pe.wait_ge(g_ready, after_chunk(c))
                for q in range(OT):
                    ins = pe.transpose(yo_bank[:, q * P:(q + 1) * P], gb[:, q * P:(q + 1) * P], ident[:])
                ins.then_inc(gt_ps, 1)

            def out_project(c):
                for k in range(OT):
                    for a, w in PASSES:
                        ins = pe.matmul(out_bank, (g_hi, g_lo)[a][:, k, :], (wo_hi, wo_lo)[w][:, k, :],
                                        start=(k == 0 and a + w == 0), stop=(k == OT - 1 and a == 1))
                ins.then_inc(out_ps, 1)

            def step(s, par, last):
                n = s * 2 + par
                more = not (last and par == 1)
                for k in range(CH):
                    c = n * CH + k
                    tok = slice(k * P, (k + 1) * P)
                    if k == 0:
                        pe.wait_ge(silu_done, after_block(n))
                    pe.wait_ge(cbm_ready, after_chunk(c - 1))
                    pe.matmul(cb_bank[:, 0:P], xbc[par][:, TB, tok], xbc[par][:, TC, tok], start=True, stop=True)
                    pe.transpose(cb_bank[:, P:2 * P], xbc[par][:, TB, tok], ident[:]).then_inc(cb_ps, 1)
                    pe.wait_ge(st_ready, after_chunk(c - 1))
                    for q in range(OT):
                        ins = pe.transpose(xt_bank[:, q * P:(q + 1) * P], xbc[par][:, q, tok], ident[:])
                    ins.then_inc(xt_ps, 1)
                    pe.wait_ge(steps_ready, after_chunk(c))
                    pe.matmul(seg_bank[:, 512:1024], after[:], steps[:, 4:8, :].rearrange("p h i -> p (h i)"), start=True, stop=True)
                    pe.wait_ge(out_ev, after_chunk(c - 2))
                    pe.matmul(seg_bank[:, 0:512], after[:], steps[:, 0:4, :].rearrange("p h i -> p (h i)"),
                              start=True, stop=True).then_inc(seg_ps, 1)
                    g_transposes(c - 1)
                    if more:
                        for item in ITEMS[k][0]:
                            project(n + 1, 1 - par, item)
                    pe.wait_ge(glo_done, after_chunk(c - 1))
                    pe.matmul(yo_bank[:], xbc[par][:, TC, tok], state[:], start=True, stop=True).then_inc(yo_ps, 1)
                    pe.wait_ge(xw_ready, after_chunk(c))
                    pe.wait_ge(cbm_ready, after_chunk(c))
                    pe.matmul(xt_bank[:], b_tok[:], xw[:], start=True, stop=True).then_inc(ds_ps, 1)
                    pe.wait_ge(mt_ready, after_chunk(c))
                    for h in range(H):
                        ins = pe.matmul(yd_bank[:, h * HD:(h + 1) * HD], mt[:, h, :], xdt[:, h * HD:(h + 1) * HD],
                                        start=True, stop=True)
                    ins.then_inc(yd_ps, 1)
                    if more:
                        for item in ITEMS[k][1]:
                            project(n + 1, 1 - par, item)
                    out_project(c - 1)

            for item in ORDER:
                project(0, 0, item)
            with pe.Fori(0, NSEQ - 1) as s:
                step(s, 0, False)
                step(s, 1, False)
            step(NSEQ - 1, 0, True)
            step(NSEQ - 1, 1, True)
            c = NBLK * CH
            g_transposes(c - 1)
            pe.wait_ge(glo_done, after_chunk(c - 1))
            out_project(c - 1)


def route(nc, x1_dram, gate, rows, picks, wts, w1, w3, w2, biases):
    slot_a, slot_b, w_a, w_b, eid, eid_f, bias, row_no = picks
    D, E = gate.shape
    LO = 64
    KT = D // P
    w13_hi, w13_lo, w2_hi, w2_lo = wts
    NE, HD = w13_hi.shape[3:]
    HT = w2_hi.shape[1] // NE
    TOK = (x1_dram.shape[0] - 1) * 512
    T = 512
    CH = T // P
    NBLK = TOK // T
    NC = TOK // P
    NS = TOK // TILE
    NR = routed_tiles(TOK, E)
    MAXT = TOK // TILE
    XR = 4
    SPLIT_V = 3
    LOWEST = -3e38
    assert TOP == 2 and NC == 1 << 5

    with ExitStack() as ctx:
        def sb(name, shape, dt=F32):
            return ctx.enter_context(nc.sbuf_tensor(name, shape, dt))

        def sem(name):
            return ctx.enter_context(nc.semaphore(name))

        xk = [sb(f"xk{i}", [P, CH, D]) for i in range(XR)]
        gate_f = sb("gate_f", [P, KT, E])
        gate_hi = sb("gate_hi", [P, KT, E], F32R)
        gate_lo = sb("gate_lo", [P, KT, E], F32R)
        gate_b = sb("gate_b", [P, 48])
        ident = sb("r_ident", [P, P])
        lower = sb("r_lower", [P, P])
        ones = sb("r_ones", [P, P])
        before = sb("before", [P, E, E])
        fills = sb("fills", [P, MAXT])
        tile_ids = sb("tile_ids", [P, NR])
        mx, sm, rc, sa_f, sb_f = (sb("r_" + n, [P, NC]) for n in ("mx", "sm", "rc", "sa", "sb"))
        lg, sh, es, sc, bi, sel, cum0, cum1 = (
            sb("r_" + n, [P, NC, E]) for n in ("lg", "sh", "es", "sc", "bi", "sel", "cum0", "cum1"))
        slot, in_a, in_b, prod = bi, es, sh, lg
        x_hi = [sb(f"r_x_hi{i}", [P, KT, T], F32R) for i in range(2)]
        x_lo = [sb(f"r_x_lo{i}", [P, KT, T], F32R) for i in range(2)]
        first_of = sb("first_of", [P, E])
        full = xk[0][:, 0, 0:E * MAXT].rearrange("p (e t) -> p e t", e=E)
        past = xk[1][:].rearrange("p c d -> p (c d)")[:, 0:NR * E].rearrange("p (t e) -> p t e", e=E)
        is_hi = sb("is_hi", [P, 1])
        is_lo = sb("is_lo", [P, 1])
        bias_f = sb("bias_f", [P, 2 * HD])
        lt = sb("lt", [E, T])
        ntiles, base, ends = (sb("r_" + n, [P, E]) for n in ("ntiles", "base", "ends"))
        base_p = sb("base_p", [P, E, E])
        last = sb("last", [P, NR])

        xt_bank = [[ctx.enter_context(nc.psum_tensor(f"r_xt{i}{k}", [P, T], F32)) for k in range(KT)] for i in range(2)]
        lt_bank = ctx.enter_context(nc.psum_tensor("lt_bank", [E, T], F32))
        lg_bank = ctx.enter_context(nc.psum_tensor("lg_bank", [P, 2, CH, E], F32))
        cnt_bank = ctx.enter_context(nc.psum_tensor("cnt_bank", [P, 2, NC, E], F32))

        s_w, s_const, s_set_a, s_set_v = sem("r_w"), sem("r_const"), sem("r_set_a"), sem("r_set_v")
        x_in = [sem(f"r_x_in{i}") for i in range(XR)]
        xt_ps, hi_done, lo_done, rt_ps = sem("r_xt_ps"), sem("r_hi"), sem("r_lo"), sem("r_ps")
        w_in = [sem(f"w_in{i}") for i in range(NE)]
        w_high, w_low = sem("w_high"), sem("w_low")
        s_zero, s_bias, s_split, s_fix = sem("r_zero"), sem("r_bias"), sem("r_split"), sem("r_fix")
        lt_out, lg_ps, lg_set = sem("lt_out"), sem("lg_ps"), sem("lg_set")
        chain, exp_done, cnt_ps = sem("r_chain"), sem("r_exp"), sem("cnt_ps")
        NCONST = 17

        x_v = x1_dram.rearrange("b (c p) d -> b p c d", p=P)
        order = [NE - 1] + list(range(NE - 1))

        def rows2(t, e):
            return t[:, e * HT:(e + 1) * HT, :]

        block = ctx.enter_context(nc.Block())

        @block.sync
        def _(sp):
            for dst, src in ((gate_f, gate.rearrange("(k p) e -> p k e", p=P)), (gate_b, rows.partition_broadcast(P))):
                sp.dma_start(dst[:], src).then_inc(s_w, 16)

            def load(b):
                sp.dma_start(xk[b % XR][:], x_v[b + 1]).then_inc(x_in[b % XR], 16)

            for b in range(NBLK):
                if b >= XR:
                    sp.wait_ge(xt_ps, b - XR + 1)
                load(b)
            sp.wait_ge(s_zero, 1)
            for row in (0, LO):
                sp.dma_start(bias_f[row:row + NE, :], biases).then_inc(s_bias, 16)
            for e in order:
                for i, w in enumerate((w1, w3)):
                    sp.dma_start(w13_lo[:, i, :, e, :].bitcast(F32),
                                 w.rearrange("(k p) (e c) -> p k e c", p=P, c=HD)[:, :, e, :]).then_inc(w_in[e], 16)
                sp.dma_start(rows2(w2_lo, e).bitcast(F32), rows2(w2, e)).then_inc(w_in[e], 16)

        @block.gpsimd
        def _(pool):
            for t, value in ((ident[:], 0.0), (lower[:], 1.0), (ones[:], 1.0), (before[:], 1.0), (is_hi[:], 1.0), (is_lo[:], 1.0), (eid[:, 0:NS], E), (eid_f[:, 0:NS], float(E))):
                nc.gpsimd.memset(t, value).then_inc(s_const, 1)
            nc.gpsimd.iota(fills[:], [[TILE, MAXT]], 0, 0, allow_small_or_imprecise_dtypes=True).then_inc(s_const, 1)
            nc.gpsimd.iota(tile_ids[:], [[1, NR]], 0, 0, allow_small_or_imprecise_dtypes=True).then_inc(s_const, 1)
            nc.gpsimd.iota(first_of[:], [[-1, E]], E, 0, allow_small_or_imprecise_dtypes=True).then_inc(s_const, 1)
            nc.gpsimd.iota(row_no[:], [[1, 1]], 0, 1, allow_small_or_imprecise_dtypes=True).then_inc(s_const, 1)
            nc.gpsimd.memset(bias_f[:], 0.0).then_inc(s_zero, 1)
            pool.wait_ge(s_const, 12)
            nc.gpsimd.affine_select(out=is_hi[:], in_=is_hi[:], compare_op=ALU.is_ge, fill=0.0, base=LO - 1,
                                    pattern=[[1, 1]], channel_multiplier=-1).then_inc(s_const, 1)
            nc.gpsimd.affine_select(out=is_lo[:], in_=is_lo[:], compare_op=ALU.is_ge, fill=0.0, base=-LO,
                                    pattern=[[1, 1]], channel_multiplier=1).then_inc(s_const, 1)
            nc.gpsimd.affine_select(out=ident[:], in_=ident[:], compare_op=ALU.not_equal, fill=1.0, base=0,
                                    pattern=[[-1, P]], channel_multiplier=1).then_inc(s_const, 1)
            nc.gpsimd.affine_select(out=lower[:], in_=lower[:], compare_op=ALU.is_ge, fill=0.0, base=-1,
                                    pattern=[[1, P]], channel_multiplier=-1).then_inc(s_const, 1)
            nc.gpsimd.affine_select(out=before[:], in_=before[:], compare_op=ALU.is_ge, fill=0.0, base=-1,
                                    pattern=[[1, E], [-1, E]], channel_multiplier=0).then_inc(s_const, 1)
            for n, e in enumerate(order[:-SPLIT_V]):
                for i in range(2):
                    pool.wait_ge(w_high, 3 * n + i + 1)
                    nc.gpsimd.tensor_tensor(w13_lo[:, i, :, e, :], w13_lo[:, i, :, e, :].bitcast(F32),
                                            w13_hi[:, i, :, e, :].bitcast(F32), ALU.subtract).then_inc(w_low, 1)
                pool.wait_ge(w_high, 3 * n + 3)
                nc.gpsimd.tensor_tensor(rows2(w2_lo, e), rows2(w2_lo, e).bitcast(F32),
                                        rows2(w2_hi, e).bitcast(F32), ALU.subtract).then_inc(w_low, 1)

        @block.scalar
        def _(act):
            act.wait_ge(s_w, 32)
            nc.scalar.copy(gate_hi[:], gate_f[:]).then_inc(s_set_a, 1)
            act.sem_inc(hi_done, 2)

            def high(b, par):
                act.wait_ge(xt_ps, b + 1)
                act.wait_ge(rt_ps, b + 1)
                for k in range(KT):
                    ins = nc.scalar.copy(x_hi[par][:, k, :], xt_bank[par][k][:])
                ins.then_inc(hi_done, 1)

            def take_logits(b):
                act.wait_ge(rt_ps, b + 3)
                act.wait_ge(lg_ps, b + 1)
                nc.scalar.copy(lt[:], lt_bank[:]).then_inc(lt_out, 1)

            act.sem_inc(lt_out, 1)
            high(0, 0)
            with act.Fori(0, NBLK // 2 - 1) as s:
                high(s * 2 + 1, 1)
                take_logits(s * 2)
                high(s * 2 + 2, 0)
                take_logits(s * 2 + 1)
            high(NBLK - 1, 1)
            take_logits(NBLK - 2)
            take_logits(NBLK - 1)
            act.wait_ge(chain, 2)
            nc.scalar.activation(es[:], sh[:], ACT.Exp).then_inc(exp_done, 1)
            act.wait_ge(s_bias, 32)
            nc.scalar.copy(bias[:], bias_f[:]).then_inc(s_split, 1)
            for e in order:
                act.wait_ge(w_in[e], 48)
                for i in range(2):
                    nc.scalar.copy(w13_hi[:, i, :, e, :], w13_lo[:, i, :, e, :].bitcast(F32)).then_inc(w_high, 1)
                nc.scalar.copy(rows2(w2_hi, e), rows2(w2_lo, e).bitcast(F32)).then_inc(w_high, 1)

        @block.vector
        def _(dve):
            dve.wait_ge(s_set_a, 1)
            nc.vector.tensor_tensor(gate_lo[:], gate_f[:], gate_hi[:].bitcast(F32), ALU.subtract).then_inc(s_set_v, 1)
            dve.sem_inc(lo_done, 2)

            def low(b, par):
                dve.wait_ge(hi_done, b + 3)
                for k in range(KT):
                    ins = nc.vector.tensor_tensor(x_lo[par][:, k, :], xt_bank[par][k][:], x_hi[par][:, k, :].bitcast(F32), ALU.subtract)
                ins.then_inc(lo_done, 1)

            def take(b, par):
                dve.wait_ge(lg_ps, b + 2)
                nc.vector.tensor_copy(lg[:, bass.ds(b * CH, CH), :], lg_bank[:, par]).then_inc(lg_set, 1)

            dve.sem_inc(lg_set, 2)
            low(0, 0)
            with dve.Fori(0, NBLK // 2 - 1) as s:
                low(s * 2 + 1, 1)
                take(s * 2, 0)
                low(s * 2 + 2, 0)
                take(s * 2 + 1, 1)
            low(NBLK - 1, 1)
            take(NBLK - 2, 0)
            take(NBLK - 1, 1)

            def over_e(t):
                return t[:].unsqueeze(2).broadcast_to([P, NC, E])

            dve.wait_ge(lg_set, NBLK + 2)
            dve.wait_ge(s_const, NCONST)
            nc.vector.tensor_reduce(mx[:], lg[:], AX.X, ALU.max).then_inc(chain, 1)
            dve.wait_ge(chain, 1)
            nc.vector.tensor_tensor(sh[:], lg[:], over_e(mx), ALU.subtract).then_inc(chain, 1)
            dve.wait_ge(exp_done, 1)
            nc.vector.tensor_reduce(sm[:], es[:], AX.X, ALU.add).then_inc(chain, 1)
            dve.wait_ge(chain, 3)
            nc.vector.reciprocal(rc[:], sm[:]).then_inc(chain, 1)
            dve.wait_ge(chain, 4)
            nc.vector.tensor_tensor(sc[:], es[:], over_e(rc), ALU.mult).then_inc(chain, 1)
            dve.wait_ge(chain, 5)
            nc.vector.tensor_tensor(bi[:], sc[:], gate_b[:, 40:48].unsqueeze(1).broadcast_to([P, NC, E]), ALU.add).then_inc(chain, 1)
            dve.wait_ge(chain, 6)
            def over_c(t):
                return t[:].unsqueeze(1).broadcast_to([P, NC, E])

            for i, chosen in enumerate((in_a, in_b)):
                at = 6 * i + 6
                nc.vector.tensor_reduce(mx[:], bi[:], AX.X, ALU.max).then_inc(chain, 1)
                dve.wait_ge(chain, at + 1)
                nc.vector.tensor_tensor(prod[:], bi[:], over_e(mx), ALU.is_equal).then_inc(chain, 1)
                dve.wait_ge(chain, at + 2)
                nc.vector.tensor_tensor(prod[:], prod[:], over_c(first_of), ALU.mult).then_inc(chain, 1)
                dve.wait_ge(chain, at + 3)
                nc.vector.tensor_reduce(mx[:], prod[:], AX.X, ALU.max).then_inc(chain, 1)
                dve.wait_ge(chain, at + 4)
                nc.vector.tensor_tensor(chosen[:], prod[:], over_e(mx), ALU.is_equal).then_inc(chain, 1)
                dve.wait_ge(chain, at + 5)
                if i == 0:
                    nc.vector.scalar_tensor_tensor(out=bi[:], in0=in_a[:], scalar=LOWEST, in1=bi[:], op0=ALU.mult,
                                                   op1=ALU.add).then_inc(chain, 1)
                else:
                    nc.vector.tensor_tensor(sel[:], in_a[:], in_b[:], ALU.add).then_inc(chain, 1)
                dve.wait_ge(chain, at + 6)
            dve.wait_ge(cnt_ps, 1)
            pos, total = cnt_bank[:, 0], cnt_bank[:, 1]
            nc.vector.tensor_copy(cum0[:], total).then_inc(chain, 1)
            dve.wait_ge(chain, 19)
            cums, step = (cum0, cum1), 1
            for i in range(5):
                a, b = cums[i % 2], cums[1 - i % 2]
                nc.vector.tensor_copy(b[:, 0:step], a[:, 0:step])
                nc.vector.tensor_tensor(b[:, step:], a[:, step:], a[:, 0:NC - step], ALU.add).then_inc(chain, 1)
                dve.wait_ge(chain, 20 + i)
                step *= 2
            cum, free = cums[1], cums[0]
            assert step == NC
            nc.vector.tensor_tensor(full, cum[:, NC - 1].unsqueeze(2).broadcast_to([P, E, MAXT]),
                                    fills[:].unsqueeze(1).broadcast_to([P, E, MAXT]), ALU.is_gt).then_inc(chain, 1)
            nc.vector.tensor_tensor(free[:], cum[:], total, ALU.subtract).then_inc(chain, 1)
            dve.wait_ge(chain, 26)
            nc.vector.tensor_reduce(ntiles[:], full, AX.X, ALU.add).then_inc(chain, 1)
            nc.vector.tensor_tensor(prod[:], free[:], pos, ALU.add).then_inc(chain, 1)
            dve.wait_ge(chain, 28)
            nc.vector.tensor_tensor(base_p[:], ntiles[:].unsqueeze(1).broadcast_to([P, E, E]), before[:], ALU.mult).then_inc(chain, 1)
            dve.wait_ge(chain, 29)
            nc.vector.tensor_reduce(base[:], base_p[:], AX.X, ALU.add).then_inc(chain, 1)
            dve.wait_ge(chain, 30)
            nc.vector.scalar_tensor_tensor(out=slot[:], in0=over_c(base), scalar=float(TILE), in1=prod[:], op0=ALU.mult,
                                           op1=ALU.add).then_inc(chain, 1)
            nc.vector.tensor_tensor(ends[:], base[:], ntiles[:], ALU.add).then_inc(chain, 1)
            dve.wait_ge(chain, 32)
            nc.vector.tensor_tensor(past, tile_ids[:].unsqueeze(2).broadcast_to([P, NR, E]),
                                    ends[:].unsqueeze(1).broadcast_to([P, NR, E]), ALU.is_ge).then_inc(chain, 1)
            nc.vector.tensor_tensor(prod[:], slot[:], in_a[:], ALU.mult).then_inc(chain, 1)
            dve.wait_ge(chain, 34)
            nc.vector.tensor_reduce(last[:], past, AX.X, ALU.add).then_inc(chain, 1)
            nc.vector.tensor_reduce(sa_f[:], prod[:], AX.X, ALU.add).then_inc(chain, 1)
            nc.vector.tensor_tensor(slot[:], slot[:], in_b[:], ALU.mult).then_inc(chain, 1)
            dve.wait_ge(chain, 37)
            nc.vector.tensor_scalar(eid[:, NS:NS + NR], last[:], float(E - 1), None, ALU.min)
            nc.vector.tensor_scalar(eid_f[:, NS:NS + NR], last[:], float(E - 1), None, ALU.min).then_inc(chain, 1)
            nc.vector.tensor_scalar(slot_a[:], sa_f[:], float(TOK + T), None, ALU.add).then_inc(chain, 1)
            nc.vector.tensor_reduce(sb_f[:], slot[:], AX.X, ALU.add).then_inc(chain, 1)
            dve.wait_ge(chain, 40)
            nc.vector.tensor_scalar(slot_b[:], sb_f[:], float(TOK + T), None, ALU.add).then_inc(chain, 1)
            nc.vector.tensor_tensor(prod[:], sc[:], in_a[:], ALU.mult).then_inc(chain, 1)
            nc.vector.tensor_tensor(sc[:], sc[:], in_b[:], ALU.mult).then_inc(chain, 1)
            dve.wait_ge(chain, 43)
            nc.vector.tensor_reduce(w_a[:], prod[:], AX.X, ALU.add).then_inc(chain, 1)
            nc.vector.tensor_reduce(w_b[:], sc[:], AX.X, ALU.add).then_inc(chain, 1)
            dve.wait_ge(s_split, 1)
            nc.vector.tensor_tensor(bias_f[:], bias_f[:], bias[:].bitcast(F32), ALU.subtract).then_inc(s_split, 1)
            dve.wait_ge(s_split, 2)
            nc.vector.tensor_scalar(bias_f[:], bias_f[:], is_lo[:, 0:1], None, ALU.mult).then_inc(s_fix, 1)
            nc.vector.tensor_scalar(row_no[:], is_lo[:], -float(LO), row_no[:, 0:1], ALU.mult, ALU.add).then_inc(s_fix, 1)
            dve.wait_ge(s_fix, 2)
            nc.vector.scalar_tensor_tensor(out=bias[:], in0=bias[:].bitcast(F32), scalar=is_hi[:, 0:1], in1=bias_f[:],
                                           op0=ALU.mult, op1=ALU.add).then_inc(s_split, 1)
            for n in range(NE - SPLIT_V, NE):
                e = order[n]
                for i in range(2):
                    dve.wait_ge(w_high, 3 * n + i + 1)
                    nc.vector.tensor_tensor(w13_lo[:, i, :, e, :], w13_lo[:, i, :, e, :].bitcast(F32),
                                            w13_hi[:, i, :, e, :].bitcast(F32), ALU.subtract).then_inc(w_low, 1)
                dve.wait_ge(w_high, 3 * n + 3)
                nc.vector.tensor_tensor(rows2(w2_lo, e), rows2(w2_lo, e).bitcast(F32),
                                        rows2(w2_hi, e).bitcast(F32), ALU.subtract).then_inc(w_low, 1)

        @block.tensor
        def _(pe):
            pe.sem_inc(lg_ps, 1)
            pe.sem_inc(rt_ps, 2)
            pe.wait_ge(s_const, NCONST)
            pe.wait_ge(s_set_v, 1)
            x_parts, gate_parts = (x_hi, x_lo), (gate_hi, gate_lo)

            def transposes(s, j):
                b = s * XR + j
                pe.wait_ge(x_in[j % XR], (s + j // XR + 1) * 16)
                pe.wait_ge(lo_done, b + 1)
                for k in range(KT):
                    for c in range(CH):
                        ins = pe.transpose(xt_bank[j % 2][k][:, c * P:(c + 1) * P], xk[j % XR][:, c, k * P:(k + 1) * P], ident[:])
                ins.then_inc(xt_ps, 1)

            def logits(b, par):
                pe.wait_ge(lo_done, b + 3)
                pe.wait_ge(lt_out, b + 1)
                for k in range(KT):
                    for a, w in PASSES:
                        ins = pe.matmul(lt_bank[:], gate_parts[w][:, k, :], x_parts[a][par][:, k, :],
                                        start=(k == 0 and a + w == 0), stop=(k == KT - 1 and a == 1))
                ins.then_inc(rt_ps, 1)
                pe.wait_ge(lt_out, b + 2)
                pe.wait_ge(lg_set, b + 2)
                for c in range(CH):
                    ins = pe.transpose(lg_bank[:, par, c, :], lt[:, c * P:(c + 1) * P], ident[0:E, 0:E])
                ins.then_inc(lg_ps, 1)

            transposes(0, 0)
            with pe.Fori(0, NBLK // XR - 1) as s:
                for j in range(XR):
                    transposes(s, j + 1)
                    logits(s * XR + j, j % 2)
            s = NBLK // XR - 1
            for j in range(XR):
                if j + 1 < XR:
                    transposes(s, j + 1)
                logits(s * XR + j, j % 2)
            pe.wait_ge(chain, 18)
            flat = sel[:].rearrange("p c e -> p (c e)")
            for i, mask in enumerate((lower, ones)):
                ins = pe.matmul(cnt_bank[:, i].rearrange("p c e -> p (c e)"), mask[:], flat, start=True, stop=True)
            ins.then_inc(cnt_ps, 1)


def experts(nc, wts, picks, xg, acc):
    w13_hi, w13_lo, w2_hi, w2_lo = wts
    slot_a, slot_b, w_a, w_b, eid, eid_f, bias, row_no = picks
    KT = w13_hi.shape[2]
    NE = w13_hi.shape[3]
    HD = w13_hi.shape[4]
    HT = w2_hi.shape[1] // NE
    D = w2_hi.shape[2]
    TOK = acc.shape[0] - 512
    NT = (xg.shape[0] - 512) // TILE
    NS = TOK // TILE
    HV = TILE // P
    U = 4
    SG = 8
    NSTEP = NS // U
    HEAD = 4
    assert TOK // P == SG * NSTEP and NT % U == U - 1

    with ExitStack() as ctx:
        def sb(name, shape, dt=F32):
            return ctx.enter_context(nc.sbuf_tensor(name, shape, dt))

        def bank(name, cols=512):
            return ctx.enter_context(nc.psum_tensor(name, [P, cols], F32))

        def sem(name):
            return ctx.enter_context(nc.semaphore(name))

        ident = sb("ident2", [P, P])
        xin = [sb(f"xin{i}", [P, HV, D + 2]) for i in range(2)]
        x_hi = [sb(f"x_hi{i}", [P, KT, TILE], F32R) for i in range(2)]
        x_lo = [sb(f"x_lo{i}", [P, KT, TILE], F32R) for i in range(2)]
        dest = [sb(f"dest{i}", [P, HV], I32) for i in range(U)]
        wgt = [sb(f"wgt{i}", [P, HV]) for i in range(U)]
        pick = [sb(f"pick{i}", [P, P], F32R) for i in range(U)]
        g = [sb(f"g{i}", [P, HV, HT * P]) for i in range(2)]
        h_hi = sb("h_hi", [P, HT, TILE], F32R)
        h_lo = sb("h_lo", [P, HT, TILE], F32R)
        y_sb = [sb(f"y_sb{i}", [P, HV, D]) for i in range(2)]
        xrow = sb("xrow", [P, SG, D + 2])
        idx_a = sb("idx_a", [P, SG], I32)
        idx_b = sb("idx_b", [P, SG], I32)

        xt_bank = bank("e_xt")
        h_bank = [[bank(f"h_bank{h}_{n}") for n in (1, 3)] for h in range(HV)]
        ht_bank = bank("ht_bank", 1024)
        y_bank = bank("y_bank")

        s_const = sem("e_const")
        x_in = [sem("e_x_in0"), sem("e_x_in1")]
        xt_ps, xhi_done, xlo_done = sem("e_xt_ps"), sem("xhi_done"), sem("xlo_done")
        h1_ps, h1_out = sem("h1_ps"), sem("h1_out")
        h_ps, g_done, silu_done, ht_ps = sem("h_ps"), sem("g_done"), sem("e_silu"), sem("ht_ps")
        hi_done, lo_done, y_ps, y_ready = sem("e_hi"), sem("e_lo"), sem("y_ps"), sem("e_y_ready")
        added, row_in, set_done, scattered = sem("added"), sem("row_in"), sem("set_done"), sem("scattered")
        gone, own_added = sem("gone"), sem("own_added")
        passed = sem("e_passed")
        NCONST = 6

        def after(t):
            return t + 1 + HEAD

        def part(t, h):
            return (t + HEAD) * HV + h + 1

        def loads(s, j):
            return (s * (U // 2) + j // 2 + 1) * 16

        def pipeline(eng, prepare, hidden, close, turn):
            prepare(0, 0)
            prepare(0, 1)
            hidden(0, 0)
            turn(0, 0)
            with eng.Fori(0, NT // U) as s:
                for j in range(1, U + 1):
                    prepare(s, j + 1)
                    hidden(s, j)
                    close(s, j - 1)
                    turn(s, j)
            s = NT // U
            prepare(s, 2)
            hidden(s, 1)
            close(s, 0)
            turn(s, 1)
            hidden(s, 2)
            close(s, 1)
            turn(s, 2)
            close(s, 2)

        xg_v = xg[512:].rearrange("(t h p) d -> t p h d", p=P, h=HV)
        own_v = acc[512:].rearrange("(t h p) d -> t p h d", p=P, h=HV)
        block = ctx.enter_context(nc.Block())

        @block.sync
        def _(sp):
            def x_load(t, j):
                sp.dma_start(xin[j % 2][:], xg_v[t]).then_inc(x_in[j % 2], 16)

            def next_load(t, j):
                sp.wait_ge(xlo_done, after(t))
                x_load(t + 2, j)

            x_load(0, 0)
            x_load(1, 1)
            with sp.Fori(0, NSTEP - 1) as s:
                for j in range(U):
                    next_load(s * U + j, j)
            next_load(NS - 4, 0)
            next_load(NS - 3, 1)
            sp.wait_ge(scattered, 16 * 2 * SG * NSTEP)
            next_load(NS - 2, 0)
            next_load(NS - 1, 1)
            with sp.Fori(NSTEP, NT // U) as s:
                for j in range(U):
                    next_load(s * U + j, j)
            next_load(NT - 3, 0)

        @block.gpsimd
        def _(pool):
            pool.sem_inc(gone, HEAD)
            for t, value in ((ident[:], 0.0), (g[0][:, :, HD + 1:], 0.0), (g[1][:, :, HD + 1:], 0.0),
                             (g[0][:, :, HD:HD + 1], 1.0), (g[1][:, :, HD:HD + 1], 1.0)):
                nc.gpsimd.memset(t, value).then_inc(s_const, 1)
            pool.wait_ge(s_const, 1)
            nc.gpsimd.affine_select(out=ident[:], in_=ident[:], compare_op=ALU.not_equal, fill=1.0, base=0,
                                    pattern=[[-1, P]], channel_multiplier=1).then_inc(s_const, 1)

            def row_load(s):
                pool.dma_start(xrow[:], xg[bass.ds(s * SG * P + 512, SG * P), :].rearrange("(c p) d -> p c d", p=P)).then_inc(row_in, 16)

            def settle(t):
                pool.wait_ge(added, 16 * HV * (t - NS + 1))
                pool.sem_inc(gone, 1)

            def add(t, j, first=False):
                if not first:
                    settle(t - 1)
                pool.wait_ge(y_ready, after(t))
                pool.sem_inc(passed, 1)
                for h in range(HV):
                    nc.gpsimd.indirect_dma_start(acc, bass.IndirectOffsetOnAxis(dest[j][:, h:h + 1], 0), y_sb[j % 2][:, h, :], None,
                                                 compute_op=ALU.add).then_inc(added, 16)

            def settle_own(t):
                pool.wait_ge(own_added, 16 * (t + 1))
                pool.sem_inc(gone, 1)

            def add_own(t, j, first=False):
                if not first:
                    settle_own(t - 1)
                pool.wait_ge(y_ready, after(t))
                pool.dma_start(own_v[t], y_sb[j % 2][:], accum_op=ALU.add).then_inc(own_added, 16)

            def scatter(idx, half):
                for c in range(half * SG // 2, (half + 1) * SG // 2):
                    nc.gpsimd.indirect_dma_start(xg, bass.IndirectOffsetOnAxis(idx[:, c:c + 1], 0), xrow[:, c, :], None).then_inc(scattered, 16)

            def put(dst, src, s):
                return nc.gpsimd.tensor_copy(dst, src[:, bass.ds(s * SG, SG)])


            def scatter_step(s, first=False, last=False):
                pool.wait_ge(row_in, (s + 1) * 16)
                pool.sem_inc(passed, 1)
                put(idx_a[:], slot_a, s).then_inc(set_done, 1)
                put(idx_b[:], slot_b, s).then_inc(set_done, 1)
                put(xrow[:, :, D + 1], w_a, s).then_inc(set_done, 1)
                pool.wait_ge(set_done, 6 * s + 3)
                pool.sem_inc(passed, 1)
                scatter(idx_a, 0)
                if not first:
                    add_own(s * U - 3, 1)
                scatter(idx_a, 1)
                pool.wait_ge(scattered, 16 * SG * (2 * s + 1))
                pool.sem_inc(passed, 1)
                put(xrow[:, :, D + 1], w_b, s).then_inc(set_done, 3)
                pool.wait_ge(set_done, 6 * s + 6)
                pool.sem_inc(passed, 1)
                scatter(idx_b, 0)
                if not first:
                    add_own(s * U - 2, 2)
                scatter(idx_b, 1)
                if not first:
                    add_own(s * U - 1, 3)
                if not last:
                    pool.wait_ge(scattered, 16 * SG * (2 * s + 2))
                    row_load(s + 1)
                add_own(s * U, 0, first=first)

            row_load(0)
            scatter_step(0, first=True)
            with pool.Fori(1, NSTEP - 1) as s:
                scatter_step(s)
            scatter_step(NSTEP - 1, last=True)
            for t in range(NS - U + 1, NS):
                add_own(t, t % U)
            settle_own(NS - 1)
            add(NS, 0, first=True)
            for t in range(NS + 1, NS + U):
                add(t, t % U)
            with pool.Fori(NSTEP + 1, NT // U) as s:
                for j in range(U):
                    add(s * U + j, j)
            for t in range(NT - U + 1, NT):
                add(t, t % U)
            settle(NT - 1)

        @block.scalar
        def _(act):
            for s_, start in ((xhi_done, HEAD), (h1_out, HEAD * HV), (silu_done, HEAD * HV), (hi_done, HEAD), (y_ready, HEAD)):
                act.sem_inc(s_, start)

            def x_high(s, j):
                t = s * U + j
                act.wait_ge(xt_ps, after(t))
                act.wait_ge(h_ps, part(t - 2, HV - 1))
                nc.scalar.copy(x_hi[j % 2][:], xt_bank[:].rearrange("p (k t) -> p k t", k=KT)).then_inc(xhi_done, 1)

            def silu(s, j):
                t = s * U + j
                for h in range(HV):
                    act.wait_ge(h1_ps, part(t, h))
                    act.wait_ge(ht_ps, after(t - 2))
                    nc.scalar.copy(g[j % 2][:, h, 0:HD], h_bank[h][0][:, 0:HD]).then_inc(h1_out, 1)
                for h in range(HV):
                    act.wait_ge(g_done, part(t, h))
                    nc.scalar.activation(g[j % 2][:, h, 0:HD], g[j % 2][:, h, 0:HD], ACT.Silu).then_inc(silu_done, 1)

            def weigh(s, j):
                t = s * U + j
                act.wait_ge(y_ps, after(t))
                act.wait_ge(gone, after(t - 2))
                for h in range(HV):
                    ins = nc.scalar.activation(y_sb[j % 2][:, h, :], y_bank[:, h * D:(h + 1) * D], ACT.Copy, scale=wgt[j % U][:, h:h + 1])
                ins.then_inc(y_ready, 1)

            def high(s, j):
                t = s * U + j
                act.wait_ge(ht_ps, after(t))
                act.wait_ge(y_ps, after(t - 1))
                nc.scalar.copy(h_hi[:], ht_bank[:, 0:HT * TILE].rearrange("p (i t) -> p i t", i=HT)).then_inc(hi_done, 1)

            pipeline(act, x_high, silu, weigh, high)

        @block.vector
        def _(dve):
            for s_, start in ((xlo_done, HEAD), (g_done, HEAD * HV), (lo_done, HEAD)):
                dve.sem_inc(s_, start)
            def x_low(s, j):
                t = s * U + j
                dve.wait_ge(xhi_done, after(t))
                nc.vector.tensor_tensor(x_lo[j % 2][:], xt_bank[:].rearrange("p (k t) -> p k t", k=KT),
                                        x_hi[j % 2][:].bitcast(F32), ALU.subtract)
                dve.wait_ge(gone, after(t - U))
                nc.vector.tensor_copy(dest[j % U][:].unsqueeze(2), xin[j % 2][:, :, D:D + 1].bitcast(I32))
                nc.vector.tensor_copy(wgt[j % U][:].unsqueeze(2), xin[j % 2][:, :, D + 1:D + 2])
                nc.vector.tensor_scalar(pick[j % U][:], eid_f[:, bass.ds(t, 1)].broadcast_to([P, P]), row_no[:, 0:1], None,
                                        ALU.is_equal).then_inc(xlo_done, 1)

            def gated(s, j):
                t = s * U + j
                for h in range(HV):
                    dve.wait_ge(h_ps, part(t, h))
                    dve.wait_ge(h1_out, part(t, h))
                    nc.vector.tensor_tensor(g[j % 2][:, h, 0:HD], h_bank[h][1][:, 0:HD], g[j % 2][:, h, 0:HD], ALU.mult).then_inc(g_done, 1)

            def low(s, j):
                t = s * U + j
                dve.wait_ge(hi_done, after(t))
                nc.vector.tensor_tensor(h_lo[:], ht_bank[:, 0:HT * TILE].rearrange("p (i t) -> p i t", i=HT),
                                        h_hi[:].bitcast(F32), ALU.subtract).then_inc(lo_done, 1)

            pipeline(dve, x_low, gated, lambda s, j: None, low)

        @block.tensor
        def _(pe):
            for s_, start in ((xt_ps, HEAD), (h1_ps, HEAD * HV), (h_ps, HEAD * HV), (y_ps, HEAD), (ht_ps, HEAD)):
                pe.sem_inc(s_, start)
            pe.wait_ge(s_const, NCONST)
            x_parts, h_parts = (x_hi, x_lo), (h_hi, h_lo)
            w13_parts, w2_parts = (w13_hi, w13_lo), (w2_hi, w2_lo)

            def expert_of(t):
                return pe.value_load(eid[0:1, bass.ds(t, 1)], min_val=0, max_val=NE - 1)

            def transposes(s, j):
                t = s * U + j
                pe.wait_ge(x_in[j % 2], loads(s, j))
                pe.wait_ge(xlo_done, after(t - 1))
                for k in range(KT):
                    for h in range(HV):
                        ins = pe.transpose(xt_bank[:, k * TILE + h * P:k * TILE + (h + 1) * P], xin[j % 2][:, h, k * P:(k + 1) * P], ident[:])
                ins.then_inc(xt_ps, 1)

            def hidden(s, j):
                t = s * U + j
                e = expert_of(t)
                pe.wait_ge(xlo_done, after(t))
                for h in range(HV):
                    pe.wait_ge(g_done, part(t - 1, h))
                    pe.wait_ge(s_const, NCONST)
                    for n in range(2):
                        pe.matmul(h_bank[h][n][:, 0:HD], pick[j % U][:], bias[:, n * HD:(n + 1) * HD], start=True, stop=False)
                        for k in range(KT):
                            for a, w in PASSES:
                                ins = pe.matmul(h_bank[h][n][:, 0:HD], x_parts[a][j % 2][:, k, h * P:(h + 1) * P],
                                                w13_parts[w][:, n, k, bass.ds(e, 1), :].rearrange("p o c -> p (o c)"),
                                                start=False, stop=(k == KT - 1 and a == 1))
                        if n == 0:
                            ins.then_inc(h1_ps, 1)
                    ins.then_inc(h_ps, 1)

            def turn(s, j):
                t = s * U + j
                pe.wait_ge(lo_done, after(t - 1))
                for h in range(HV):
                    pe.wait_ge(silu_done, part(t, h))
                    for i in range(HT):
                        ins = pe.transpose(ht_bank[:, i * TILE + h * P:i * TILE + (h + 1) * P], g[j % 2][:, h, i * P:(i + 1) * P], ident[:])
                ins.then_inc(ht_ps, 1)

            def down(s, j):
                t = s * U + j
                e = expert_of(t)
                pe.wait_ge(lo_done, after(t))
                pe.wait_ge(y_ready, after(t - 1))
                pe.wait_ge(s_const, NCONST)
                for h in range(HV):
                    for i in range(HT):
                        for a, w in PASSES:
                            ins = pe.matmul(y_bank[:, h * D:(h + 1) * D], h_parts[a][:, i, h * P:(h + 1) * P],
                                            w2_parts[w][:, bass.ds(e * HT + i, 1), :].rearrange("p o d -> p (o d)"),
                                            start=(i == 0 and a + w == 0), stop=(i == HT - 1 and a == 1))
                ins.then_inc(y_ps, 1)

            pipeline(pe, transposes, hidden, down, turn)


def finish(nc, acc, out):
    D = out.shape[1]
    T = 512
    CH = T // P
    NBLK = out.shape[0] // T
    with ExitStack() as ctx:
        def sb(name, shape):
            return ctx.enter_context(nc.sbuf_tensor(name, shape, F32))

        def sem(name):
            return ctx.enter_context(nc.semaphore(name))

        r = [sb(f"r{i}", [P, CH, D]) for i in range(NBLK)]
        stat = [sb(f"f_stat{i}", [P, CH, 6]) for i in range(NBLK)]
        mv = [sb(f"f_mv{i}", [P, CH, 2]) for i in range(NBLK)]
        rs = [sb(f"f_rs{i}", [P, CH]) for i in range(NBLK)]
        nb = [sb(f"f_nb{i}", [P, CH]) for i in range(NBLK)]
        c_eps = sb("f_eps", [P, CH])
        c_mhalf = sb("f_mhalf", [P, CH])
        c_zero = sb("f_zero", [P, CH])
        loaded = [sem(f"f_in{i}") for i in range(NBLK)]
        s_const, stat_done, mv_ready, rs_chain, done_v, done_a, stored = (
            sem("f_" + n) for n in ("const", "stat", "mv", "rs", "v", "a", "out"))
        acc_v = acc[512:, :].rearrange("(b c p) d -> b p c d", p=P, c=CH)
        out_v = out.rearrange("(b c p) d -> b p c d", p=P, c=CH)
        block = ctx.enter_context(nc.Block())

        @block.sync
        def _(sp):
            for b in range(NBLK):
                sp.dma_start(r[b][:], acc_v[b]).then_inc(loaded[b], 16)
            for b in range(NBLK):
                sp.wait_ge(done_v, b + 1)
                sp.wait_ge(done_a, b + 1)
                sp.dma_start(out_v[b], r[b][:]).then_inc(stored, 16)
            sp.wait_ge(stored, NBLK * 16)

        @block.gpsimd
        def _(pool):
            nc.gpsimd.memset(c_eps[:], EPS).then_inc(s_const, 1)
            nc.gpsimd.memset(c_mhalf[:], -0.5).then_inc(s_const, 1)
            nc.gpsimd.memset(c_zero[:], 0.0).then_inc(s_const, 1)
            pool.wait_ge(s_const, 3)
            for b in range(NBLK):
                pool.wait_ge(mv_ready, b + 1)
                nc.gpsimd.tensor_tensor(rs[b][:], mv[b][:, :, 1], c_eps[:], ALU.add).then_inc(rs_chain, 1)
                pool.wait_ge(rs_chain, 4 * b + 1)
                nc.gpsimd.tensor_tensor(rs[b][:], rs[b][:], c_mhalf[:], ALU.pow).then_inc(rs_chain, 1)
                pool.wait_ge(rs_chain, 4 * b + 2)
                nc.gpsimd.tensor_tensor(nb[b][:], mv[b][:, :, 0], rs[b][:], ALU.mult).then_inc(rs_chain, 1)
                pool.wait_ge(rs_chain, 4 * b + 3)
                nc.gpsimd.tensor_tensor(nb[b][:], c_zero[:], nb[b][:], ALU.subtract).then_inc(rs_chain, 1)

        @block.vector
        def _(dve):
            def stats(b):
                dve.wait_ge(loaded[b], 16)
                for k in range(CH):
                    ins = nc.vector.bn_stats(stat[b][:, k, :], r[b][:, k, :])
                ins.then_inc(stat_done, 1)
                dve.wait_ge(stat_done, b + 1)
                for k in range(CH):
                    ins = nc.vector.bn_aggr(mv[b][:, k, :], stat[b][:, k, :])
                ins.then_inc(mv_ready, 1)

            def scale(b):
                dve.wait_ge(rs_chain, 4 * b + 4)
                for k in range(CH // 2):
                    ins = nc.vector.tensor_scalar(r[b][:, k, :], r[b][:, k, :], mv[b][:, k, 0:1], rs[b][:, k:k + 1], ALU.subtract, ALU.mult)
                ins.then_inc(done_v, 1)

            for b in range(NBLK):
                stats(b)
                if b:
                    scale(b - 1)
            scale(NBLK - 1)

        @block.scalar
        def _(act):
            for b in range(NBLK):
                act.wait_ge(rs_chain, 4 * b + 4)
                for k in range(CH // 2, CH):
                    ins = nc.scalar.activation(r[b][:, k, :], r[b][:, k, :], ACT.Identity, bias=nb[b][:, k:k + 1], scale=rs[b][:, k:k + 1])
                ins.then_inc(done_a, 1)


def build(nc, a, out):
    tok, d = out.shape
    ne = a["f_gate"].shape[1]
    nr = routed_tiles(tok, ne)
    nt = tok // TILE + nr
    hd = a["f_w1"].shape[1] // (ne + 1)
    x1_dram = nc.dram_tensor("x1_dram", (tok // 512 + 1, 512, d), F32, kind="Internal").ap()
    xg = nc.dram_tensor("xg", (512 + nt * TILE, d + 2), F32, kind="Internal").ap()
    acc = x1_dram.rearrange("b t d -> (b t) d")
    mixer(nc, a["uT"], a["u"], a["w_in"], a["conv_w"], a["conv_b"], a["rows"], a["norm_w"], a["w_out"], x1_dram, xg)
    with ExitStack() as ctx:
        picks = [ctx.enter_context(nc.sbuf_tensor(n, [P, k], dt)) for n, k, dt in (
            ("slot_a", tok // P, I32), ("slot_b", tok // P, I32), ("w_a", tok // P, F32), ("w_b", tok // P, F32), ("eid", nt, I32), ("eid_f", nt, F32),
            ("bias", a["f_bias"].shape[1], F32R), ("row_no", 1, F32))]
        wts = [ctx.enter_context(nc.sbuf_tensor(n, s, F32R)) for n, s in (
            ("w13_hi", [P, 2, d // P, ne + 1, hd]), ("w13_lo", [P, 2, d // P, ne + 1, hd]),
            ("w2_hi", [P, a["f_w2"].shape[1], d]), ("w2_lo", [P, a["f_w2"].shape[1], d]))]
        route(nc, x1_dram, a["f_gate"], a["rows"], picks, wts, a["f_w1"], a["f_w3"], a["f_w2"], a["f_bias"])
        experts(nc, wts, picks, xg, acc)
    finish(nc, acc, out)


def _layout(inputs):
    import numpy as np
    g = {k.split("_", 2)[2] if k.startswith("L0_attn") else "f_" + k.split("_", 2)[2]: np.asarray(v) for k, v in inputs.items()}
    u = g["u"].reshape(-1, g["u"].shape[-1])
    D = u.shape[1]
    H = g["f_sw1"].shape[1]
    HP = (H + P - 1) // P * P
    a = {
        "uT": u.T, "u": u, "w_in": g["in_proj_w"].T,
        "conv_w": g["conv_w"][:, 0, :].reshape(-1, P, 4).transpose(1, 0, 2), "conv_b": g["conv_b"].reshape(-1, P).T,
        "rows": np.concatenate([g["A_log"].ravel(), g["dt_bias"], g["D"], g["f_gate_b"]]),
        "norm_w": g["norm_w"].reshape(-1, P).T, "w_out": g["out_proj_w"].T,
    }

    def with_shared(per_expert, shared):
        return np.concatenate([per_expert, shared[None]])

    for i in "13":
        a["f_w" + i] = with_shared(g["f_w" + i], g["f_sw" + i]).transpose(1, 0, 2).reshape(D, -1)
    w2 = with_shared(g["f_w2"], g["f_sw2"])
    b2 = with_shared(g["f_b2"], g["f_sb2"])[:, None, :]
    w2 = np.concatenate([w2, b2, np.zeros((len(w2), HP - H - 1, D), w2.dtype)], 1)
    a["f_w2"] = w2.reshape(-1, P, D).transpose(1, 0, 2)
    a["f_bias"] = np.concatenate([with_shared(g["f_b" + i], g["f_sb" + i]) for i in "13"], 1)
    a["f_gate"] = g["f_gate_w"].T
    return {k: np.ascontiguousarray(v) for k, v in a.items()}


def kernel(**inputs):
    import concourse.bacc as bacc
    from concourse.bass_utils import run_bass_kernel_spmd

    shape = inputs["L0_attn_u"].shape
    arrays = _layout(inputs)
    nc = bacc.Bacc("TRN2", target_bir_lowering=False, num_devices=1)
    a = {k: nc.dram_tensor("in_" + k, v.shape, mybir.dt.from_np(v.dtype), kind="ExternalInput").ap() for k, v in arrays.items()}
    tok, d = arrays["u"].shape
    out = nc.dram_tensor("out", (tok, d), F32, kind="ExternalOutput").ap()
    build(nc, a, out)
    r = run_bass_kernel_spmd(nc, [{"in_" + k: v for k, v in arrays.items()}], core_ids=[0])
    return r.results[0]["out"].reshape(shape)
```
